# Optimizing a Trainium2 kernel written in Bass

```python
import numpy as np
import jax
import jax.numpy as jnp

def _softmax(x, axis=-1):
    return jax.nn.softmax(x, axis=axis)

def _gelu(x):
    return jax.nn.gelu(x, approximate=True)

def _silu(x):
    return jax.nn.silu(x)

def _sigmoid(x):
    return jax.nn.sigmoid(x)

def _layernorm(x, axis=-1, eps=1e-05):
    m = jnp.mean(x, axis=axis, keepdims=True)
    v = jnp.var(x, axis=axis, keepdims=True)
    return (x - m) / jnp.sqrt(v + eps)

def _scatter_add(tgt, idx, src, axis=0):
    return tgt.at[idx].add(src)

def _segment_sum(src, seg, n):
    return jax.ops.segment_sum(src, seg, n)
kernel_name = 'mk_prb_d2_jaxref_r8_15246b'

def setup_inputs(seed: int=0):
    np.random.seed(seed)
    _w = jnp.asarray

    def _L0_attn_setup():
        import jax, jax.numpy as jnp
        import numpy as np
        D_STATE = 16
        D_CONV = 4

        def silu(x):
            return x * jax.nn.sigmoid(x)

        def _reference_tuple_inner(x, in_w, in_b, conv_w, conv_b, xp_w, xp_b, out_w, out_b):
            B, S, D = x.shape
            h = x @ in_w.T + in_b
            hc = jax.lax.conv_general_dilated(h.transpose(0, 2, 1), conv_w, window_strides=(1,), padding=[(D_CONV - 1, 0)], feature_group_count=conv_w.shape[0], dimension_numbers=('NCH', 'OIH', 'NCH')) + conv_b[None, :, None]
            h = silu(hc.transpose(0, 2, 1))
            xp = h @ xp_w.T + xp_b
            a = jnp.exp(-jnp.exp(xp[..., :D_STATE]))
            b = silu(xp[..., D_STATE:]) * jnp.sum(h, axis=-1, keepdims=True)

            def step(state, ab):
                a_t, b_t = ab
                state = state * a_t + b_t
                return (state, state)
            init = jnp.zeros((B, D_STATE), x.dtype)
            final_state, ys = jax.lax.scan(step, init, (a.transpose(1, 0, 2), b.transpose(1, 0, 2)))
            out = ys.transpose(1, 0, 2) @ out_w.T + out_b
            return (out, final_state)
        key = jax.random.key(seed)
        ks = jax.random.split(key, 9)
        B, S, D = (8, 512, 128)
        DI = 2 * D

        def w(k, shape, fan_in):
            bound = 1.0 / np.sqrt(fan_in)
            return jax.random.uniform(k, shape, jnp.float32, -bound, bound)
        return {'x': jax.random.normal(ks[0], (B, S, D), jnp.float32), 'in_w': w(ks[1], (DI, D), D), 'in_b': w(ks[2], (DI,), D), 'conv_w': w(ks[3], (DI, 1, D_CONV), D_CONV), 'conv_b': w(ks[4], (DI,), D_CONV), 'xp_w': w(ks[5], (2 * D_STATE, DI), DI), 'xp_b': w(ks[6], (2 * D_STATE,), DI), 'out_w': w(ks[7], (D, D_STATE), D_STATE), 'out_b': w(ks[8], (D,), D_STATE)}
    _L0_attn_in = _L0_attn_setup()

    def _L0_ffn_setup():
        import jax, jax.numpy as jnp
        import numpy as np
        D_IN, D_HID = (128, 512)

        def _ternary(key, shape):
            return jax.random.randint(key, shape, -1, 2).astype(jnp.float32)

        def _tlin(x, w, s):
            return jnp.einsum('bsi,oi->bso', x, w) * s
        key = jax.random.key(seed)
        ks = jax.random.split(key, 12)
        inv = lambda fan: 1.0 / np.sqrt(fan).astype(np.float32)
        return {'x': jax.random.normal(ks[0], (4, 256, D_IN), dtype=jnp.float32), 'w1_w': _ternary(ks[1], (D_HID, D_IN)), 'w1_s': jax.random.uniform(ks[2], (D_HID,), dtype=jnp.float32) * inv(D_IN), 'w2_w': _ternary(ks[3], (D_HID, D_IN)), 'w2_s': jax.random.uniform(ks[4], (D_HID,), dtype=jnp.float32) * inv(D_IN), 'h1_w': _ternary(ks[5], (D_HID, D_HID)), 'h1_s': jax.random.uniform(ks[6], (D_HID,), dtype=jnp.float32) * inv(D_HID), 'h2_w': _ternary(ks[7], (D_HID, D_HID)), 'h2_s': jax.random.uniform(ks[8], (D_HID,), dtype=jnp.float32) * inv(D_HID), 'w3_w': _ternary(ks[9], (D_IN, D_HID)), 'w3_s': jax.random.uniform(ks[10], (D_IN,), dtype=jnp.float32) * inv(D_HID)}
    _L0_ffn_in = _L0_ffn_setup()

    def _L1_attn_setup():
        import jax, jax.numpy as jnp
        import numpy as np
        B, L, DM, H, HD, K = (4, 256, 128, 16, 64, 64)
        BASE_LR = 1.0
        EPS = 1e-06

        def _ttt_forward(hidden_states, wq, wk, wv, wo, W1, b1, theta, theta_bias, alpha, gamma, beta):
            Bs, Ls, _ = hidden_states.shape
            n_chunks = Ls // K

            def proj(w):
                return (hidden_states @ w).reshape(Bs, Ls, H, HD).transpose(0, 2, 1, 3)
            xq, xk, xv = (proj(wq), proj(wk), proj(wv))

            def to_chunks(x):
                return x.reshape(Bs, H, n_chunks, K, HD).transpose(2, 0, 1, 3, 4)
            cq, ck, cv = (to_chunks(xq), to_chunks(xk), to_chunks(xv))
            token_eta = jnp.clip(1.0 / jnp.arange(1, K + 1, dtype=jnp.float32) + alpha, 0.0)[None, None, :, None]
            g = gamma[None]
            be = beta[None]
            tb = theta_bias.reshape(1, H, 1, 1)
            W0 = jnp.broadcast_to(W1[None], (Bs, H, HD, HD))
            b0 = jnp.broadcast_to(b1[None], (Bs, H, 1, HD))

            def step(carry, inp):
                W, bb = carry
                xq_c, xk_c, xv_c = inp
                lr = jax.nn.sigmoid(jnp.einsum('bhkc,hcd->bhkd', xk_c, theta) + tb)
                eta = token_eta * (BASE_LR * lr / HD)
                Z1 = xk_c @ W + bb
                mu = Z1.mean(-1, keepdims=True)
                std = jnp.sqrt(Z1.var(-1, keepdims=True) + EPS)
                x_hat = (Z1 - mu) / std
                y = g * x_hat + be
                grad_output = y - (xv_c - xk_c)
                gxh = grad_output * g
                grad_x = (HD * gxh - gxh.sum(-1, keepdims=True) - x_hat * (gxh * x_hat).sum(-1, keepdims=True)) / (HD * std)
                dW = jnp.einsum('bhkc,bhkd->bhcd', eta * xk_c, grad_x)
                db = (eta * grad_x).sum(-2, keepdims=True)
                Wn, bn = (W - dW, bb - db)
                Zq = xq_c @ Wn + bn
                mu2 = Zq.mean(-1, keepdims=True)
                std2 = jnp.sqrt(Zq.var(-1, keepdims=True) + EPS)
                out = xq_c + g * ((Zq - mu2) / std2) + be
                return ((Wn, bn), out)
            _, outs = jax.lax.scan(step, (W0, b0), (cq, ck, cv))
            out = outs.transpose(1, 2, 0, 3, 4).reshape(Bs, H, Ls, HD)
            out = out.transpose(0, 2, 1, 3).reshape(Bs, Ls, H * HD)
            return out @ wo
        key = jax.random.key(seed)
        ks = jax.random.split(key, 8)
        s = 0.02
        return {'hidden_states': jax.random.normal(ks[0], (B, L, DM), jnp.float32), 'wq': jax.random.normal(ks[1], (DM, H * HD), jnp.float32) * s, 'wk': jax.random.normal(ks[2], (DM, H * HD), jnp.float32) * s, 'wv': jax.random.normal(ks[3], (DM, H * HD), jnp.float32) * s, 'wo': jax.random.normal(ks[4], (H * HD, DM), jnp.float32) * s, 'W1': jax.random.normal(ks[5], (H, HD, HD), jnp.float32) * s, 'b1': jnp.zeros((H, 1, HD), jnp.float32), 'theta': jax.random.normal(ks[6], (H, HD, 1), jnp.float32) * s, 'theta_bias': jnp.zeros((H, 1, 1), jnp.float32), 'alpha': jnp.zeros((K,), jnp.float32), 'gamma': jnp.ones((H, 1, HD), jnp.float32), 'beta': jnp.zeros((H, 1, HD), jnp.float32)}
    _L1_attn_in = _L1_attn_setup()

    def _L1_ffn_setup():
        import jax, jax.numpy as jnp
        import numpy as np
        H = 128
        E = 8
        TOP_K = 2
        FF = 4 * H
        B, S = (2, 256)

        def _moe_forward(x, gate_w, gate_b, w1, b1, w2, b2, sw1, sb1, sw2, sb2):
            b, s, h = x.shape
            xf = x.reshape(-1, h)
            scores = jax.nn.sigmoid(xf @ gate_w.T + gate_b)
            top_scores, top_idx = jax.lax.top_k(scores, TOP_K)
            top_scores = top_scores / (top_scores.sum(-1, keepdims=True) + 1e-06)
            comb = (jax.nn.one_hot(top_idx, E, dtype=xf.dtype) * top_scores[..., None]).sum(1)
            hdn = jax.nn.gelu(jnp.einsum('th,ehf->etf', xf, w1) + b1[:, None, :], approximate=False)
            y = jnp.einsum('etf,efh->eth', hdn, w2) + b2[:, None, :]
            routed = jnp.einsum('te,eth->th', comb, y)
            shared = (jax.nn.gelu(xf @ sw1 + sb1, approximate=False) @ sw2 + sb2) * 0.1
            return (routed + shared).reshape(b, s, h)
        key = jax.random.key(seed)
        ks = jax.random.split(key, 12)
        std = 0.02 / np.sqrt(H)
        return {'x': jax.random.normal(ks[0], (B, S, H), dtype=jnp.float32), 'gate_w': jax.random.normal(ks[1], (E, H), dtype=jnp.float32) * std, 'gate_b': jnp.zeros((E,), dtype=jnp.float32), 'w1': jax.random.normal(ks[2], (E, H, FF), dtype=jnp.float32) * (1.0 / np.sqrt(H)), 'b1': jnp.zeros((E, FF), dtype=jnp.float32), 'w2': jax.random.normal(ks[3], (E, FF, H), dtype=jnp.float32) * (1.0 / np.sqrt(FF)), 'b2': jnp.zeros((E, H), dtype=jnp.float32), 'sw1': jax.random.normal(ks[4], (H, FF), dtype=jnp.float32) * (1.0 / np.sqrt(H)), 'sb1': jnp.zeros((FF,), dtype=jnp.float32), 'sw2': jax.random.normal(ks[5], (FF, H), dtype=jnp.float32) * (1.0 / np.sqrt(FF)), 'sb2': jnp.zeros((H,), dtype=jnp.float32)}
    _L1_ffn_in = _L1_ffn_setup()
    _d = {'L0_attn_x': _L0_attn_in['x'], 'L0_attn_in_w': _L0_attn_in['in_w'], 'L0_attn_in_b': _L0_attn_in['in_b'], 'L0_attn_conv_w': _L0_attn_in['conv_w'], 'L0_attn_conv_b': _L0_attn_in['conv_b'], 'L0_attn_xp_w': _L0_attn_in['xp_w'], 'L0_attn_xp_b': _L0_attn_in['xp_b'], 'L0_attn_out_w': _L0_attn_in['out_w'], 'L0_attn_out_b': _L0_attn_in['out_b'], 'L0_ffn_w1_w': _L0_ffn_in['w1_w'], 'L0_ffn_w1_s': _L0_ffn_in['w1_s'], 'L0_ffn_w2_w': _L0_ffn_in['w2_w'], 'L0_ffn_w2_s': _L0_ffn_in['w2_s'], 'L0_ffn_h1_w': _L0_ffn_in['h1_w'], 'L0_ffn_h1_s': _L0_ffn_in['h1_s'], 'L0_ffn_h2_w': _L0_ffn_in['h2_w'], 'L0_ffn_h2_s': _L0_ffn_in['h2_s'], 'L0_ffn_w3_w': _L0_ffn_in['w3_w'], 'L0_ffn_w3_s': _L0_ffn_in['w3_s'], 'L1_attn_wq': _L1_attn_in['wq'], 'L1_attn_wk': _L1_attn_in['wk'], 'L1_attn_wv': _L1_attn_in['wv'], 'L1_attn_wo': _L1_attn_in['wo'], 'L1_attn_W1': _L1_attn_in['W1'], 'L1_attn_b1': _L1_attn_in['b1'], 'L1_attn_theta': _L1_attn_in['theta'], 'L1_attn_theta_bias': _L1_attn_in['theta_bias'], 'L1_attn_alpha': _L1_attn_in['alpha'], 'L1_attn_gamma': _L1_attn_in['gamma'], 'L1_attn_beta': _L1_attn_in['beta'], 'L1_ffn_gate_w': _L1_ffn_in['gate_w'], 'L1_ffn_gate_b': _L1_ffn_in['gate_b'], 'L1_ffn_w1': _L1_ffn_in['w1'], 'L1_ffn_b1': _L1_ffn_in['b1'], 'L1_ffn_w2': _L1_ffn_in['w2'], 'L1_ffn_b2': _L1_ffn_in['b2'], 'L1_ffn_sw1': _L1_ffn_in['sw1'], 'L1_ffn_sb1': _L1_ffn_in['sb1'], 'L1_ffn_sw2': _L1_ffn_in['sw2'], 'L1_ffn_sb2': _L1_ffn_in['sb2']}
    _x0 = _d['L0_attn_x']
    _d['L0_attn_x'] = jax.random.normal(jax.random.fold_in(jax.random.key(seed), 1), (8, 256, 128), dtype=_x0.dtype)
    del _x0
    return _d

def reference(L0_attn_x, L0_attn_in_w, L0_attn_in_b, L0_attn_conv_w, L0_attn_conv_b, L0_attn_xp_w, L0_attn_xp_b, L0_attn_out_w, L0_attn_out_b, L0_ffn_w1_w, L0_ffn_w1_s, L0_ffn_w2_w, L0_ffn_w2_s, L0_ffn_h1_w, L0_ffn_h1_s, L0_ffn_h2_w, L0_ffn_h2_s, L0_ffn_w3_w, L0_ffn_w3_s, L1_attn_wq, L1_attn_wk, L1_attn_wv, L1_attn_wo, L1_attn_W1, L1_attn_b1, L1_attn_theta, L1_attn_theta_bias, L1_attn_alpha, L1_attn_gamma, L1_attn_beta, L1_ffn_gate_w, L1_ffn_gate_b, L1_ffn_w1, L1_ffn_b1, L1_ffn_w2, L1_ffn_b2, L1_ffn_sw1, L1_ffn_sb1, L1_ffn_sw2, L1_ffn_sb2):

    def _L0_attn_ref(x, in_w, in_b, conv_w, conv_b, xp_w, xp_b, out_w, out_b):
        import jax, jax.numpy as jnp
        import numpy as np
        D_STATE = 16
        D_CONV = 4

        def silu(x):
            return x * jax.nn.sigmoid(x)

        def _reference_tuple_inner(x, in_w, in_b, conv_w, conv_b, xp_w, xp_b, out_w, out_b):
            B, S, D = x.shape
            h = x @ in_w.T + in_b
            hc = jax.lax.conv_general_dilated(h.transpose(0, 2, 1), conv_w, window_strides=(1,), padding=[(D_CONV - 1, 0)], feature_group_count=conv_w.shape[0], dimension_numbers=('NCH', 'OIH', 'NCH')) + conv_b[None, :, None]
            h = silu(hc.transpose(0, 2, 1))
            xp = h @ xp_w.T + xp_b
            a = jnp.exp(-jnp.exp(xp[..., :D_STATE]))
            b = silu(xp[..., D_STATE:]) * jnp.sum(h, axis=-1, keepdims=True)

            def step(state, ab):
                a_t, b_t = ab
                state = state * a_t + b_t
                return (state, state)
            init = jnp.zeros((B, D_STATE), x.dtype)
            final_state, ys = jax.lax.scan(step, init, (a.transpose(1, 0, 2), b.transpose(1, 0, 2)))
            out = ys.transpose(1, 0, 2) @ out_w.T + out_b
            return (out, final_state)
        return _reference_tuple_inner(x, in_w, in_b, conv_w, conv_b, xp_w, xp_b, out_w, out_b)[0]

    def _L0_ffn_ref(x, w1_w, w1_s, w2_w, w2_s, h1_w, h1_s, h2_w, h2_s, w3_w, w3_s):
        import jax, jax.numpy as jnp
        import numpy as np
        D_IN, D_HID = (128, 512)

        def _ternary(key, shape):
            return jax.random.randint(key, shape, -1, 2).astype(jnp.float32)

        def _tlin(x, w, s):
            return jnp.einsum('bsi,oi->bso', x, w) * s
        h = jax.nn.silu(_tlin(x, w1_w, w1_s)) * _tlin(x, w2_w, w2_s)
        h = jax.nn.gelu(_tlin(h, h1_w, h1_s), approximate=False)
        h = jax.nn.gelu(_tlin(h, h2_w, h2_s), approximate=False)
        return _tlin(h, w3_w, w3_s)

    def _L1_attn_ref(hidden_states, wq, wk, wv, wo, W1, b1, theta, theta_bias, alpha, gamma, beta):
        import jax, jax.numpy as jnp
        import numpy as np
        B, L, DM, H, HD, K = (4, 256, 128, 16, 64, 64)
        BASE_LR = 1.0
        EPS = 1e-06

        def _ttt_forward(hidden_states, wq, wk, wv, wo, W1, b1, theta, theta_bias, alpha, gamma, beta):
            Bs, Ls, _ = hidden_states.shape
            n_chunks = Ls // K

            def proj(w):
                return (hidden_states @ w).reshape(Bs, Ls, H, HD).transpose(0, 2, 1, 3)
            xq, xk, xv = (proj(wq), proj(wk), proj(wv))

            def to_chunks(x):
                return x.reshape(Bs, H, n_chunks, K, HD).transpose(2, 0, 1, 3, 4)
            cq, ck, cv = (to_chunks(xq), to_chunks(xk), to_chunks(xv))
            token_eta = jnp.clip(1.0 / jnp.arange(1, K + 1, dtype=jnp.float32) + alpha, 0.0)[None, None, :, None]
            g = gamma[None]
            be = beta[None]
            tb = theta_bias.reshape(1, H, 1, 1)
            W0 = jnp.broadcast_to(W1[None], (Bs, H, HD, HD))
            b0 = jnp.broadcast_to(b1[None], (Bs, H, 1, HD))

            def step(carry, inp):
                W, bb = carry
                xq_c, xk_c, xv_c = inp
                lr = jax.nn.sigmoid(jnp.einsum('bhkc,hcd->bhkd', xk_c, theta) + tb)
                eta = token_eta * (BASE_LR * lr / HD)
                Z1 = xk_c @ W + bb
                mu = Z1.mean(-1, keepdims=True)
                std = jnp.sqrt(Z1.var(-1, keepdims=True) + EPS)
                x_hat = (Z1 - mu) / std
                y = g * x_hat + be
                grad_output = y - (xv_c - xk_c)
                gxh = grad_output * g
                grad_x = (HD * gxh - gxh.sum(-1, keepdims=True) - x_hat * (gxh * x_hat).sum(-1, keepdims=True)) / (HD * std)
                dW = jnp.einsum('bhkc,bhkd->bhcd', eta * xk_c, grad_x)
                db = (eta * grad_x).sum(-2, keepdims=True)
                Wn, bn = (W - dW, bb - db)
                Zq = xq_c @ Wn + bn
                mu2 = Zq.mean(-1, keepdims=True)
                std2 = jnp.sqrt(Zq.var(-1, keepdims=True) + EPS)
                out = xq_c + g * ((Zq - mu2) / std2) + be
                return ((Wn, bn), out)
            _, outs = jax.lax.scan(step, (W0, b0), (cq, ck, cv))
            out = outs.transpose(1, 2, 0, 3, 4).reshape(Bs, H, Ls, HD)
            out = out.transpose(0, 2, 1, 3).reshape(Bs, Ls, H * HD)
            return out @ wo
        return _ttt_forward(hidden_states, wq, wk, wv, wo, W1, b1, theta, theta_bias, alpha, gamma, beta)

    def _L1_ffn_ref(x, gate_w, gate_b, w1, b1, w2, b2, sw1, sb1, sw2, sb2):
        import jax, jax.numpy as jnp
        import numpy as np
        H = 128
        E = 8
        TOP_K = 2
        FF = 4 * H
        B, S = (2, 256)

        def _moe_forward(x, gate_w, gate_b, w1, b1, w2, b2, sw1, sb1, sw2, sb2):
            b, s, h = x.shape
            xf = x.reshape(-1, h)
            scores = jax.nn.sigmoid(xf @ gate_w.T + gate_b)
            top_scores, top_idx = jax.lax.top_k(scores, TOP_K)
            top_scores = top_scores / (top_scores.sum(-1, keepdims=True) + 1e-06)
            comb = (jax.nn.one_hot(top_idx, E, dtype=xf.dtype) * top_scores[..., None]).sum(1)
            hdn = jax.nn.gelu(jnp.einsum('th,ehf->etf', xf, w1) + b1[:, None, :], approximate=False)
            y = jnp.einsum('etf,efh->eth', hdn, w2) + b2[:, None, :]
            routed = jnp.einsum('te,eth->th', comb, y)
            shared = (jax.nn.gelu(xf @ sw1 + sb1, approximate=False) @ sw2 + sb2) * 0.1
            return (routed + shared).reshape(b, s, h)
        return _moe_forward(x, gate_w, gate_b, w1, b1, w2, b2, sw1, sb1, sw2, sb2)
    x = L0_attn_x
    xn = _layernorm(x, axis=-1)
    x = x + _L0_attn_ref(xn, L0_attn_in_w, L0_attn_in_b, L0_attn_conv_w, L0_attn_conv_b, L0_attn_xp_w, L0_attn_xp_b, L0_attn_out_w, L0_attn_out_b) + _L0_ffn_ref(xn, L0_ffn_w1_w, L0_ffn_w1_s, L0_ffn_w2_w, L0_ffn_w2_s, L0_ffn_h1_w, L0_ffn_h1_s, L0_ffn_h2_w, L0_ffn_h2_s, L0_ffn_w3_w, L0_ffn_w3_s)
    xn = _layernorm(x, axis=-1)
    x = x + _L1_attn_ref(xn, L1_attn_wq, L1_attn_wk, L1_attn_wv, L1_attn_wo, L1_attn_W1, L1_attn_b1, L1_attn_theta, L1_attn_theta_bias, L1_attn_alpha, L1_attn_gamma, L1_attn_beta) + _L1_ffn_ref(xn, L1_ffn_gate_w, L1_ffn_gate_b, L1_ffn_w1, L1_ffn_b1, L1_ffn_w2, L1_ffn_b2, L1_ffn_sw1, L1_ffn_sb1, L1_ffn_sw2, L1_ffn_sb2)
    return x

_drawn_inputs = setup_inputs


def setup_inputs(seed=0):
    import zlib

    import numpy as np

    out = dict(_drawn_inputs(seed))
    spreads = {'L1_attn_b1': (0.0, 0.1),
     'L1_attn_theta_bias': (0.0, 0.1),
     'L1_attn_alpha': (0.0, 0.1),
     'L1_attn_gamma': (1.0, 0.2),
     'L1_attn_beta': (0.0, 0.1),
     'L1_ffn_gate_b': (0.0, 0.1),
     'L1_ffn_b1': (0.0, 0.1),
     'L1_ffn_b2': (0.0, 0.1),
     'L1_ffn_sb1': (0.0, 0.1),
     'L1_ffn_sb2': (0.0, 0.1)}
    factors = {}
    for name, (base, spread) in spreads.items():
        noise = np.random.default_rng([zlib.crc32(name.encode()), seed]).standard_normal(out[name].shape)
        drawn = base * np.exp(spread * noise) if base else spread * noise
        out[name] = jnp.asarray(drawn.astype(out[name].dtype))
    for name, factor in factors.items():
        out[name] = (out[name] * factor).astype(out[name].dtype)
    return out
```

```python
from contextlib import ExitStack

import concourse.bass as bass
from concourse import mybir

F32 = mybir.dt.float32
I32 = mybir.dt.int32
U32 = mybir.dt.uint32
ALU = mybir.AluOpType
ACT = mybir.ActivationFunctionType
AX_X = mybir.AxisListType.X

P = 128
BATCH, SEQ, D = 8, 256, 128
TOK = BATCH * SEQ
NB = 512
NBLK = TOK // NB
BPB = NB // SEQ
HID = 512
KC = HID // P
DI, NST, TAPS = 256, 16, 4
DC = DI // P
PAD = TAPS - 1
NH, HD, CH = 16, 64, 64
NCH = SEQ // CH
NQ = NH // 2
QD = NQ * HD
EXP = 8
NE = EXP + 1
LN_EPS, TTT_EPS, TOPK_EPS = 1e-5, 1e-6, 1e-6

COLS = {}
_at = 0
for _name, _n in (("in_b", DC), ("conv_w", DC * TAPS), ("conv_b", DC), ("w1_s", KC), ("w2_s", KC),
                  ("h1_s", KC), ("h2_s", KC), ("w3_s", 1), ("out_b", 1), ("gamma", NQ), ("beta", NQ),
                  ("b1", NE * KC), ("sb2", 1), ("theta", 2 * NQ), ("alpha", 1), ("inv_index", 1),
                  ("theta_bias", NH), ("gate_b", EXP), ("expert_no", EXP)):
    COLS[_name] = (_at, _n)
    _at += _n
NCOLS = _at
M_CENTER, M_MEAN, M_NEG, M_VAR, M_IDENT = range(5)


class Signal:

    def __init__(self, sem, per):
        self.sem, self.per = sem, per

    def at(self, i, k):
        return i * self.per + (k + self.per)

    def before(self, i, k):
        return i * self.per + k


def build(nc, a, out):
    with ExitStack() as ctx:
        def sb(name, shape, dt=F32):
            return ctx.enter_context(nc.sbuf_tensor(name, shape, dt))

        def sem(name):
            return ctx.enter_context(nc.semaphore(name))

        credited = []

        def signal(name, per):
            s = Signal(sem(name), per)
            credited.append(s)
            return s

        x_sb = sb("x_sb", [P, TOK])
        xn = sb("xn", [P, TOK])
        mats = sb("mats", [P, 5 * P])
        cols = sb("cols", [P, NCOLS])
        eps_ln = sb("eps_ln", [P, 2])

        def mat(n):
            return mats[:, n * P:(n + 1) * P]

        def col(name, k=0, n=1, rows=P):
            return cols[0:rows, COLS[name][0] + k:COLS[name][0] + k + n]

        in_w = sb("in_w", [P, DI])
        l0 = sb("l0", [P, 2 * KC * HID + 2 * HID + KC * D])
        h1 = l0[:, 0:KC * HID].rearrange("p (k n) -> p k n", k=KC)
        h2 = l0[:, KC * HID:2 * KC * HID].rearrange("p (k n) -> p k n", k=KC)
        w1, w2 = (l0[:, 2 * KC * HID + n * HID:2 * KC * HID + (n + 1) * HID] for n in range(2))
        w3 = l0[:, 2 * KC * HID + 2 * HID:].rearrange("p (k n) -> p k n", k=KC)
        xp_w = sb("xp_w", [P, DC, 96])
        xp_row = sb("xp_row", [1, 96 + NB])
        out_w = sb("out_w", [NST, D])

        wq = sb("wq", [P, NH * HD])
        wk = sb("wk", [P, NH * HD])
        wt = sb("wt", [P, NH * HD])
        wo = sb("wo", [P, NQ, D])
        mw1 = sb("mw1", [P, NE, HID])
        mw2 = sb("mw2", [P, NE * KC, D])
        mb2 = sb("mb2", [EXP, D])
        gate_w = sb("gate_w", [P, EXP])
        wqo = sb("wqo", [P, D])
        w_th = sb("w_th", [P, NH])
        be_wo = sb("be_wo", [P, 1])
        w_init = sb("w_init", [P, QD])
        e_init = sb("e_init", [P, NH * HD])
        gg = sb("gg", [P, NH * HD])
        gb = sb("gb", [P, NH * HD])

        work = sb("work", [P, 12288])
        used = [0]

        def cut(n):
            used[0] += n
            assert used[0] <= 12288
            return work[:, used[0] - n:used[0]]

        hpad = cut(DC * BPB * (PAD + SEQ)).rearrange("p (c b s) -> p c b s", c=DC, b=BPB)
        conv = cut(DC * NB).rearrange("p (c n) -> p c n", c=DC)
        hs = cut(DC * NB).rearrange("p (c n) -> p c n", c=DC)
        u0 = cut(KC * NB).rearrange("p (c n) -> p c n", c=KC)
        g1 = cut(KC * NB).rearrange("p (c n) -> p c n", c=KC)
        g2 = u0
        ssm = cut(5 * NB).rearrange("p (c n) -> p c n", c=5)
        res = cut(NB)
        lsq = cut(2 * NB)
        used[0] = 0
        wqT = cut(NQ * P).rearrange("p (q n) -> p q n", q=NQ)
        wkT = cut(NQ * P).rearrange("p (q n) -> p q n", q=NQ)
        prep = cut(NH * HD)
        gam = cut(NH * HD)
        bet = cut(NH * HD)
        pstat = cut(16)
        used[0] = 0
        xkT = cut(NQ * NB).rearrange("p (q n) -> p q n", q=NQ)
        xqT = cut(NQ * NB).rearrange("p (q n) -> p q n", q=NQ)
        hid = cut(2 * KC * NB).rearrange("p (e f n) -> p e f n", e=2, f=KC)
        xb = sb("xb", [P, NB])
        combT = sb("combT", [EXP, NB])
        comb_bc = sb("comb_bc", [P, EXP, NB])
        xh, gx, eg, esum, kt_even = (l0[:, n * NH * HD:(n + 1) * NH * HD] for n in range(5))
        ktok = [kt_even, sb("kt_odd", [P, NH * HD])]
        ttok = sb("ttok", [P, 2, NH * HD])
        sq = sb("sq", [P, NH * HD])
        wst = sb("wst", [P, BPB, QD])
        macc = sb("macc", [P, NB])
        mtmp = sb("mtmp", [P, NB])
        osb = l0[:, 5 * NH * HD:5 * NH * HD + NB]
        small = sb("small", [P, 400])
        idx = sb("idx", [P, 4, 8], U32)

        ps = ctx.enter_context(nc.psum_tensor("ps", [P, 8 * NB], F32))

        def bank(n, rows=P, a0=0):
            return ps[a0:a0 + rows, n * NB:(n + 1) * NB]

        comb_dram = nc.dram_tensor("comb_dram", (EXP, NB), F32, kind="Internal").ap()

        ld_x, ld_small, ld_a, ld_b, ld_c = (sem(n) for n in ("ld_x", "ld_small", "ld_a", "ld_b", "ld_c"))
        ld_prep = sem("ld_prep")
        eps_set, pads_set = sem("eps_set"), sem("pads_set")
        stand, stand_dve = sem("stand"), sem("stand_dve")
        ln_centred, ln_sq, ln_var, ln_sd, ln_rs = (
            sem(n) for n in ("ln_centred", "ln_sq", "ln_var", "ln_sd", "ln_rs"))
        ln_out = signal("ln_out", 1)
        a_in = signal("a_in", DC)
        a_pad = signal("a_pad", DC)
        a_conv = signal("a_conv", DC)
        a_hs = signal("a_hs", DC)
        a_w12 = signal("a_w12", KC)
        a_silu = signal("a_silu", KC)
        a_u = signal("a_u", KC)
        a_h1 = signal("a_h1", KC)
        a_g1 = signal("a_g1", KC)
        a_h2 = signal("a_h2", KC)
        a_g2 = signal("a_g2", KC)
        a_xp = signal("a_xp", 1)
        a_ex = signal("a_ex", 5)
        a_b = signal("a_b", 2)
        a_y = signal("a_y", BPB)
        a_o = signal("a_o", 1)
        a_w3 = signal("a_w3", 1)
        a_res = signal("a_res", 2)
        a_step = sem("a_step")
        p_dve, p_pe, p_act = sem("p_dve"), sem("p_pe"), sem("p_act")
        b_xb = signal("b_xb", 1)
        b_gate = signal("b_gate", 1)
        b_gz = signal("b_gz", 2)
        b_th = signal("b_th", 2)
        b_comb = signal("b_comb", 1)
        b_ct = signal("b_ct", 1)
        b_ctc = signal("b_ctc", 1)
        b_cst = signal("b_cst", 16)
        b_cbc = signal("b_cbc", 16)
        NRING = 2 * NQ + 4 * NCH + NE * KC + NQ
        r_pe = signal("r_pe", NRING)
        RA = NQ + 2 * NCH + NE * KC + NQ
        r_act = signal("r_act", RA)
        r_dve = signal("r_dve", NQ + 2 * NCH)
        b_eta = signal("b_eta", 1)
        z_pe = signal("z_pe", 2 * NCH)
        z_sq = signal("z_sq", 2 * NCH)
        z_ve = signal("z_ve", NCH)
        z_r = signal("z_r", NCH)
        z_xh = signal("z_xh", 2 * NCH)
        z_gm = signal("z_gm", 2 * NCH)
        z_gx = signal("z_gx", 2 * NCH)
        z_s2 = signal("z_s2", 2 * NCH)
        z_u = signal("z_u", 2 * NCH)
        z_eg = signal("z_eg", 2 * NCH)
        z_es = signal("z_es", 2 * NCH)
        w_pe = signal("w_pe", 2 * NCH)
        w_dve = signal("w_dve", 2 * NCH)
        q_pe = signal("q_pe", 2 * NCH)
        q_act = signal("q_act", 2 * NCH)
        m_pe = signal("m_pe", NE)
        m_mul = signal("m_mul", NE)
        m_add = signal("m_add", NE - 1)
        t_sq = signal("t_sq", NQ)
        t_rs = signal("t_rs", NQ)
        t_xh = signal("t_xh", NQ)
        t_out = signal("t_out", 1)
        t_res = signal("t_res", 2)
        t_dma = signal("t_dma", 16)
        b_step = sem("b_step")
        BSTEPS = 12 + 14 * NCH

        RING0 = 4
        ring = [("k", q, r_act) for q in range(NQ)] + [("q", q, r_dve) for q in range(NQ)]

        def ring_tok(c):
            return [("t", (c, p), r_dve) for p in range(2)] + [("kt", (c, p), r_act) for p in range(2)]

        def ring_up(e):
            return [("up", (e, f), r_act) for f in range(KC)]

        ring += ring_tok(0)
        for c in range(NCH):
            if c + 1 < NCH:
                ring += ring_tok(c + 1)
            ring += ring_up(2 * c) + ring_up(2 * c + 1)
        ring += ring_up(EXP)
        ring += [("v", q, r_act) for q in range(NQ)]
        assert len(ring) == NRING
        ring_no = {(k, w): n for n, (k, w, _) in enumerate(ring)}
        taken_no = {}
        for s in (r_act, r_dve):
            for n, (k, w, _) in enumerate([r for r in ring if r[2] is s]):
                taken_no[(k, w)] = n + 1
        assert sum(r[2] is r_act for r in ring) == RA

        def ring_bank(kind, which):
            return RING0 + ring_no[(kind, which)] % 3

        def by_parity(t, p):
            return t[:, :].rearrange("p (q h d) -> p h q d", h=2, d=HD)[:, p]

        def by_batch(t):
            return t.rearrange("p (b c k) -> p b c k", b=BPB, c=NCH)

        def by_chunk(t):
            return t.rearrange("p (c b k) -> p b c k", b=BPB, c=NCH)

        def over_d(t):
            return t.unsqueeze(2).to_broadcast([P, NQ, HD])

        def qd(t):
            return t.rearrange("p (q d) -> p q d", q=NQ)

        def blk(i):
            return bass.ds(i * NB, NB)

        block = ctx.enter_context(nc.Block())

        @block.sync
        def _(sp):
            for s in credited:
                sp.sem_inc(s.sem, s.per)
            sp.dma_start(mats[:, :], a["mats"]).then_inc(ld_x, 16)
            sp.dma_start(x_sb[:, :], a["xT"]).then_inc(ld_x, 16)
            sp.dma_start(cols[:, :], a["cols"]).then_inc(ld_small, 16)
            sp.dma_start(in_w[:, :], a["in_w"]).then_inc(ld_a, 16)
            sp.dma_start(w1[:, :], a["w1"]).then_inc(ld_a, 16)
            sp.dma_start(w2[:, :], a["w2"]).then_inc(ld_a, 16)
            sp.dma_start(xp_w[:, :, :], a["xp_w"]).then_inc(ld_a, 16)
            sp.dma_start(xp_row[:, :], a["xp_row"]).then_inc(ld_a, 16)
            sp.dma_start(out_w[:, :], a["out_w"]).then_inc(ld_a, 16)
            sp.dma_start(h1[:, :, :], a["h1"]).then_inc(ld_b, 16)
            sp.dma_start(h2[:, :, :], a["h2"]).then_inc(ld_b, 16)
            sp.dma_start(w3[:, :, :], a["w3"]).then_inc(ld_b, 16)
            for dst, name in ((wq, "wq"), (wk, "wk"), (wt, "wv"), (mb2, "mb2"), (gate_w, "gate_w"),
                              (w_init, "w_init")):
                sp.dma_start(dst[:, :], a[name]).then_inc(ld_c, 16)
            sp.dma_start(e_init[:, :], a["e_init"]).then_inc(ld_c, 16)
            sp.dma_start(wo[:, :, :], a["wo"]).then_inc(ld_c, 16)
            sp.dma_start(mw1[:, :, :], a["mw1"]).then_inc(ld_c, 16)
            sp.dma_start(mw2[:, :, :], a["mw2"]).then_inc(ld_c, 16)
            sp.wait_ge(ln_out.sem, ln_out.at(2 * NBLK - 1, 1))
            sp.dma_start(wqT, a["wqT"]).then_inc(ld_prep, 16)
            sp.dma_start(wkT, a["wkT"]).then_inc(ld_prep, 16)
            sp.dma_start(gam, a["gamma_row"].partition_broadcast(P)).then_inc(ld_prep, 16)
            sp.dma_start(bet, a["beta_row"].partition_broadcast(P)).then_inc(ld_prep, 16)
            with sp.Fori(0, NBLK) as i:
                sp.wait_ge(b_ctc.sem, b_ctc.at(i, 1))
                sp.wait_ge(b_cbc.sem, b_cbc.before(i, 16))
                sp.dma_start(comb_dram, combT[:, :]).then_inc(b_cst.sem, 16)
                sp.wait_ge(b_cst.sem, b_cst.at(i, 16))
                sp.wait_ge(m_mul.sem, m_mul.before(i, NE))
                sp.dma_start(comb_bc[:, :, :], comb_dram.partition_broadcast(P)).then_inc(b_cbc.sem, 16)
                sp.wait_ge(t_res.sem, t_res.at(i, 2))
                sp.dma_start(out[:, bass.ds(i * NB, NB)], osb[:, :]).then_inc(t_dma.sem, 16)
            sp.wait_ge(t_dma.sem, t_dma.at(NBLK - 1, 16))

        @block.gpsimd
        def _(pool):
            pool.memset(eps_ln[:, 0:1], LN_EPS).then_inc(eps_set, 1)
            pool.memset(eps_ln[:, 1:2], TTT_EPS).then_inc(eps_set, 1)
            pool.memset(hpad[:, :, :, 0:PAD], 0.0).then_inc(pads_set, 1)
            pool.memset(small[:, 384:400], -0.5).then_inc(eps_set, 1)
            pool.wait_ge(eps_set, 3)
            with pool.Fori(0, NBLK) as i:
                for c in range(NCH):
                    pool.wait_ge(z_ve.sem, z_ve.at(i, c + 1))
                    pool.wait_ge(w_dve.sem, w_dve.before(i, 2 * c + 2) if c == 0 else w_dve.at(i, 2 * c))
                    pool.tensor_tensor(small[:, 16:32], small[:, 0:16], small[:, 384:400],
                                       ALU.pow).then_inc(z_r.sem, 1)
                    for p in range(2):
                        h = slice(p * QD, (p + 1) * QD)
                        pool.wait_ge(z_xh.sem, z_xh.at(i, 2 * c + p + 1))
                        pool.tensor_tensor(gx[:, h].rearrange("p (q d) -> p q d", q=NQ),
                                           xh[:, h].rearrange("p (q d) -> p q d", q=NQ),
                                           by_parity(gg, p), ALU.mult).then_inc(z_gm.sem, 1)
                        pool.wait_ge(z_gm.sem, z_gm.at(i, 2 * c + p + 1))
                        pool.wait_ge(r_dve.sem, r_dve.at(i, taken_no[("t", (c, p))]))
                        pool.tensor_tensor(gx[:, h], gx[:, h], ttok[:, c % 2, h],
                                           ALU.add).then_inc(z_gx.sem, 1)
                    for p in range(2):
                        h = slice(p * QD, (p + 1) * QD)
                        pool.wait_ge(z_s2.sem, z_s2.at(i, 2 * c + p + 1))
                        pool.tensor_tensor(sq[:, h].rearrange("p (q d) -> p q d", q=NQ),
                                           xh[:, h].rearrange("p (q d) -> p q d", q=NQ),
                                           over_d(small[:, 48 + 8 * p:56 + 8 * p]),
                                           ALU.mult).then_inc(z_u.sem, 1)
                    for p in range(2):
                        h = slice(p * QD, (p + 1) * QD)
                        pool.wait_ge(z_eg.sem, z_eg.at(i, 2 * c + p + 1))
                        pool.tensor_tensor(by_parity(esum, p), by_parity(e_init if c == 0 else esum, p),
                                           by_parity(eg, p), ALU.add).then_inc(z_es.sem, 1)

        @block.tensor
        def _(pe):
            def layernorm(turn):
                base = turn * NBLK
                with pe.Fori(0, NBLK) as i:
                    if turn:
                        pe.wait_ge(a_res.sem, a_res.at(NBLK - 1, 2))
                    pe.matmul(ps[:, bass.ds(i * 2 * NB, NB)], mat(M_CENTER), x_sb[:, blk(i)],
                              start=True, stop=True).then_inc(ln_centred, 1)
                    pe.wait_ge(ln_sq, i + base + 1)
                    pe.matmul(ps[:, bass.ds(i * 2 * NB + NB, NB)], mat(M_MEAN), lsq[:, bass.ds(0, NB)],
                              start=True, stop=True).then_inc(ln_var, 1)

            pe.wait_ge(ld_x, 32)
            layernorm(0)
            pe.wait_ge(ln_out.sem, ln_out.at(NBLK - 1, 1))
            pe.wait_ge(ld_a, 6 * 16)
            with pe.Fori(0, NBLK) as i:
                for m in range(DC):
                    pe.wait_ge(a_g2.sem, a_g2.before(i, 2 + m + 1))
                    pe.matmul(bank(m), in_w[:, m * P:(m + 1) * P], xn[:, blk(i)],
                              start=True, stop=True).then_inc(a_in.sem, 1)
                for m in range(KC):
                    b = (2 + 2 * m) % 8
                    if m == 0:
                        pe.wait_ge(a_res.sem, a_res.before(i, 2))
                    if m == 1:
                        pe.wait_ge(a_g2.sem, a_g2.before(i, 2))
                    if m == 3:
                        pe.wait_ge(a_pad.sem, a_pad.at(i, DC))
                    pe.matmul(bank(b), w1[:, m * P:(m + 1) * P], xn[:, blk(i)], start=True, stop=True)
                    pe.matmul(bank(b + 1), w2[:, m * P:(m + 1) * P], xn[:, blk(i)],
                              start=True, stop=True).then_inc(a_w12.sem, 1)
                pe.wait_ge(ld_b, 3 * 16)
                pe.wait_ge(a_u.sem, a_u.at(i, 2))
                for k in range(KC):
                    pe.wait_ge(a_u.sem, a_u.at(i, k + 1))
                    for m in range(KC):
                        mm = pe.matmul(bank(2 + m), h1[:, k, m * P:(m + 1) * P], u0[:, k],
                                       start=(k == 0), stop=(k == KC - 1), skip_group_check=True)
                        if k == KC - 1:
                            mm.then_inc(a_h1.sem, 1)
                for k in range(KC):
                    pe.wait_ge(a_g1.sem, a_g1.at(i, k + 1))
                    for m in range(KC):
                        mm = pe.matmul(bank((6 + m) % 8), h2[:, k, m * P:(m + 1) * P], g1[:, k],
                                       start=(k == 0), stop=(k == KC - 1), skip_group_check=True)
                        if k == KC - 1:
                            mm.then_inc(a_h2.sem, 1)
                pe.wait_ge(a_hs.sem, a_hs.at(i, DC))
                for k in range(DC):
                    pe.matmul(bank(3, 96), xp_w[:, k], hs[:, k], start=(k == 0), stop=False)
                pe.matmul(bank(3, 96), xp_row[:, 0:96], xp_row[:, 96:96 + NB], start=False,
                          stop=True).then_inc(a_xp.sem, 1)
                for k in range(KC):
                    pe.wait_ge(a_g2.sem, a_g2.at(i, k + 1))
                    mm = pe.matmul(bank(2), w3[:, k], g2[:, k], start=(k == 0), stop=(k == KC - 1))
                mm.then_inc(a_w3.sem, 1)
                pe.wait_ge(a_y.sem, a_y.at(i, BPB))
                pe.matmul(bank(4), out_w[:, :], ssm[0:NST, 4], start=True, stop=True).then_inc(a_o.sem, 1)
            layernorm(1)

            pe.wait_ge(ln_out.sem, ln_out.at(2 * NBLK - 1, 1))
            pe.wait_ge(ld_c, 10 * 16)
            pe.wait_ge(ld_prep, 4 * 16)
            for q in range(NQ):
                pe.matmul(ps[:, 0:P], wqT[:, q], wo[:, q], start=(q == 0), stop=(q == NQ - 1))
            for q in range(NQ):
                pe.matmul(ps[:, NB:NB + 1], wo[:, q], col("beta", q), start=(q == 0), stop=(q == NQ - 1))
            for q in range(NQ):
                mm = pe.matmul(ps[:, 2 * NB:2 * NB + NH].rearrange("p (h q) -> p q h", h=2)[:, q],
                               wkT[:, q], col("theta", 2 * q, 2), start=True, stop=True)
            mm.then_inc(p_pe, 1)
            pe.wait_ge(p_dve, 14)

            with pe.Fori(0, NBLK) as i:
                def free(kind, which):
                    n = ring_no[(kind, which)] - 3
                    if n < 0:
                        n = max(m for m in range(-3, 0) if (m + NRING) % 3 == (n + 3) % 3)
                    k, w, s = ring[n]
                    pe.wait_ge(s.sem, (s.before if n < 0 else s.at)(i, taken_no[(k, w)]))
                    return bank(ring_bank(kind, which))

                def tokens(c):
                    return xb[:, c * P:(c + 1) * P]

                def project_tokens(c):
                    for kind, w in (("t", wt), ("kt", wk)):
                        for p in range(2):
                            pe.matmul(free(kind, (c, p)), tokens(c), by_parity(w, p), start=True,
                                      stop=True).then_inc(r_pe.sem, 1)

                def up(e):
                    for f in range(KC):
                        pe.matmul(free("up", (e, f)), mw1[:, e, f * P:(f + 1) * P], xn[:, blk(i)],
                                  start=True, stop=True).then_inc(r_pe.sem, 1)

                def down(e):
                    pe.wait_ge(m_mul.sem, m_mul.at(i, e) if e else m_mul.before(i, NE))
                    for f in range(KC):
                        pe.wait_ge(r_act.sem, r_act.at(i, taken_no[("up", (e, f))]))
                        mm = pe.matmul(bank(7), mw2[:, e * KC + f], hid[:, e % 2, f], start=(f == 0),
                                       stop=(f == KC - 1))
                    mm.then_inc(m_pe.sem, 1)

                pe.wait_ge(b_xb.sem, b_xb.at(i, 1))
                pe.wait_ge(t_res.sem, t_res.before(i, 2))
                for j in range(NB // P):
                    pe.matmul(ps[:, j * EXP:(j + 1) * EXP], xb[:, j * P:(j + 1) * P], gate_w[:, :],
                              start=True, stop=True)
                for c in range(NCH):
                    mm = pe.matmul(ps[:, 64 + c * NH:64 + (c + 1) * NH], tokens(c), w_th[:, :],
                                   start=True, stop=True)
                mm.then_inc(b_gate.sem, 1)
                for q in range(NQ):
                    pe.matmul(free("k", q), wk[:, q * P:(q + 1) * P], xb[:, :], start=True,
                              stop=True).then_inc(r_pe.sem, 1)
                pe.wait_ge(b_comb.sem, b_comb.at(i, 1))
                for j in range(NB // P):
                    mm = pe.transpose(ps[0:EXP, NB + j * P:NB + (j + 1) * P],
                                      small[:, 96 + 8 * j:104 + 8 * j], mat(M_IDENT))
                mm.then_inc(b_ct.sem, 1)
                for q in range(NQ):
                    pe.matmul(free("q", q), wq[:, q * P:(q + 1) * P], xb[:, :], start=True,
                              stop=True).then_inc(r_pe.sem, 1)
                project_tokens(0)
                pe.wait_ge(b_gz.sem, b_gz.at(i, 2))
                pe.wait_ge(b_ctc.sem, b_ctc.at(i, 1))
                for c in range(NCH):
                    w_now = w_init[:, :] if c == 0 else None
                    e_now = e_init if c == 0 else esum
                    if c:
                        pe.wait_ge(z_es.sem, z_es.at(i, 2 * c))
                        pe.wait_ge(w_dve.sem, w_dve.at(i, 2 * c))
                    else:
                        pe.wait_ge(r_act.sem, r_act.at(i, taken_no[("k", NQ - 1)]))
                    for p in range(2):
                        pe.matmul(bank(p), mat(M_NEG), by_parity(e_now, p), start=True,
                                  stop=False, skip_group_check=True)
                        for q in range(NQ):
                            for b in range(BPB):
                                r = slice(64 * p, 64 * p + 64)
                                w_b = w_init[r, q * HD:(q + 1) * HD] if c == 0 else \
                                    wst[r, b, q * HD:(q + 1) * HD]
                                at = c * P + b * CH
                                mm = pe.matmul(ps[64 * b:64 * b + 64, p * NB + q * HD:p * NB + (q + 1) * HD],
                                               xkT[r, q, at:at + CH], w_b, start=False, stop=True,
                                               skip_group_check=True)
                        mm.then_inc(z_pe.sem, 1)
                    if c + 1 < NCH:
                        project_tokens(c + 1)
                    up(2 * c)
                    down(2 * c)
                    up(2 * c + 1)
                    pe.wait_ge(z_eg.sem, z_eg.at(i, 2 * c + 2))
                    pe.wait_ge(r_act.sem, r_act.at(i, taken_no[("kt", (c, 1))]))
                    pe.wait_ge(q_act.sem, q_act.at(i, 2 * c) if c else q_act.before(i, 2 * NCH))
                    pe.sem_inc(stand, 1)
                    for b in range(BPB):
                        for q in range(NQ):
                            for p in range(2):
                                r = slice(64 * b, 64 * b + 64)
                                h = slice(p * QD + q * HD, p * QD + (q + 1) * HD)
                                nat = slice((2 * q + p) * HD, (2 * q + p + 1) * HD)
                                mm = pe.matmul(ps[64 * p:64 * p + 64, (2 + b) * NB + q * HD:(2 + b) * NB + (q + 1) * HD],
                                               ktok[c % 2][r, h], eg[r, nat], start=True, stop=True,
                                               skip_group_check=True)
                        mm.then_inc(w_pe.sem, 1)
                    down(2 * c + 1)
                    pe.wait_ge(w_dve.sem, w_dve.at(i, 2 * c + 2))
                    pe.wait_ge(z_es.sem, z_es.at(i, 2 * c + 2))
                    if c == 0:
                        pe.wait_ge(r_dve.sem, r_dve.at(i, taken_no[("q", NQ - 1)]))
                    for s in range(2):
                        for q in range(4 * s, 4 * s + 4):
                            at = (2 + s) * NB + (q % 4) * P
                            pe.matmul(ps[:, at:at + P],
                                      esum[:, q * P:(q + 1) * P],
                                      mat(M_NEG), start=(q % 4 == 0), stop=False, skip_group_check=True)
                        for q in range(4 * s, 4 * s + 4):
                            for b in range(BPB):
                                for p in range(2):
                                    r = slice(64 * p, 64 * p + 64)
                                    at = (2 + s) * NB + (q % 4) * P + b * CH
                                    fr = c * P + b * CH
                                    mm = pe.matmul(ps[r, at:at + CH], wst[r, b, q * HD:(q + 1) * HD],
                                                   xqT[r, q, fr:fr + CH], start=False, stop=True,
                                                   skip_group_check=True)
                        mm.then_inc(q_pe.sem, 1)
                up(EXP)
                down(EXP)
                pe.wait_ge(q_act.sem, q_act.at(i, 2 * NCH))
                pe.matmul(bank(2), wqo[:, :], xn[:, blk(i)], start=True, stop=False)
                pe.matmul(bank(2), mb2[:, :], combT[:, :], start=False, stop=False)
                for q in range(NQ):
                    pe.wait_ge(t_sq.sem, t_sq.at(i, q + 1))
                    pe.matmul(free("v", q), mat(M_VAR), sq[:, (q % 2) * NB:(q % 2) * NB + NB], start=True,
                              stop=True).then_inc(r_pe.sem, 1)
                    if q:
                        pe.wait_ge(t_xh.sem, t_xh.at(i, q))
                        pe.matmul(bank(2), wo[:, q - 1], xqT[:, q - 1], start=False, stop=False)
                pe.wait_ge(t_xh.sem, t_xh.at(i, NQ))
                pe.matmul(bank(2), wo[:, NQ - 1], xqT[:, NQ - 1], start=False, stop=True).then_inc(t_out.sem, 1)

        @block.scalar
        def _(act):
            def layernorm(turn):
                base = turn * NBLK
                with act.Fori(0, NBLK) as i:
                    act.wait_ge(ln_centred, i + base + 1)
                    act.activation(lsq[:, 0:NB], ps[:, bass.ds(i * 2 * NB, NB)],
                                   ACT.Square).then_inc(ln_sq, 1)
                    act.wait_ge(ln_var, i + base + 1)
                    act.activation(lsq[:, NB:2 * NB], ps[:, bass.ds(i * 2 * NB + NB, NB)], ACT.Sqrt,
                                   bias=eps_ln[:, 0:1]).then_inc(ln_sd, 1)
                    act.wait_ge(ln_rs, i + base + 1)

            act.wait_ge(eps_set, 3)
            layernorm(0)
            act.wait_ge(ld_small, 16)
            act.wait_ge(pads_set, 1)
            with act.Fori(0, NBLK) as i:
                for m in range(DC):
                    act.wait_ge(a_in.sem, a_in.at(i, m + 1))
                    act.wait_ge(a_conv.sem, a_conv.before(i, m + 1))
                    act.activation(hpad[:, m, :, PAD:PAD + SEQ], bank(m).rearrange("p (b s) -> p b s", b=BPB),
                                   ACT.Identity, bias=col("in_b", m)).then_inc(a_pad.sem, 1)
                for m in range(KC):
                    act.wait_ge(a_w12.sem, a_w12.at(i, m + 1))
                    if m == 0:
                        act.wait_ge(a_w3.sem, a_w3.before(i, 1))
                    act.activation(u0[:, m], bank((2 + 2 * m) % 8), ACT.Silu,
                                   scale=col("w1_s", m)).then_inc(a_silu.sem, 1)
                for m in range(DC):
                    act.wait_ge(a_conv.sem, a_conv.at(i, m + 1))
                    act.activation(hs[:, m], conv[:, m], ACT.Silu, bias=col("conv_b", m)).then_inc(a_hs.sem, 1)
                for m in range(KC):
                    act.wait_ge(a_h1.sem, a_h1.at(i, m + 1))
                    act.activation(g1[:, m], bank(2 + m), ACT.Gelu, scale=col("h1_s", m)).then_inc(a_g1.sem, 1)
                for m in range(KC):
                    act.wait_ge(a_h2.sem, a_h2.at(i, m + 1))
                    act.activation(g2[:, m], bank((6 + m) % 8), ACT.Gelu, scale=col("h2_s", m)).then_inc(a_g2.sem, 1)
                act.wait_ge(a_xp.sem, a_xp.at(i, 1))
                act.wait_ge(a_y.sem, a_y.before(i, BPB))
                act.activation(ssm[0:NST, 0], bank(3, NST), ACT.Exp).then_inc(a_ex.sem, 1)
                act.activation(ssm[0:NST, 1], bank(3, NST, 32), ACT.Copy).then_inc(a_ex.sem, 1)
                act.activation(ssm[0:NST, 2], bank(3, NST, 64), ACT.Copy).then_inc(a_ex.sem, 1)
                act.activation(ssm[0:NST, 3], bank(3, NST, 32), ACT.Tanh, scale=0.5).then_inc(a_ex.sem, 1)
                act.wait_ge(a_ex.sem, a_ex.at(i, 1))
                act.activation(ssm[0:NST, 0], ssm[0:NST, 0], ACT.Exp, scale=-1.0).then_inc(a_ex.sem, 1)
            layernorm(1)

            act.wait_ge(p_dve, 14)
            with act.Fori(0, NBLK) as i:
                def take(kind, which):
                    act.wait_ge(r_pe.sem, r_pe.at(i, ring_no[(kind, which)] + 1))
                    return bank(ring_bank(kind, which))

                def keys_by_token(c):
                    for p in range(2):
                        src = take("kt", (c, p))
                        act.wait_ge(w_pe.sem, w_pe.at(i, 2 * c - 2) if c >= 2 else w_pe.before(i, 2 * NCH))
                        act.activation(ktok[c % 2][:, p * QD:(p + 1) * QD], src, ACT.Copy).then_inc(r_act.sem, 1)

                def gelus(e):
                    act.wait_ge(m_pe.sem, m_pe.at(i, e - 1) if e >= 2 else m_pe.before(i, NE))
                    for f in range(KC):
                        act.activation(hid[:, e % 2, f], take("up", (e, f)), ACT.Gelu,
                                       bias=col("b1", e * KC + f)).then_inc(r_act.sem, 1)

                act.wait_ge(b_gz.sem, b_gz.at(i, 2))
                for n, (o, w) in enumerate(((0, 32), (32, 64))):
                    act.activation(small[:, 128 + o:128 + o + w], small[:, 224 + o:224 + o + w], ACT.Tanh,
                                   scale=0.5).then_inc(b_th.sem, 1)
                for q in range(NQ):
                    src = take("k", q)
                    act.wait_ge(z_pe.sem, z_pe.before(i, 2 * NCH))
                    act.activation(xkT[:, q], src, ACT.Copy).then_inc(r_act.sem, 1)
                keys_by_token(0)
                for c in range(NCH):
                    for p in range(2):
                        act.wait_ge(z_pe.sem, z_pe.at(i, 2 * c + p + 1))
                        if c:
                            act.wait_ge(z_eg.sem, z_eg.at(i, 2 * c))
                        else:
                            act.wait_ge(r_act.sem, r_act.before(i, RA))
                        act.activation(sq[:, p * QD:(p + 1) * QD], bank(p), ACT.Square).then_inc(z_sq.sem, 1)
                    if c + 1 < NCH:
                        keys_by_token(c + 1)
                    gelus(2 * c)
                    gelus(2 * c + 1)
                    for s in range(2):
                        act.wait_ge(q_pe.sem, q_pe.at(i, 2 * c + s + 1))
                        act.activation(
                            xqT[:, 4 * s:4 * s + 4, c * P:(c + 1) * P],
                            bank(2 + s).rearrange("p (q t) -> p q t", q=4), ACT.Copy).then_inc(q_act.sem, 1)
                gelus(EXP)
                act.wait_ge(q_act.sem, q_act.at(i, 2 * NCH))
                def deviation(q):
                    src = take("v", q)
                    act.activation(xh[:, (q % 2) * NB:(q % 2) * NB + NB], src, ACT.Sqrt,
                                   bias=eps_ln[:, 1:2]).then_inc(r_act.sem, 1)

                for q in range(NQ):
                    if q >= 2:
                        act.wait_ge(r_pe.sem, r_pe.at(i, ring_no[("v", q - 2)] + 1))
                    else:
                        act.wait_ge(z_eg.sem, z_eg.at(i, 2 * NCH))
                    act.activation(sq[:, (q % 2) * NB:(q % 2) * NB + NB], xqT[:, q],
                                   ACT.Square).then_inc(t_sq.sem, 1)
                    if q:
                        if q >= 3:
                            act.wait_ge(t_rs.sem, t_rs.at(i, q - 2))
                        deviation(q - 1)
                act.wait_ge(t_rs.sem, t_rs.at(i, NQ - 2))
                deviation(NQ - 1)

        @block.vector
        def _(dve):
            tt, ts, stt = dve.tensor_tensor, dve.tensor_scalar, dve.scalar_tensor_tensor

            def layernorm(turn):
                base = turn * NBLK
                with dve.Fori(0, NBLK) as i:
                    dve.wait_ge(ln_sd, i + base + 1)
                    dve.wait_ge(ln_out.sem, ln_out.before(i + base, 1))
                    dve.reciprocal(res[:, :], lsq[:, NB:2 * NB]).then_inc(ln_rs, 1)
                    dve.wait_ge(ln_rs, i + base + 1)
                    o = by_chunk(xn[:, blk(i)]) if turn else xn[:, blk(i)]
                    centred = ps[:, bass.ds(i * 2 * NB, NB)]
                    tt(o, by_batch(centred) if turn else centred, by_batch(res) if turn else res, ALU.mult)\
                        .then_inc(ln_out.sem, 1)

            layernorm(0)
            dve.wait_ge(ln_out.sem, ln_out.at(NBLK - 1, 1))
            dve.wait_ge(ld_small, 16)
            dve.wait_ge(ld_x, 32)
            with dve.Fori(0, NBLK) as i:
                for m in range(KC):
                    dve.wait_ge(a_silu.sem, a_silu.at(i, m + 1))
                    stt(u0[:, m], bank((3 + 2 * m) % 8), col("w2_s", m), u0[:, m], ALU.mult,
                        ALU.mult).then_inc(a_u.sem, 1)
                for m in range(DC):
                    dve.wait_ge(a_pad.sem, a_pad.at(i, m + 1))
                    dve.wait_ge(a_hs.sem, a_hs.before(i, m + 1))
                    o = conv[:, m].rearrange("p (b s) -> p b s", b=BPB)
                    ts(o, hpad[:, m, :, 0:SEQ], col("conv_w", m * TAPS), None, ALU.mult).then_inc(a_step, 1)
                    for t in range(1, TAPS):
                        dve.wait_ge(a_step, i * (DC * (TAPS - 1)) + (m * (TAPS - 1) + t))
                        ins = stt(o, hpad[:, m, :, t:t + SEQ], col("conv_w", m * TAPS + t), o, ALU.mult, ALU.add)
                        ins.then_inc(a_conv.sem if t == TAPS - 1 else a_step, 1)
                dve.wait_ge(a_ex.sem, a_ex.at(i, 4))
                stt(ssm[0:NST, 3], ssm[0:NST, 3], 1.0, ssm[0:NST, 1], ALU.add, ALU.mult).then_inc(a_b.sem, 1)
                dve.wait_ge(a_b.sem, a_b.at(i, 1))
                stt(ssm[0:NST, 3], ssm[0:NST, 3], 0.5, ssm[0:NST, 2], ALU.mult, ALU.mult).then_inc(a_b.sem, 1)
                dve.wait_ge(a_b.sem, a_b.at(i, 2))
                dve.wait_ge(a_ex.sem, a_ex.at(i, 5))
                dve.wait_ge(a_o.sem, a_o.before(i, 1))
                for b in range(BPB):
                    s = slice(b * SEQ, (b + 1) * SEQ)
                    dve.tensor_tensor_scan(ssm[0:NST, 4, s], ssm[0:NST, 0, s], ssm[0:NST, 3, s], 0.0,
                                           ALU.mult, ALU.add).then_inc(a_y.sem, 1)
                dve.wait_ge(a_w3.sem, a_w3.at(i, 1))
                stt(res[:, :], bank(2), col("w3_s"), x_sb[:, blk(i)], ALU.mult, ALU.add).then_inc(a_res.sem, 1)
                dve.wait_ge(a_res.sem, a_res.at(i, 1))
                dve.wait_ge(a_o.sem, a_o.at(i, 1))
                stt(x_sb[:, blk(i)], bank(4), col("out_b"), res[:, :], ALU.add, ALU.add).then_inc(a_res.sem, 1)
            layernorm(1)

            done = [0]

            def step(ins):
                done[0] += 1
                ins.then_inc(p_dve, 1)
                dve.wait_ge(p_dve, done[0])

            dve.wait_ge(ld_c, 10 * 16)
            dve.wait_ge(ld_prep, 4 * 16)
            step(tt(wt[:, :], wk[:, :], wt[:, :], ALU.subtract))
            step(tt(wt[:, :], wt[:, :], gam, ALU.mult))
            step(tt(gg[:, :], gam, gam, ALU.mult))
            step(tt(gb[:, :], gam, bet, ALU.mult))
            step(dve.tensor_reduce(pstat[:, 0:NQ], qd(w_init[:, :]), AX_X, ALU.add))
            step(ts(pstat[:, 0:NQ], pstat[:, 0:NQ], 1.0 / HD, None, ALU.mult))
            step(tt(qd(w_init[:, :]), qd(w_init[:, :]), over_d(pstat[:, 0:NQ]), ALU.subtract))
            e3 = e_init[:, :].rearrange("p (h d) -> p h d", d=HD)
            step(dve.tensor_reduce(pstat[:, 0:NH], e3, AX_X, ALU.add))
            step(ts(pstat[:, 0:NH], pstat[:, 0:NH], 1.0 / HD, None, ALU.mult))
            step(tt(e3, pstat[:, 0:NH].unsqueeze(2).to_broadcast([P, NH, HD]), e3, ALU.subtract))
            dve.wait_ge(p_pe, 1)
            for q in range(NQ):
                ins = ts(wo[:, q], wo[:, q], col("gamma", q), None, ALU.mult)
            step(ins)
            step(dve.tensor_copy(wqo[:, :], ps[:, 0:P]))
            step(dve.tensor_copy(be_wo[:, :], ps[:, NB:NB + 1]))
            step(dve.tensor_copy(w_th[:, :], ps[:, 2 * NB:2 * NB + NH]))
            assert done[0] == 14
            te = small[:, 383:384]
            t1 = small[:, 382:383]
            tt(t1, col("alpha"), col("inv_index"), ALU.add).then_inc(p_dve, 1)
            dve.wait_ge(p_dve, 15)
            ts(te, t1, 0.0, 0.5 / HD, ALU.max, ALU.mult).then_inc(p_dve, 1)
            dve.wait_ge(p_dve, 16)

            with dve.Fori(0, NBLK) as i:
                n_steps = [0]

                def link(ins):
                    n_steps[0] += 1
                    ins.then_inc(b_step, 1)
                    dve.wait_ge(b_step, i * BSTEPS + n_steps[0])

                def take(kind, which):
                    dve.wait_ge(r_pe.sem, r_pe.at(i, ring_no[(kind, which)] + 1))
                    return bank(ring_bank(kind, which))

                def targets(c):
                    for p in range(2):
                        src = take("t", (c, p))
                        tt(qd(ttok[:, c % 2, p * QD:(p + 1) * QD]), qd(src), by_parity(gb, p),
                           ALU.add).then_inc(r_dve.sem, 1)

                def mix(e):
                    dve.wait_ge(m_pe.sem, m_pe.at(i, e + 1))
                    if e == 0:
                        dve.wait_ge(b_cbc.sem, b_cbc.at(i, 16))
                        dve.wait_ge(t_res.sem, t_res.before(i, 2))
                        tt(macc[:, :], bank(7), comb_bc[:, 0], ALU.mult).then_inc(m_mul.sem, 1)
                        return
                    if e >= 2:
                        dve.wait_ge(m_add.sem, m_add.at(i, e - 1))
                    if e < EXP:
                        tt(mtmp[:, :], bank(7), comb_bc[:, e], ALU.mult).then_inc(m_mul.sem, 1)
                    else:
                        ts(mtmp[:, :], bank(7), col("sb2"), 0.1, ALU.add, ALU.mult).then_inc(m_mul.sem, 1)
                    dve.wait_ge(m_mul.sem, m_mul.at(i, e + 1))
                    tt(macc[:, :], macc[:, :], mtmp[:, :], ALU.add).then_inc(m_add.sem, 1)

                dve.tensor_copy(xb[:, :], xn[:, blk(i)]).then_inc(b_xb.sem, 1)
                dve.wait_ge(b_gate.sem, b_gate.at(i, 1))
                tt(small[:, 224:256].rearrange("p (j e) -> p j e", e=EXP),
                   ps[:, 0:32].rearrange("p (j e) -> p j e", e=EXP),
                   col("gate_b", 0, EXP).unsqueeze(1).to_broadcast([P, 4, EXP]), ALU.add).then_inc(b_gz.sem, 1)
                tt(small[:, 256:320].rearrange("p (c h) -> p c h", h=NH),
                   ps[:, 64:128].rearrange("p (c h) -> p c h", h=NH),
                   col("theta_bias", 0, NH).unsqueeze(1).to_broadcast([P, NCH, NH]), ALU.add).then_inc(b_gz.sem, 1)
                dve.wait_ge(b_th.sem, b_th.at(i, 2))
                score = small[:, 320:352]
                link(ts(score, small[:, 128:160], 1.0, 0.5, ALU.add, ALU.mult))
                top = small[:, 64:96]
                dve.sem_inc(stand_dve, 1)
                for j in range(4):
                    ins = dve.max(top[:, 8 * j:8 * j + 8], score[:, 8 * j:8 * j + 8])
                link(ins)
                dve.sem_inc(stand_dve, 1)
                for j in range(4):
                    ins = dve.max_index(idx[:, j], top[:, 8 * j:8 * j + 8], score[:, 8 * j:8 * j + 8])
                link(ins)
                t3 = top.rearrange("p (j e) -> p j e", e=8)
                idf = small[:, 352:360].rearrange("p (j e) -> p j e", e=2)
                tsum = small[:, 360:364].rearrange("p (j e) -> p j e", e=1)
                link(dve.tensor_copy(idf, idx[:, :, 0:2]))
                link(tt(tsum, t3[:, :, 0:1], t3[:, :, 1:2], ALU.add))
                link(ts(tsum, tsum, TOPK_EPS, None, ALU.add))
                link(dve.reciprocal(tsum, tsum))
                link(tt(t3[:, :, 0:2], t3[:, :, 0:2], tsum.to_broadcast([P, 4, 2]), ALU.mult))
                comb = small[:, 96:128].rearrange("p (j e) -> p j e", e=EXP)
                c1 = small[:, 32:64].rearrange("p (j e) -> p j e", e=EXP)
                nos = col("expert_no", 0, EXP).unsqueeze(1).to_broadcast([P, 4, EXP])
                link(tt(comb, nos, idf[:, :, 0:1].to_broadcast([P, 4, EXP]), ALU.is_equal))
                link(tt(comb, comb, t3[:, :, 0:1].to_broadcast([P, 4, EXP]), ALU.mult))
                link(tt(c1, nos, idf[:, :, 1:2].to_broadcast([P, 4, EXP]), ALU.is_equal))
                link(tt(c1, c1, t3[:, :, 1:2].to_broadcast([P, 4, EXP]), ALU.mult))
                tt(comb, comb, c1, ALU.add).then_inc(b_comb.sem, 1)
                eta = small[:, 160:224]
                ts(eta, eta, 1.0, te, ALU.add, ALU.mult).then_inc(b_eta.sem, 1)
                dve.wait_ge(b_ct.sem, b_ct.at(i, 1))
                dve.wait_ge(b_cst.sem, b_cst.before(i, 16))
                dve.wait_ge(t_out.sem, t_out.before(i, 1))
                dve.tensor_copy(combT[:, :], bank(1, EXP)).then_inc(b_ctc.sem, 1)
                for q in range(NQ):
                    src = take("q", q)
                    dve.tensor_copy(xqT[:, q], src).then_inc(r_dve.sem, 1)
                targets(0)
                for c in range(NCH):
                    ve = small[:, 0:16]
                    rr = small[:, 16:32]
                    s1, s2, ce = small[:, 32:48], small[:, 48:64], small[:, 64:80]
                    for p in range(2):
                        dve.wait_ge(z_sq.sem, z_sq.at(i, 2 * c + p + 1))
                        ins = dve.tensor_reduce(ve[:, 8 * p:8 * p + 8], qd(sq[:, p * QD:(p + 1) * QD]), AX_X, ALU.add)
                    link(ins)
                    ts(ve, ve, 1.0 / HD, TTT_EPS, ALU.mult, ALU.add).then_inc(z_ve.sem, 1)
                    if c + 1 < NCH:
                        targets(c + 1)
                    dve.wait_ge(z_r.sem, z_r.at(i, c + 1))
                    for p in range(2):
                        h = slice(p * QD, (p + 1) * QD)
                        tt(qd(xh[:, h]), qd(bank(p)), over_d(rr[:, 8 * p:8 * p + 8]), ALU.mult).then_inc(z_xh.sem, 1)
                    link(tt(ce, rr, eta[:, c * NH:(c + 1) * NH], ALU.mult))
                    for p in range(2):
                        h = slice(p * QD, (p + 1) * QD)
                        e8 = slice(8 * p, 8 * p + 8)
                        dve.wait_ge(z_gx.sem, z_gx.at(i, 2 * c + p + 1))
                        link(tt(sq[:, h], gx[:, h], xh[:, h], ALU.mult))
                        link(dve.tensor_reduce(s2[:, e8], qd(sq[:, h]), AX_X, ALU.add))
                        ts(s2[:, e8], s2[:, e8], 1.0 / HD, None, ALU.mult).then_inc(z_s2.sem, 1)
                    for p in range(2):
                        h = slice(p * QD, (p + 1) * QD)
                        e8 = slice(8 * p, 8 * p + 8)
                        link(dve.tensor_reduce(s1[:, e8], qd(gx[:, h]), AX_X, ALU.add))
                        link(ts(s1[:, e8], s1[:, e8], 1.0 / HD, None, ALU.mult))
                        tt(by_parity(eg, p), qd(gx[:, h]), over_d(s1[:, e8]), ALU.subtract).then_inc(b_step, 1)
                        n_steps[0] += 1
                        dve.wait_ge(b_step, i * BSTEPS + n_steps[0])
                    for p in range(2):
                        h = slice(p * QD, (p + 1) * QD)
                        e8 = slice(8 * p, 8 * p + 8)
                        dve.wait_ge(z_u.sem, z_u.at(i, 2 * c + p + 1))
                        link(tt(by_parity(eg, p), by_parity(eg, p), qd(sq[:, h]), ALU.subtract))
                        tt(by_parity(eg, p), by_parity(eg, p), over_d(ce[:, e8]), ALU.mult).then_inc(z_eg.sem, 1)
                    mix(2 * c)
                    for b in range(BPB):
                        dve.wait_ge(w_pe.sem, w_pe.at(i, 2 * c + b + 1))
                        tt(wst[:, b], (w_init[:, :] if c == 0 else wst[:, b]), bank(2 + b),
                           ALU.subtract).then_inc(w_dve.sem, 1)
                    mix(2 * c + 1)
                mix(EXP)
                for q in range(NQ):
                    dve.wait_ge(r_act.sem, r_act.at(i, taken_no[("v", q)]))
                    half = slice((q % 2) * NB, (q % 2) * NB + NB)
                    dve.reciprocal(gx[:, half], xh[:, half]).then_inc(t_rs.sem, 1)
                    dve.wait_ge(t_rs.sem, t_rs.at(i, q + 1))
                    tt(xqT[:, q], xqT[:, q], gx[:, half], ALU.mult).then_inc(t_xh.sem, 1)
                dve.wait_ge(t_out.sem, t_out.at(i, 1))
                dve.wait_ge(t_dma.sem, t_dma.before(i, 16))
                dve.wait_ge(m_add.sem, m_add.at(i, NE - 1))
                stt(mtmp[:, :], bank(2), be_wo[:, 0:1], macc[:, :], ALU.add, ALU.add).then_inc(t_res.sem, 1)
                dve.wait_ge(t_res.sem, t_res.at(i, 1))
                tt(by_batch(osb), by_chunk(mtmp[:, :]), by_batch(x_sb[:, blk(i)]), ALU.add).then_inc(t_res.sem, 1)
                assert n_steps[0] == BSTEPS, n_steps[0]


def kernel(**v):
    import numpy as np
    import concourse.bacc as bacc
    from concourse.bass_utils import run_bass_kernel_spmd as run

    v = {k: np.ascontiguousarray(x) for k, x in v.items()}

    def A(n):
        return v["L0_attn_" + n]

    def M(n):
        return v["L0_ffn_" + n]

    def T(n):
        return v["L1_attn_" + n]

    def E(n):
        return v["L1_ffn_" + n]

    f = np.float32

    def chunks(w, n):
        return w.reshape(n, P, -1).transpose(1, 0, 2)

    half = np.arange(P) // 64
    same = half[:, None] == half[None, :]
    eye = np.eye(P, dtype=f)
    mats = np.concatenate([eye - f(1 / P), np.full((P, P), 1 / P, f), -same.astype(f),
                           same.astype(f) / f(HD), eye], axis=1)
    packed = {
        "in_b": A("in_b").reshape(DC, P).T, "conv_w": A("conv_w").reshape(DC, P, TAPS).transpose(1, 0, 2).reshape(P, -1),
        "conv_b": A("conv_b").reshape(DC, P).T,
        "w1_s": M("w1_s").reshape(KC, P).T, "w2_s": M("w2_s").reshape(KC, P).T,
        "h1_s": M("h1_s").reshape(KC, P).T, "h2_s": M("h2_s").reshape(KC, P).T,
        "w3_s": M("w3_s").reshape(1, P).T, "out_b": A("out_b").reshape(1, P).T,
        "gamma": T("gamma").reshape(NQ, P).T, "beta": T("beta").reshape(NQ, P).T,
        "b1": np.concatenate([E("b1").reshape(EXP * KC, P), E("sb1").reshape(KC, P)]).T,
        "sb2": E("sb2").reshape(1, P).T,
        "alpha": np.tile(T("alpha"), 2).reshape(P, 1),
        "inv_index": np.tile(f(1) / np.arange(1, CH + 1, dtype=f), 2).reshape(P, 1),
        "theta_bias": np.broadcast_to(T("theta_bias").reshape(NQ, 2).T.reshape(1, NH), (P, NH)),
        "gate_b": np.broadcast_to(E("gate_b").reshape(1, EXP), (P, EXP)),
        "expert_no": np.broadcast_to(np.arange(EXP, dtype=f).reshape(1, EXP), (P, EXP)),
    }
    cols = np.zeros((P, NCOLS), f)
    for name, x in packed.items():
        at, n = COLS[name]
        cols[:, at:at + n] = x
    th = T("theta").reshape(NQ, 2, HD)
    for q in range(NQ):
        for p in range(2):
            cols[64 * p:64 * p + 64, COLS["theta"][0] + 2 * q + p] = th[q, p]
    xp_w = np.zeros((P, DC, 96), f)
    xw = A("xp_w").T.reshape(DC, P, 2 * NST).transpose(1, 0, 2)
    xp_w[:, :, 0:16], xp_w[:, :, 32:48], xp_w[:, :, 64:80] = xw[:, :, 0:16], xw[:, :, 16:32], 1
    xp_row = np.zeros((1, 96 + NB), f)
    xp_row[0, 0:16], xp_row[0, 32:48], xp_row[0, 96:] = A("xp_b")[0:16], A("xp_b")[16:32], 1
    e_init = np.zeros((P, NH * HD), f)
    e_init[0] = e_init[64] = T("b1").reshape(NH * HD)
    arrays = {
        "xT": A("x").reshape(TOK, D).T, "mats": mats, "cols": cols,
        "in_w": A("in_w").T, "w1": M("w1_w").T, "w2": M("w2_w").T,
        "h1": chunks(M("h1_w").T, KC), "h2": chunks(M("h2_w").T, KC), "w3": chunks(M("w3_w").T, KC),
        "xp_w": xp_w, "xp_row": xp_row, "out_w": A("out_w").T,
        "wq": T("wq"), "wk": T("wk"), "wv": T("wv"), "wo": chunks(T("wo"), NQ),
        "wqT": chunks(T("wq").T, NQ), "wkT": chunks(T("wk").T, NQ),
        "gamma_row": T("gamma").reshape(NH * HD), "beta_row": T("beta").reshape(NH * HD),
        "w_init": T("W1").reshape(NQ, P, HD).transpose(1, 0, 2).reshape(P, QD),
        "e_init": e_init,
        "mw1": np.concatenate([E("w1"), E("sw1")[None]]).transpose(1, 0, 2),
        "mw2": np.concatenate([E("w2").reshape(EXP * KC, P, D), E("sw2").reshape(KC, P, D)]).transpose(1, 0, 2),
        "mb2": E("b2"), "gate_w": E("gate_w").T,
    }
    nc = bacc.Bacc("TRN2", target_bir_lowering=False, num_devices=1)
    fed, aps = {}, {}
    for name, x in arrays.items():
        x = np.ascontiguousarray(x)
        fed["in_" + name] = x
        aps[name] = nc.dram_tensor("in_" + name, x.shape, mybir.dt.from_np(x.dtype), kind="ExternalInput").ap()
    out = nc.dram_tensor("out", (D, TOK), F32, kind="ExternalOutput").ap()
    build(nc, aps, out)
    r = run(nc, [fed], core_ids=[0])
    return np.ascontiguousarray(np.asarray(r.results[0]["out"]).T).reshape(BATCH, SEQ, D)
```

```python
from contextlib import ExitStack

import concourse.bass as bass
from concourse import mybir

F32 = mybir.dt.float32
I32 = mybir.dt.int32
U32 = mybir.dt.uint32
ALU = mybir.AluOpType
ACT = mybir.ActivationFunctionType
AX_X = mybir.AxisListType.X

P = 128
BATCH, SEQ, D = 8, 256, 128
TOK = BATCH * SEQ
NB = 512
NBLK = TOK // NB
BPB = NB // SEQ
HID = 512
KC = HID // P
DI, NST, TAPS = 256, 16, 4
DC = DI // P
PAD = TAPS - 1
NH, HD, CH = 16, 64, 64
NCH = SEQ // CH
NQ = NH // 2
QD = NQ * HD
EXP = 8
NE = EXP + 1
LN_EPS, TTT_EPS, TOPK_EPS = 1e-5, 1e-6, 1e-6

COLS = {}
_at = 0
for _name, _n in (("in_b", DC), ("conv_w", DC * TAPS), ("conv_b", DC), ("w1_s", KC), ("w2_s", KC),
                  ("h1_s", KC), ("h2_s", KC), ("w3_s", 1), ("out_b", 1), ("gamma", NQ), ("beta", NQ),
                  ("b1", NE * KC), ("sb2", 1), ("theta", 2 * NQ), ("alpha", 1), ("inv_index", 1),
                  ("theta_bias", NH), ("gate_b", EXP), ("expert_no", EXP)):
    COLS[_name] = (_at, _n)
    _at += _n
NCOLS = _at
M_CENTER, M_MEAN, M_NEG, M_VAR, M_IDENT = range(5)


class Signal:

    def __init__(self, sem, per):
        self.sem, self.per = sem, per

    def at(self, i, k):
        return i * self.per + (k + self.per)

    def before(self, i, k):
        return i * self.per + k


def build(nc, a, out):
    with ExitStack() as ctx:
        def sb(name, shape, dt=F32):
            return ctx.enter_context(nc.sbuf_tensor(name, shape, dt))

        def sem(name):
            return ctx.enter_context(nc.semaphore(name))

        credited = []

        def signal(name, per):
            s = Signal(sem(name), per)
            credited.append(s)
            return s

        x_sb = sb("x_sb", [P, TOK])
        xn = sb("xn", [P, TOK])
        mats = sb("mats", [P, 5 * P])
        cols = sb("cols", [P, NCOLS])
        eps_ln = sb("eps_ln", [P, 2])

        def mat(n):
            return mats[:, n * P:(n + 1) * P]

        def col(name, k=0, n=1, rows=P):
            return cols[0:rows, COLS[name][0] + k:COLS[name][0] + k + n]

        in_w = sb("in_w", [P, DI])
        l0 = sb("l0", [P, 2 * KC * HID + 2 * HID + KC * D])
        h1 = l0[:, 0:KC * HID].rearrange("p (k n) -> p k n", k=KC)
        h2 = l0[:, KC * HID:2 * KC * HID].rearrange("p (k n) -> p k n", k=KC)
        w1, w2 = (l0[:, 2 * KC * HID + n * HID:2 * KC * HID + (n + 1) * HID] for n in range(2))
        w3 = l0[:, 2 * KC * HID + 2 * HID:].rearrange("p (k n) -> p k n", k=KC)
        xp_w = sb("xp_w", [P, DC, 96])
        xp_row = sb("xp_row", [1, 96 + NB])
        out_w = sb("out_w", [NST, D])

        wq = sb("wq", [P, NH * HD])
        wk = sb("wk", [P, NH * HD])
        wt = sb("wt", [P, NH * HD])
        wo = sb("wo", [P, NQ, D])
        mw1 = sb("mw1", [P, NE, HID])
        mw2 = sb("mw2", [P, NE * KC, D])
        mb2 = sb("mb2", [EXP, D])
        gate_w = sb("gate_w", [P, EXP])
        wqo = sb("wqo", [P, D])
        w_th = sb("w_th", [P, NH])
        be_wo = sb("be_wo", [P, 1])
        w_init = sb("w_init", [P, QD])
        e_init = sb("e_init", [P, NH * HD])
        gg = sb("gg", [P, NH * HD])
        gb = sb("gb", [P, NH * HD])

        work = sb("work", [P, 12288])
        used = [0]

        def cut(n):
            used[0] += n
            assert used[0] <= 12288
            return work[:, used[0] - n:used[0]]

        hpad = cut(DC * BPB * (PAD + SEQ)).rearrange("p (c b s) -> p c b s", c=DC, b=BPB)
        conv = cut(DC * NB).rearrange("p (c n) -> p c n", c=DC)
        hs = cut(DC * NB).rearrange("p (c n) -> p c n", c=DC)
        u0 = cut(KC * NB).rearrange("p (c n) -> p c n", c=KC)
        g1 = cut(KC * NB).rearrange("p (c n) -> p c n", c=KC)
        g2 = u0
        ssm = cut(5 * NB).rearrange("p (c n) -> p c n", c=5)
        res = cut(NB)
        used[0] = DC * BPB * (PAD + SEQ)
        lsq = cut(2 * TOK)
        used[0] = 0
        xkT = cut(NQ * NB).rearrange("p (q n) -> p q n", q=NQ)
        xqT = cut(NQ * NB).rearrange("p (q n) -> p q n", q=NQ)
        hid = cut(2 * KC * NB).rearrange("p (e f n) -> p e f n", e=2, f=KC)
        xb = sb("xb", [P, NB])
        combT = sb("combT", [EXP, NB])
        comb_bc = sb("comb_bc", [P, EXP, NB])
        xh, gx, eg, esum, ktok = (l0[:, n * NH * HD:(n + 1) * NH * HD] for n in range(5))
        wqT, wkT = comb_bc[:, 0:2], comb_bc[:, 2:4]
        sq2 = sb("sq2", [P, NH * HD])
        ttok = sb("ttok", [P, 2, NH * HD])
        sq = sb("sq", [P, NH * HD])
        wst = sb("wst", [P, BPB, QD])
        macc = sb("macc", [P, NB])
        mtmp = sb("mtmp", [P, NB])
        osb = l0[:, 5 * NH * HD:5 * NH * HD + NB]
        small = sb("small", [P, 400])
        pstat = small[:, 0:16]
        idx = sb("idx", [P, 4, 8], U32)

        ps = ctx.enter_context(nc.psum_tensor("ps", [P, 8 * NB], F32))

        def bank(n, rows=P, a0=0):
            return ps[a0:a0 + rows, n * NB:(n + 1) * NB]

        comb_dram = nc.dram_tensor("comb_dram", (EXP, NB), F32, kind="Internal").ap()

        ld_x, ld_small, ld_a, ld_b, ld_c = (sem(n) for n in ("ld_x", "ld_small", "ld_a", "ld_b", "ld_c"))
        ld_m = sem("ld_m")
        PREP = 12
        CLOADS = 12 * 16
        eps_set, pads_set = sem("eps_set"), sem("pads_set")
        stand, stand_dve = sem("stand"), sem("stand_dve")
        ln_centred, ln_sq, ln_var, ln_sd, ln_rs = (
            sem(n) for n in ("ln_centred", "ln_sq", "ln_var", "ln_sd", "ln_rs"))
        ln_out = signal("ln_out", 1)
        a_in = signal("a_in", DC)
        a_pad = signal("a_pad", DC)
        a_conv = signal("a_conv", DC)
        a_hs = signal("a_hs", DC)
        a_w12 = signal("a_w12", KC)
        a_silu = signal("a_silu", KC)
        a_u = signal("a_u", KC)
        a_h1 = signal("a_h1", KC)
        a_g1 = signal("a_g1", KC)
        a_h2 = signal("a_h2", KC)
        a_g2 = signal("a_g2", KC)
        a_xp = signal("a_xp", 1)
        a_ex = signal("a_ex", 5)
        a_b = signal("a_b", 2)
        a_y = signal("a_y", BPB)
        a_o = signal("a_o", 1)
        a_w3 = signal("a_w3", 1)
        a_res = signal("a_res", 2)
        a_step = sem("a_step")
        p_dve, p_pe, p_pool = sem("p_dve"), sem("p_pe"), sem("p_pool")
        b_xb = signal("b_xb", 1)
        b_gate = signal("b_gate", 1)
        b_gz = signal("b_gz", 2)
        b_th = signal("b_th", 2)
        b_comb = signal("b_comb", 1)
        b_ct = signal("b_ct", 1)
        b_ctc = signal("b_ctc", 1)
        b_cst = signal("b_cst", 16)
        b_cbc = signal("b_cbc", 16)
        NRING = 2 * NQ + 6 * NCH + NE * KC
        r_pe = signal("r_pe", NRING)
        RA = 2 * NQ + 4 * NCH + NE * KC
        r_act = signal("r_act", RA)
        r_dve = signal("r_dve", 2 * NCH)
        b_eta = signal("b_eta", 1)
        z_pe = signal("z_pe", 2 * NCH)
        z_sq = signal("z_sq", 2 * NCH)
        z_ve = signal("z_ve", NCH)
        z_r = signal("z_r", NCH)
        z_xh = signal("z_xh", 2 * NCH)
        z_gm = signal("z_gm", NCH)
        z_gx = signal("z_gx", NCH)
        z_s2 = signal("z_s2", NCH)
        z_u = signal("z_u", NCH)
        z_eg = signal("z_eg", 2 * NCH)
        z_es = signal("z_es", 2 * NCH)
        w_pe = signal("w_pe", 2 * NCH)
        w_dve = signal("w_dve", 2 * NCH)
        q_pe = signal("q_pe", 2 * NCH)
        q_sq = signal("q_sq", 2 * NCH)
        q_ve = signal("q_ve", NCH)
        q_r = signal("q_r", NCH)
        q_n = signal("q_n", 2 * NCH)
        m_pe = signal("m_pe", NE)
        m_mul = signal("m_mul", NE)
        m_add = signal("m_add", NE - 1)
        t_out = signal("t_out", 1)
        t_res = signal("t_res", 2)
        t_dma = signal("t_dma", 16)
        b_step = sem("b_step")
        BSTEPS = 12 + 17 * NCH

        RING0 = 4
        ring = [("k", q, r_act) for q in range(NQ)]

        def ring_pair(kind, c, who):
            return [(kind, (c, p), who) for p in range(2)]

        def ring_up(e):
            return [("up", (e, f), r_act) for f in range(KC)]

        ring += ring_pair("t", 0, r_dve)
        ring += [("q", q, r_act) for q in range(NQ)]
        for c in range(NCH):
            ring += ring_pair("kt", c, r_act)
            if c + 1 < NCH:
                ring += ring_pair("t", c + 1, r_dve)
            ring += ring_up(2 * c) + ring_up(2 * c + 1)
            if c:
                ring += ring_pair("v", c - 1, r_act)
        ring += ring_up(EXP)
        ring += ring_pair("v", NCH - 1, r_act)
        assert len(ring) == NRING
        ring_no = {(k, w): n for n, (k, w, _) in enumerate(ring)}
        taken_no = {}
        for s in (r_act, r_dve):
            for n, (k, w, _) in enumerate([r for r in ring if r[2] is s]):
                taken_no[(k, w)] = n + 1
        assert sum(r[2] is r_act for r in ring) == RA

        def ring_bank(kind, which):
            return RING0 + ring_no[(kind, which)] % 3

        def by_parity(t, p):
            return t[:, :].rearrange("p (q h d) -> p h q d", h=2, d=HD)[:, p]

        def by_batch(t):
            return t.rearrange("p (b c k) -> p b c k", b=BPB, c=NCH)

        def by_chunk(t):
            return t.rearrange("p (c b k) -> p b c k", b=BPB, c=NCH)

        def over_d(t):
            return t.unsqueeze(2).to_broadcast([P, NQ, HD])

        def qd(t):
            return t.rearrange("p (q d) -> p q d", q=NQ)

        def blk(i):
            return bass.ds(i * NB, NB)

        block = ctx.enter_context(nc.Block())

        @block.sync
        def _(sp):
            for s in credited:
                sp.sem_inc(s.sem, s.per)
            sp.dma_start(mats[:, :], a["mats"]).then_inc(ld_x, 16)
            sp.dma_start(x_sb[:, :], a["xT"]).then_inc(ld_x, 16)
            sp.dma_start(cols[:, :], a["cols"]).then_inc(ld_small, 16)
            sp.dma_start(in_w[:, :], a["in_w"]).then_inc(ld_a, 16)
            sp.dma_start(w1[:, :], a["w1"]).then_inc(ld_a, 16)
            sp.dma_start(w2[:, :], a["w2"]).then_inc(ld_a, 16)
            sp.dma_start(xp_w[:, :, :], a["xp_w"]).then_inc(ld_a, 16)
            sp.dma_start(xp_row[:, :], a["xp_row"]).then_inc(ld_a, 16)
            sp.dma_start(out_w[:, :], a["out_w"]).then_inc(ld_a, 16)
            sp.dma_start(h1[:, :, :], a["h1"]).then_inc(ld_b, 16)
            sp.dma_start(h2[:, :, :], a["h2"]).then_inc(ld_b, 16)
            sp.dma_start(w3[:, :, :], a["w3"]).then_inc(ld_b, 16)
            for dst, name in ((wq, "wq"), (wk, "wk"), (wt, "wv"), (mb2, "mb2"), (gate_w, "gate_w"),
                              (w_init, "w_init")):
                sp.dma_start(dst[:, :], a[name]).then_inc(ld_c, 16)
            sp.dma_start(e_init[:, :], a["e_init"]).then_inc(ld_c, 16)
            sp.dma_start(wo[:, :, :], a["wo"]).then_inc(ld_c, 16)
            sp.dma_start(gg[:, :], a["gamma_row"].partition_broadcast(P)).then_inc(ld_c, 16)
            sp.dma_start(gb[:, :], a["beta_row"].partition_broadcast(P)).then_inc(ld_c, 16)
            sp.dma_start(comb_bc[:, 0:2, :], a["wqT"]).then_inc(ld_c, 16)
            sp.dma_start(comb_bc[:, 2:4, :], a["wkT"]).then_inc(ld_c, 16)
            sp.dma_start(mw1[:, :, :], a["mw1"]).then_inc(ld_m, 16)
            sp.dma_start(mw2[:, :, :], a["mw2"]).then_inc(ld_m, 16)
            with sp.Fori(0, NBLK) as i:
                sp.wait_ge(b_ctc.sem, b_ctc.at(i, 1))
                sp.wait_ge(b_cbc.sem, b_cbc.before(i, 16))
                sp.dma_start(comb_dram, combT[:, :]).then_inc(b_cst.sem, 16)
                sp.wait_ge(b_cst.sem, b_cst.at(i, 16))
                sp.wait_ge(m_mul.sem, m_mul.before(i, NE))
                sp.dma_start(comb_bc[:, :, :], comb_dram.partition_broadcast(P)).then_inc(b_cbc.sem, 16)
                sp.wait_ge(t_res.sem, t_res.at(i, 2))
                sp.dma_start(out[:, bass.ds(i * NB, NB)], osb[:, :]).then_inc(t_dma.sem, 16)
            sp.wait_ge(t_dma.sem, t_dma.at(NBLK - 1, 16))

        @block.gpsimd
        def _(pool):
            pool.memset(eps_ln[:, 0:1], LN_EPS).then_inc(eps_set, 1)
            pool.memset(eps_ln[:, 1:2], TTT_EPS).then_inc(eps_set, 1)
            pool.memset(hpad[:, :, :, 0:PAD], 0.0).then_inc(pads_set, 1)
            pool.memset(small[:, 384:400], -0.5).then_inc(eps_set, 1)
            pool.wait_ge(eps_set, 3)
            pool.wait_ge(ld_c, CLOADS)
            pool.tensor_tensor(wt[:, :], wk[:, :], wt[:, :], ALU.subtract).then_inc(p_pool, 1)
            pool.tensor_tensor(gb[:, :], gg[:, :], gb[:, :], ALU.mult).then_inc(p_pool, 1)
            pool.wait_ge(p_pool, 2)
            pool.tensor_tensor(wt[:, :], wt[:, :], gg[:, :], ALU.mult).then_inc(p_pool, 1)
            pool.wait_ge(p_pool, 3)
            pool.tensor_tensor(gg[:, :], gg[:, :], gg[:, :], ALU.mult).then_inc(p_pool, 1)
            pool.wait_ge(p_pool, 4)
            with pool.Fori(0, NBLK) as i:
                def query_deviations(c):
                    pool.wait_ge(q_ve.sem, q_ve.at(i, c + 1))
                    pool.tensor_tensor(small[:, 240:256], small[:, 224:240], small[:, 384:400],
                                       ALU.pow).then_inc(q_r.sem, 1)

                for c in range(NCH):
                    pool.wait_ge(z_ve.sem, z_ve.at(i, c + 1))
                    pool.wait_ge(w_dve.sem, w_dve.before(i, 2 * c + 2) if c == 0 else w_dve.at(i, 2 * c))
                    pool.tensor_tensor(small[:, 16:32], small[:, 0:16], small[:, 384:400],
                                       ALU.pow).then_inc(z_r.sem, 1)
                    h = slice(0, QD)
                    pool.wait_ge(z_xh.sem, z_xh.at(i, 2 * c + 1))
                    pool.tensor_tensor(qd(gx[:, h]), qd(xh[:, h]), by_parity(gg, 0),
                                       ALU.mult).then_inc(z_gm.sem, 1)
                    pool.wait_ge(z_gm.sem, z_gm.at(i, c + 1))
                    pool.wait_ge(r_dve.sem, r_dve.at(i, taken_no[("t", (c, 0))]))
                    pool.tensor_tensor(gx[:, h], gx[:, h], ttok[:, c % 2, h], ALU.add).then_inc(z_gx.sem, 1)
                    if c:
                        query_deviations(c - 1)
                    pool.wait_ge(z_s2.sem, z_s2.at(i, c + 1))
                    pool.tensor_tensor(qd(sq[:, h]), qd(xh[:, h]), over_d(small[:, 48:56]),
                                       ALU.mult).then_inc(z_u.sem, 1)
                    if c:
                        pool.wait_ge(q_pe.sem, q_pe.at(i, 2 * c))
                    for p in range(2):
                        pool.wait_ge(z_eg.sem, z_eg.at(i, 2 * c + 1 + p))
                        pool.tensor_tensor(by_parity(esum, 1 - p), by_parity(e_init if c == 0 else esum, 1 - p),
                                           by_parity(eg, 1 - p), ALU.add).then_inc(z_es.sem, 1)
                query_deviations(NCH - 1)

        @block.tensor
        def _(pe):
            def layernorm(turn):
                base = turn * NBLK
                with pe.Fori(0, NBLK) as i:
                    pe.matmul(ps[:, bass.ds(i * 2 * NB, NB)], mat(M_CENTER), x_sb[:, blk(i)],
                              start=True, stop=True).then_inc(ln_centred, 1)
                with pe.Fori(0, NBLK) as i:
                    pe.wait_ge(ln_sq, i + base + 1)
                    pe.matmul(ps[:, bass.ds(i * 2 * NB + NB, NB)], mat(M_MEAN), lsq[:, bass.ds(i * 2 * NB, NB)],
                              start=True, stop=True).then_inc(ln_var, 1)

            pe.wait_ge(ld_x, 32)
            layernorm(0)
            pe.wait_ge(ln_out.sem, ln_out.at(NBLK - 1, 1))
            pe.wait_ge(ld_a, 6 * 16)
            with pe.Fori(0, NBLK) as i:
                for m in range(DC):
                    pe.wait_ge(a_g2.sem, a_g2.before(i, 2 + m + 1))
                    pe.matmul(bank(m), in_w[:, m * P:(m + 1) * P], xn[:, blk(i)],
                              start=True, stop=True).then_inc(a_in.sem, 1)
                for m in range(KC):
                    b = (2 + 2 * m) % 8
                    if m == 0:
                        pe.wait_ge(a_res.sem, a_res.before(i, 2))
                    if m == 1:
                        pe.wait_ge(a_g2.sem, a_g2.before(i, 2))
                    if m == 3:
                        pe.wait_ge(a_pad.sem, a_pad.at(i, DC))
                    pe.matmul(bank(b), w1[:, m * P:(m + 1) * P], xn[:, blk(i)], start=True, stop=True)
                    pe.matmul(bank(b + 1), w2[:, m * P:(m + 1) * P], xn[:, blk(i)],
                              start=True, stop=True).then_inc(a_w12.sem, 1)
                pe.wait_ge(ld_b, 3 * 16)
                pe.wait_ge(a_u.sem, a_u.at(i, 2))
                for k in range(KC):
                    pe.wait_ge(a_u.sem, a_u.at(i, k + 1))
                    for m in range(KC):
                        mm = pe.matmul(bank(2 + m), h1[:, k, m * P:(m + 1) * P], u0[:, k],
                                       start=(k == 0), stop=(k == KC - 1), skip_group_check=True)
                        if k == KC - 1:
                            mm.then_inc(a_h1.sem, 1)
                for k in range(KC):
                    pe.wait_ge(a_g1.sem, a_g1.at(i, k + 1))
                    for m in range(KC):
                        mm = pe.matmul(bank((6 + m) % 8), h2[:, k, m * P:(m + 1) * P], g1[:, k],
                                       start=(k == 0), stop=(k == KC - 1), skip_group_check=True)
                        if k == KC - 1:
                            mm.then_inc(a_h2.sem, 1)
                pe.wait_ge(a_hs.sem, a_hs.at(i, DC))
                for k in range(DC):
                    pe.matmul(bank(3, 96), xp_w[:, k], hs[:, k], start=(k == 0), stop=False)
                pe.matmul(bank(3, 96), xp_row[:, 0:96], xp_row[:, 96:96 + NB], start=False,
                          stop=True).then_inc(a_xp.sem, 1)
                for k in range(KC):
                    pe.wait_ge(a_g2.sem, a_g2.at(i, k + 1))
                    mm = pe.matmul(bank(2), w3[:, k], g2[:, k], start=(k == 0), stop=(k == KC - 1))
                mm.then_inc(a_w3.sem, 1)
                pe.wait_ge(a_y.sem, a_y.at(i, BPB))
                pe.matmul(bank(4), out_w[:, :], ssm[0:NST, 4], start=True, stop=True).then_inc(a_o.sem, 1)

            pe.wait_ge(ld_c, CLOADS)
            for q in range(NQ):
                pe.matmul(bank(6)[:, 0:P], wqT[:, q // 4, (q % 4) * P:(q % 4 + 1) * P], wo[:, q],
                          start=(q == 0), stop=(q == NQ - 1))
            for q in range(NQ):
                pe.matmul(bank(7)[:, 0:1], wo[:, q], col("beta", q), start=(q == 0), stop=(q == NQ - 1))
            for q in range(NQ):
                mm = pe.matmul(bank(7)[:, NH:2 * NH].rearrange("p (h q) -> p q h", h=2)[:, q],
                               wkT[:, q // 4, (q % 4) * P:(q % 4 + 1) * P], col("theta", 2 * q, 2),
                               start=True, stop=True)
            mm.then_inc(p_pe, 1)
            pe.wait_ge(a_res.sem, a_res.at(NBLK - 1, 2))
            pe.wait_ge(p_dve, 3)
            layernorm(1)
            pe.wait_ge(ln_out.sem, ln_out.at(2 * NBLK - 1, 1))
            pe.wait_ge(p_dve, PREP)
            pe.wait_ge(p_pool, 4)
            pe.wait_ge(ld_m, 2 * 16)

            with pe.Fori(0, NBLK) as i:
                def free(kind, which):
                    n = ring_no[(kind, which)] - 3
                    if n < 0:
                        n = max(m for m in range(-3, 0) if (m + NRING) % 3 == (n + 3) % 3)
                    k, w, s = ring[n]
                    pe.wait_ge(s.sem, (s.before if n < 0 else s.at)(i, taken_no[(k, w)]))
                    return bank(ring_bank(kind, which))

                def tokens(c):
                    return xb[:, c * P:(c + 1) * P]

                def project_targets(c):
                    for p in range(2):
                        pe.matmul(free("t", (c, p)), tokens(c), by_parity(wt, p), start=True,
                                  stop=True).then_inc(r_pe.sem, 1)

                def turn(kind, c, pair):
                    for s in range(2):
                        to = free(kind, (c, s))
                        for n in range(4):
                            mm = pe.transpose(to[:, n * P:(n + 1) * P], pair(4 * s + n), mat(M_IDENT))
                        mm.then_inc(r_pe.sem, 1)

                def turn_queries(c):
                    pe.wait_ge(q_n.sem, q_n.at(i, 2 * c + 2))
                    turn("v", c, lambda q: sq2[:, q * P:(q + 1) * P])

                def up(e):
                    for f in range(KC):
                        pe.matmul(free("up", (e, f)), mw1[:, e, f * P:(f + 1) * P], xn[:, blk(i)],
                                  start=True, stop=True).then_inc(r_pe.sem, 1)

                def down(e):
                    pe.wait_ge(m_mul.sem, m_mul.at(i, e) if e else m_mul.before(i, NE))
                    for f in range(KC):
                        pe.wait_ge(r_act.sem, r_act.at(i, taken_no[("up", (e, f))]))
                        mm = pe.matmul(bank(7), mw2[:, e * KC + f], hid[:, e % 2, f], start=(f == 0),
                                       stop=(f == KC - 1))
                    mm.then_inc(m_pe.sem, 1)

                def through(to, sums, x, w, c, done):
                    for p in range(2):
                        pe.matmul(bank(to + p), mat(M_NEG), by_parity(sums, p), start=True, stop=False,
                                  skip_group_check=True)
                        for q in range(NQ):
                            for b in range(BPB):
                                r = slice(64 * p, 64 * p + 64)
                                at = (to + p) * NB + q * HD
                                fr = c * P + b * CH
                                mm = pe.matmul(ps[64 * b:64 * b + 64, at:at + HD], x[r, q, fr:fr + CH],
                                               w(r, b, q), start=False, stop=True, skip_group_check=True)
                        mm.then_inc(done.sem, 1)

                pe.wait_ge(b_xb.sem, b_xb.at(i, 1))
                pe.wait_ge(t_res.sem, t_res.before(i, 2))
                for j in range(NB // P):
                    pe.matmul(ps[:, j * EXP:(j + 1) * EXP], xb[:, j * P:(j + 1) * P], gate_w[:, :],
                              start=True, stop=True)
                for c in range(NCH):
                    mm = pe.matmul(ps[:, 64 + c * NH:64 + (c + 1) * NH], tokens(c), w_th[:, :],
                                   start=True, stop=True)
                mm.then_inc(b_gate.sem, 1)
                for q in range(NQ):
                    pe.matmul(free("k", q), wk[:, q * P:(q + 1) * P], xb[:, :], start=True,
                              stop=True).then_inc(r_pe.sem, 1)
                pe.wait_ge(b_comb.sem, b_comb.at(i, 1))
                for j in range(NB // P):
                    mm = pe.transpose(ps[0:EXP, NB + j * P:NB + (j + 1) * P],
                                      small[:, 96 + 8 * j:104 + 8 * j], mat(M_IDENT))
                mm.then_inc(b_ct.sem, 1)
                project_targets(0)
                pe.wait_ge(b_gz.sem, b_gz.at(i, 2))
                pe.wait_ge(b_ctc.sem, b_ctc.at(i, 1))
                def keys_through(c):
                    if c:
                        pe.wait_ge(z_es.sem, z_es.at(i, 2 * c))
                        pe.wait_ge(w_dve.sem, w_dve.at(i, 2 * c))
                        through(0, esum, xkT, lambda r, b, q: wst[r, b, q * HD:(q + 1) * HD], c, z_pe)
                    else:
                        pe.wait_ge(r_act.sem, r_act.at(i, taken_no[("k", NQ - 1)]))
                        through(0, e_init, xkT, lambda r, b, q: w_init[r, q * HD:(q + 1) * HD], c, z_pe)

                def queries_through(c):
                    pe.wait_ge(w_dve.sem, w_dve.at(i, 2 * c + 2))
                    pe.wait_ge(z_es.sem, z_es.at(i, 2 * c + 2))
                    if c == 0:
                        pe.wait_ge(r_act.sem, r_act.at(i, taken_no[("q", NQ - 1)]))
                    through(2, esum, xqT, lambda r, b, q: wst[r, b, q * HD:(q + 1) * HD], c, q_pe)

                keys_through(0)
                for q in range(NQ):
                    pe.matmul(free("q", q), wq[:, q * P:(q + 1) * P], xb[:, :], start=True,
                              stop=True).then_inc(r_pe.sem, 1)
                for c in range(NCH):
                    turn("kt", c, lambda q: xkT[:, q, c * P:(c + 1) * P])
                    if c + 1 < NCH:
                        project_targets(c + 1)
                    up(2 * c)
                    down(2 * c)
                    up(2 * c + 1)
                    if c:
                        turn_queries(c - 1)
                    pe.wait_ge(z_eg.sem, z_eg.at(i, 2 * c + 2))
                    pe.wait_ge(r_act.sem, r_act.at(i, taken_no[("kt", (c, 1))]))
                    pe.sem_inc(stand, 1)
                    for b in range(BPB):
                        for q in range(NQ):
                            for p in range(2):
                                r = slice(64 * b, 64 * b + 64)
                                nat = slice((2 * q + p) * HD, (2 * q + p + 1) * HD)
                                mm = pe.matmul(ps[64 * p:64 * p + 64, (2 + b) * NB + q * HD:(2 + b) * NB + (q + 1) * HD],
                                               ktok[r, nat], eg[r, nat], start=True, stop=True,
                                               skip_group_check=True)
                        mm.then_inc(w_pe.sem, 1)
                    down(2 * c + 1)
                    if c + 1 < NCH:
                        keys_through(c + 1)
                    queries_through(c)
                up(EXP)
                down(EXP)
                turn_queries(NCH - 1)
                pe.wait_ge(r_act.sem, r_act.at(i, RA))
                pe.matmul(bank(2), wqo[:, :], xn[:, blk(i)], start=True, stop=False)
                pe.matmul(bank(2), mb2[:, :], combT[:, :], start=False, stop=False)
                for q in range(NQ):
                    mm = pe.matmul(bank(2), wo[:, q], xqT[:, q], start=False, stop=(q == NQ - 1))
                mm.then_inc(t_out.sem, 1)

        @block.scalar
        def _(act):
            def layernorm(turn):
                base = turn * NBLK
                with act.Fori(0, NBLK) as i:
                    act.wait_ge(ln_centred, i + base + 1)
                    act.activation(lsq[:, bass.ds(i * 2 * NB, NB)], ps[:, bass.ds(i * 2 * NB, NB)],
                                   ACT.Square).then_inc(ln_sq, 1)
                with act.Fori(0, NBLK) as i:
                    act.wait_ge(ln_var, i + base + 1)
                    act.activation(lsq[:, bass.ds(i * 2 * NB + NB, NB)], ps[:, bass.ds(i * 2 * NB + NB, NB)],
                                   ACT.Sqrt, bias=eps_ln[:, 0:1]).then_inc(ln_sd, 1)

            act.wait_ge(eps_set, 3)
            layernorm(0)
            act.wait_ge(ld_small, 16)
            act.wait_ge(pads_set, 1)
            with act.Fori(0, NBLK) as i:
                for m in range(DC):
                    act.wait_ge(a_in.sem, a_in.at(i, m + 1))
                    act.wait_ge(a_conv.sem, a_conv.before(i, m + 1))
                    act.activation(hpad[:, m, :, PAD:PAD + SEQ], bank(m).rearrange("p (b s) -> p b s", b=BPB),
                                   ACT.Identity, bias=col("in_b", m)).then_inc(a_pad.sem, 1)
                for m in range(KC):
                    act.wait_ge(a_w12.sem, a_w12.at(i, m + 1))
                    if m == 0:
                        act.wait_ge(a_w3.sem, a_w3.before(i, 1))
                    act.activation(u0[:, m], bank((2 + 2 * m) % 8), ACT.Silu,
                                   scale=col("w1_s", m)).then_inc(a_silu.sem, 1)
                for m in range(DC):
                    act.wait_ge(a_conv.sem, a_conv.at(i, m + 1))
                    act.activation(hs[:, m], conv[:, m], ACT.Silu, bias=col("conv_b", m)).then_inc(a_hs.sem, 1)
                for m in range(KC):
                    act.wait_ge(a_h1.sem, a_h1.at(i, m + 1))
                    act.activation(g1[:, m], bank(2 + m), ACT.Gelu, scale=col("h1_s", m)).then_inc(a_g1.sem, 1)
                for m in range(KC):
                    act.wait_ge(a_h2.sem, a_h2.at(i, m + 1))
                    act.activation(g2[:, m], bank((6 + m) % 8), ACT.Gelu, scale=col("h2_s", m)).then_inc(a_g2.sem, 1)
                act.wait_ge(a_xp.sem, a_xp.at(i, 1))
                act.wait_ge(a_y.sem, a_y.before(i, BPB))
                act.activation(ssm[0:NST, 0], bank(3, NST), ACT.Exp).then_inc(a_ex.sem, 1)
                act.activation(ssm[0:NST, 1], bank(3, NST, 32), ACT.Copy).then_inc(a_ex.sem, 1)
                act.activation(ssm[0:NST, 2], bank(3, NST, 64), ACT.Copy).then_inc(a_ex.sem, 1)
                act.activation(ssm[0:NST, 3], bank(3, NST, 32), ACT.Tanh, scale=0.5).then_inc(a_ex.sem, 1)
                act.wait_ge(a_ex.sem, a_ex.at(i, 1))
                act.activation(ssm[0:NST, 0], ssm[0:NST, 0], ACT.Exp, scale=-1.0).then_inc(a_ex.sem, 1)
            layernorm(1)

            act.wait_ge(p_dve, PREP)
            with act.Fori(0, NBLK) as i:
                def take(kind, which):
                    act.wait_ge(r_pe.sem, r_pe.at(i, ring_no[(kind, which)] + 1))
                    return bank(ring_bank(kind, which))

                def keys_by_token(c):
                    for p in range(2):
                        src = take("kt", (c, p))
                        act.wait_ge(w_pe.sem, w_pe.at(i, 2 * c) if c else w_pe.before(i, 2 * NCH))
                        act.activation(ktok[:, p * QD:(p + 1) * QD], src, ACT.Copy).then_inc(r_act.sem, 1)

                def queries_turned(c):
                    for s in range(2):
                        act.activation(xqT[:, 4 * s:4 * s + 4, c * P:(c + 1) * P],
                                       take("v", (c, s)).rearrange("p (q t) -> p q t", q=4),
                                       ACT.Copy).then_inc(r_act.sem, 1)

                def query_squares(c):
                    for p in range(2):
                        act.wait_ge(q_pe.sem, q_pe.at(i, 2 * c + p + 1))
                        act.activation(sq2[:, p * QD:(p + 1) * QD], bank(2 + p), ACT.Square)\
                            .then_inc(q_sq.sem, 1)

                def gelus(e):
                    act.wait_ge(m_pe.sem, m_pe.at(i, e - 1) if e >= 2 else m_pe.before(i, NE))
                    for f in range(KC):
                        act.activation(hid[:, e % 2, f], take("up", (e, f)), ACT.Gelu,
                                       bias=col("b1", e * KC + f)).then_inc(r_act.sem, 1)

                act.wait_ge(b_gz.sem, b_gz.at(i, 2))
                for n, (o, w) in enumerate(((0, 32), (32, 64))):
                    act.activation(small[:, 128 + o:128 + o + w], small[:, 224 + o:224 + o + w], ACT.Tanh,
                                   scale=0.5).then_inc(b_th.sem, 1)
                for q in range(NQ):
                    src = take("k", q)
                    act.wait_ge(z_pe.sem, z_pe.before(i, 2 * NCH))
                    act.activation(xkT[:, q], src, ACT.Copy).then_inc(r_act.sem, 1)
                for c in range(NCH):
                    for p in range(2):
                        act.wait_ge(z_pe.sem, z_pe.at(i, 2 * c + p + 1))
                        act.wait_ge(z_eg.sem, z_eg.at(i, 2 * c) if c else z_eg.before(i, 2 * NCH))
                        act.activation(sq[:, p * QD:(p + 1) * QD], bank(p), ACT.Square).then_inc(z_sq.sem, 1)
                    if c:
                        query_squares(c - 1)
                    else:
                        for q in range(NQ):
                            src = take("q", q)
                            act.wait_ge(t_out.sem, t_out.before(i, 1))
                            act.activation(xqT[:, q], src, ACT.Copy).then_inc(r_act.sem, 1)
                    keys_by_token(c)
                    gelus(2 * c)
                    gelus(2 * c + 1)
                    if c:
                        queries_turned(c - 1)
                query_squares(NCH - 1)
                gelus(EXP)
                queries_turned(NCH - 1)

        @block.vector
        def _(dve):
            tt, ts, stt = dve.tensor_tensor, dve.tensor_scalar, dve.scalar_tensor_tensor

            def layernorm(turn):
                base = turn * NBLK
                with dve.Fori(0, NBLK) as i:
                    dve.wait_ge(ln_sd, i + base + 1)
                    dev = lsq[:, bass.ds(i * 2 * NB + NB, NB)]
                    dve.reciprocal(dev, dev).then_inc(ln_rs, 1)
                with dve.Fori(0, NBLK) as i:
                    dve.wait_ge(ln_rs, i + base + 1)
                    dev = lsq[:, bass.ds(i * 2 * NB + NB, NB)]
                    o = by_chunk(xn[:, blk(i)]) if turn else xn[:, blk(i)]
                    centred = ps[:, bass.ds(i * 2 * NB, NB)]
                    tt(o, by_batch(centred) if turn else centred, by_batch(dev) if turn else dev, ALU.mult)\
                        .then_inc(ln_out.sem, 1)

            layernorm(0)
            dve.wait_ge(ln_out.sem, ln_out.at(NBLK - 1, 1))
            dve.wait_ge(ld_small, 16)
            dve.wait_ge(ld_x, 32)
            with dve.Fori(0, NBLK) as i:
                for m in range(KC):
                    dve.wait_ge(a_silu.sem, a_silu.at(i, m + 1))
                    stt(u0[:, m], bank((3 + 2 * m) % 8), col("w2_s", m), u0[:, m], ALU.mult,
                        ALU.mult).then_inc(a_u.sem, 1)
                for m in range(DC):
                    dve.wait_ge(a_pad.sem, a_pad.at(i, m + 1))
                    dve.wait_ge(a_hs.sem, a_hs.before(i, m + 1))
                    o = conv[:, m].rearrange("p (b s) -> p b s", b=BPB)
                    ts(o, hpad[:, m, :, 0:SEQ], col("conv_w", m * TAPS), None, ALU.mult).then_inc(a_step, 1)
                    for t in range(1, TAPS):
                        dve.wait_ge(a_step, i * (DC * (TAPS - 1)) + (m * (TAPS - 1) + t))
                        ins = stt(o, hpad[:, m, :, t:t + SEQ], col("conv_w", m * TAPS + t), o, ALU.mult, ALU.add)
                        ins.then_inc(a_conv.sem if t == TAPS - 1 else a_step, 1)
                dve.wait_ge(a_ex.sem, a_ex.at(i, 4))
                stt(ssm[0:NST, 3], ssm[0:NST, 3], 1.0, ssm[0:NST, 1], ALU.add, ALU.mult).then_inc(a_b.sem, 1)
                dve.wait_ge(a_b.sem, a_b.at(i, 1))
                stt(ssm[0:NST, 3], ssm[0:NST, 3], 0.5, ssm[0:NST, 2], ALU.mult, ALU.mult).then_inc(a_b.sem, 1)
                dve.wait_ge(a_b.sem, a_b.at(i, 2))
                dve.wait_ge(a_ex.sem, a_ex.at(i, 5))
                dve.wait_ge(a_o.sem, a_o.before(i, 1))
                for b in range(BPB):
                    s = slice(b * SEQ, (b + 1) * SEQ)
                    dve.tensor_tensor_scan(ssm[0:NST, 4, s], ssm[0:NST, 0, s], ssm[0:NST, 3, s], 0.0,
                                           ALU.mult, ALU.add).then_inc(a_y.sem, 1)
                dve.wait_ge(a_w3.sem, a_w3.at(i, 1))
                stt(res[:, :], bank(2), col("w3_s"), x_sb[:, blk(i)], ALU.mult, ALU.add).then_inc(a_res.sem, 1)
                dve.wait_ge(a_res.sem, a_res.at(i, 1))
                dve.wait_ge(a_o.sem, a_o.at(i, 1))
                stt(x_sb[:, blk(i)], bank(4), col("out_b"), res[:, :], ALU.add, ALU.add).then_inc(a_res.sem, 1)

            done = [0]

            def step(ins):
                done[0] += 1
                ins.then_inc(p_dve, 1)
                dve.wait_ge(p_dve, done[0])

            dve.wait_ge(ld_c, CLOADS)
            dve.wait_ge(p_pe, 1)
            step(dve.tensor_copy(wqo[:, :], bank(6)[:, 0:P]))
            step(dve.tensor_copy(be_wo[:, :], bank(7)[:, 0:1]))
            step(dve.tensor_copy(w_th[:, :], bank(7)[:, NH:2 * NH]))
            for q in range(NQ):
                ins = ts(wo[:, q], wo[:, q], col("gamma", q), None, ALU.mult)
            step(ins)
            step(dve.tensor_reduce(pstat[:, 0:NQ], qd(w_init[:, :]), AX_X, ALU.add))
            step(ts(pstat[:, 0:NQ], pstat[:, 0:NQ], 1.0 / HD, None, ALU.mult))
            step(tt(qd(w_init[:, :]), qd(w_init[:, :]), over_d(pstat[:, 0:NQ]), ALU.subtract))
            e3 = e_init[:, :].rearrange("p (h d) -> p h d", d=HD)
            step(dve.tensor_reduce(pstat[:, 0:NH], e3, AX_X, ALU.add))
            step(ts(pstat[:, 0:NH], pstat[:, 0:NH], 1.0 / HD, None, ALU.mult))
            step(tt(e3, pstat[:, 0:NH].unsqueeze(2).to_broadcast([P, NH, HD]), e3, ALU.subtract))
            te = small[:, 383:384]
            t1 = small[:, 382:383]
            step(tt(t1, col("alpha"), col("inv_index"), ALU.add))
            step(ts(te, t1, 0.0, 0.5 / HD, ALU.max, ALU.mult))
            assert done[0] == PREP
            layernorm(1)
            dve.wait_ge(ln_out.sem, ln_out.at(2 * NBLK - 1, 1))
            dve.wait_ge(p_pool, 4)

            with dve.Fori(0, NBLK) as i:
                n_steps = [0]

                def link(ins):
                    n_steps[0] += 1
                    ins.then_inc(b_step, 1)
                    dve.wait_ge(b_step, i * BSTEPS + n_steps[0])

                def link_later(ins):
                    n_steps[0] += 1
                    return ins.then_inc(b_step, 1) and n_steps[0]

                def after(n):
                    dve.wait_ge(b_step, i * BSTEPS + n)

                def take(kind, which):
                    dve.wait_ge(r_pe.sem, r_pe.at(i, ring_no[(kind, which)] + 1))
                    return bank(ring_bank(kind, which))

                def targets(c):
                    for p in range(2):
                        src = take("t", (c, p))
                        tt(qd(ttok[:, c % 2, p * QD:(p + 1) * QD]), qd(src), by_parity(gb, p),
                           ALU.add).then_inc(r_dve.sem, 1)

                def query_variances(c):
                    v2 = small[:, 224:240]
                    for p in range(2):
                        dve.wait_ge(q_sq.sem, q_sq.at(i, 2 * c + p + 1))
                        ins = dve.tensor_reduce(v2[:, 8 * p:8 * p + 8], qd(sq2[:, p * QD:(p + 1) * QD]), AX_X, ALU.add)
                    link(ins)
                    ts(v2, v2, 1.0 / HD, TTT_EPS, ALU.mult, ALU.add).then_inc(q_ve.sem, 1)

                def normalise_queries(c):
                    dve.wait_ge(q_r.sem, q_r.at(i, c + 1))
                    for p in range(2):
                        tt(by_parity(sq2, p), qd(bank(2 + p)), over_d(small[:, 240 + 8 * p:248 + 8 * p]),
                           ALU.mult).then_inc(q_n.sem, 1)

                def mix(e):
                    dve.wait_ge(m_pe.sem, m_pe.at(i, e + 1))
                    if e == 0:
                        dve.wait_ge(b_cbc.sem, b_cbc.at(i, 16))
                        dve.wait_ge(t_res.sem, t_res.before(i, 2))
                        tt(macc[:, :], bank(7), comb_bc[:, 0], ALU.mult).then_inc(m_mul.sem, 1)
                        return
                    if e >= 2:
                        dve.wait_ge(m_add.sem, m_add.at(i, e - 1))
                    if e < EXP:
                        tt(mtmp[:, :], bank(7), comb_bc[:, e], ALU.mult).then_inc(m_mul.sem, 1)
                    else:
                        ts(mtmp[:, :], bank(7), col("sb2"), 0.1, ALU.add, ALU.mult).then_inc(m_mul.sem, 1)
                    dve.wait_ge(m_mul.sem, m_mul.at(i, e + 1))
                    tt(macc[:, :], macc[:, :], mtmp[:, :], ALU.add).then_inc(m_add.sem, 1)

                dve.tensor_copy(xb[:, :], xn[:, blk(i)]).then_inc(b_xb.sem, 1)
                dve.wait_ge(b_gate.sem, b_gate.at(i, 1))
                tt(small[:, 224:256].rearrange("p (j e) -> p j e", e=EXP),
                   ps[:, 0:32].rearrange("p (j e) -> p j e", e=EXP),
                   col("gate_b", 0, EXP).unsqueeze(1).to_broadcast([P, 4, EXP]), ALU.add).then_inc(b_gz.sem, 1)
                tt(small[:, 256:320].rearrange("p (c h) -> p c h", h=NH),
                   ps[:, 64:128].rearrange("p (c h) -> p c h", h=NH),
                   col("theta_bias", 0, NH).unsqueeze(1).to_broadcast([P, NCH, NH]), ALU.add).then_inc(b_gz.sem, 1)
                dve.wait_ge(b_th.sem, b_th.at(i, 2))
                score = small[:, 320:352]
                link(ts(score, small[:, 128:160], 1.0, 0.5, ALU.add, ALU.mult))
                top = small[:, 64:96]
                dve.sem_inc(stand_dve, 1)
                for j in range(4):
                    ins = dve.max(top[:, 8 * j:8 * j + 8], score[:, 8 * j:8 * j + 8])
                link(ins)
                dve.sem_inc(stand_dve, 1)
                for j in range(4):
                    ins = dve.max_index(idx[:, j], top[:, 8 * j:8 * j + 8], score[:, 8 * j:8 * j + 8])
                link(ins)
                t3 = top.rearrange("p (j e) -> p j e", e=8)
                idf = small[:, 352:360].rearrange("p (j e) -> p j e", e=2)
                tsum = small[:, 360:364].rearrange("p (j e) -> p j e", e=1)
                link(dve.tensor_copy(idf, idx[:, :, 0:2]))
                link(tt(tsum, t3[:, :, 0:1], t3[:, :, 1:2], ALU.add))
                link(ts(tsum, tsum, TOPK_EPS, None, ALU.add))
                link(dve.reciprocal(tsum, tsum))
                link(tt(t3[:, :, 0:2], t3[:, :, 0:2], tsum.to_broadcast([P, 4, 2]), ALU.mult))
                comb = small[:, 96:128].rearrange("p (j e) -> p j e", e=EXP)
                c1 = small[:, 32:64].rearrange("p (j e) -> p j e", e=EXP)
                nos = col("expert_no", 0, EXP).unsqueeze(1).to_broadcast([P, 4, EXP])
                link(tt(comb, nos, idf[:, :, 0:1].to_broadcast([P, 4, EXP]), ALU.is_equal))
                link(tt(comb, comb, t3[:, :, 0:1].to_broadcast([P, 4, EXP]), ALU.mult))
                link(tt(c1, nos, idf[:, :, 1:2].to_broadcast([P, 4, EXP]), ALU.is_equal))
                link(tt(c1, c1, t3[:, :, 1:2].to_broadcast([P, 4, EXP]), ALU.mult))
                tt(comb, comb, c1, ALU.add).then_inc(b_comb.sem, 1)
                eta = small[:, 160:224]
                ts(eta, eta, 1.0, te, ALU.add, ALU.mult).then_inc(b_eta.sem, 1)
                dve.wait_ge(b_ct.sem, b_ct.at(i, 1))
                dve.wait_ge(b_cst.sem, b_cst.before(i, 16))
                dve.wait_ge(t_out.sem, t_out.before(i, 1))
                dve.tensor_copy(combT[:, :], bank(1, EXP)).then_inc(b_ctc.sem, 1)
                targets(0)
                for c in range(NCH):
                    ve = small[:, 0:16]
                    rr = small[:, 16:32]
                    s1, s2, ce = small[:, 32:48], small[:, 48:64], small[:, 64:80]
                    for p in range(2):
                        dve.wait_ge(z_sq.sem, z_sq.at(i, 2 * c + p + 1))
                        ins = dve.tensor_reduce(ve[:, 8 * p:8 * p + 8], qd(sq[:, p * QD:(p + 1) * QD]), AX_X, ALU.add)
                    link(ins)
                    ts(ve, ve, 1.0 / HD, TTT_EPS, ALU.mult, ALU.add).then_inc(z_ve.sem, 1)
                    if c:
                        query_variances(c - 1)
                    if c + 1 < NCH:
                        targets(c + 1)
                    dve.wait_ge(z_r.sem, z_r.at(i, c + 1))
                    for p in range(2):
                        h = slice(p * QD, (p + 1) * QD)
                        tt(qd(xh[:, h]), qd(bank(p)), over_d(rr[:, 8 * p:8 * p + 8]), ALU.mult).then_inc(z_xh.sem, 1)
                    ev, od = slice(0, QD), slice(QD, 2 * QD)
                    e8, o8 = slice(0, 8), slice(8, 16)
                    dve.wait_ge(z_xh.sem, z_xh.at(i, 2 * c + 2))
                    a1 = link_later(tt(qd(gx[:, od]), qd(xh[:, od]), by_parity(gg, 1), ALU.mult))
                    tt(ce, rr, eta[:, c * NH:(c + 1) * NH], ALU.mult)
                    after(a1)
                    a1 = link_later(tt(gx[:, od], gx[:, od], ttok[:, c % 2, od], ALU.add))
                    after(a1)
                    a1 = link_later(tt(sq[:, od], gx[:, od], xh[:, od], ALU.mult))
                    a2 = link_later(dve.tensor_reduce(s1[:, o8], qd(gx[:, od]), AX_X, ALU.add))
                    after(a1)
                    a1 = link_later(dve.tensor_reduce(s2[:, o8], qd(sq[:, od]), AX_X, ALU.add))
                    dve.wait_ge(z_gx.sem, z_gx.at(i, c + 1))
                    b1 = link_later(tt(sq[:, ev], gx[:, ev], xh[:, ev], ALU.mult))
                    after(b1)
                    b1 = link_later(dve.tensor_reduce(s2[:, e8], qd(sq[:, ev]), AX_X, ALU.add))
                    a1 = link_later(ts(s2[:, o8], s2[:, o8], 1.0 / HD, None, ALU.mult))
                    after(b1)
                    ts(s2[:, e8], s2[:, e8], 1.0 / HD, None, ALU.mult).then_inc(z_s2.sem, 1)
                    b2 = link_later(dve.tensor_reduce(s1[:, e8], qd(gx[:, ev]), AX_X, ALU.add))
                    after(a1)
                    a1 = link_later(tt(qd(sq[:, od]), qd(xh[:, od]), over_d(s2[:, o8]), ALU.mult))
                    after(b2)
                    b2 = link_later(ts(s1, s1, 1.0 / HD, None, ALU.mult))
                    after(a1)
                    a1 = link_later(tt(gx[:, od], gx[:, od], sq[:, od], ALU.subtract))
                    after(b2)
                    b2 = link_later(tt(qd(gx[:, ev]), qd(gx[:, ev]), over_d(s1[:, e8]), ALU.subtract))
                    after(a1)
                    a1 = link_later(tt(qd(gx[:, od]), qd(gx[:, od]), over_d(s1[:, o8]), ALU.subtract))
                    dve.wait_ge(z_u.sem, z_u.at(i, c + 1))
                    after(b2)
                    b2 = link_later(tt(gx[:, ev], gx[:, ev], sq[:, ev], ALU.subtract))
                    after(a1)
                    tt(by_parity(eg, 1), qd(gx[:, od]), over_d(ce[:, o8]), ALU.mult).then_inc(z_eg.sem, 1)
                    after(b2)
                    tt(by_parity(eg, 0), qd(gx[:, ev]), over_d(ce[:, e8]), ALU.mult).then_inc(z_eg.sem, 1)
                    if c:
                        normalise_queries(c - 1)
                    mix(2 * c)
                    for b in range(BPB):
                        dve.wait_ge(w_pe.sem, w_pe.at(i, 2 * c + b + 1))
                        tt(wst[:, b], (w_init[:, :] if c == 0 else wst[:, b]), bank(2 + b),
                           ALU.subtract).then_inc(w_dve.sem, 1)
                    mix(2 * c + 1)
                query_variances(NCH - 1)
                mix(EXP)
                normalise_queries(NCH - 1)
                dve.wait_ge(t_out.sem, t_out.at(i, 1))
                dve.wait_ge(t_dma.sem, t_dma.before(i, 16))
                dve.wait_ge(m_add.sem, m_add.at(i, NE - 1))
                stt(mtmp[:, :], bank(2), be_wo[:, 0:1], macc[:, :], ALU.add, ALU.add).then_inc(t_res.sem, 1)
                dve.wait_ge(t_res.sem, t_res.at(i, 1))
                tt(by_batch(osb), by_chunk(mtmp[:, :]), by_batch(x_sb[:, blk(i)]), ALU.add).then_inc(t_res.sem, 1)
                assert n_steps[0] == BSTEPS, n_steps[0]


def kernel(**v):
    import numpy as np
    import concourse.bacc as bacc
    from concourse.bass_utils import run_bass_kernel_spmd as run

    v = {k: np.ascontiguousarray(x) for k, x in v.items()}

    def A(n):
        return v["L0_attn_" + n]

    def M(n):
        return v["L0_ffn_" + n]

    def T(n):
        return v["L1_attn_" + n]

    def E(n):
        return v["L1_ffn_" + n]

    f = np.float32

    def chunks(w, n):
        return w.reshape(n, P, -1).transpose(1, 0, 2)

    half = np.arange(P) // 64
    same = half[:, None] == half[None, :]
    eye = np.eye(P, dtype=f)
    mats = np.concatenate([eye - f(1 / P), np.full((P, P), 1 / P, f), -same.astype(f),
                           same.astype(f) / f(HD), eye], axis=1)
    packed = {
        "in_b": A("in_b").reshape(DC, P).T, "conv_w": A("conv_w").reshape(DC, P, TAPS).transpose(1, 0, 2).reshape(P, -1),
        "conv_b": A("conv_b").reshape(DC, P).T,
        "w1_s": M("w1_s").reshape(KC, P).T, "w2_s": M("w2_s").reshape(KC, P).T,
        "h1_s": M("h1_s").reshape(KC, P).T, "h2_s": M("h2_s").reshape(KC, P).T,
        "w3_s": M("w3_s").reshape(1, P).T, "out_b": A("out_b").reshape(1, P).T,
        "gamma": T("gamma").reshape(NQ, P).T, "beta": T("beta").reshape(NQ, P).T,
        "b1": np.concatenate([E("b1").reshape(EXP * KC, P), E("sb1").reshape(KC, P)]).T,
        "sb2": E("sb2").reshape(1, P).T,
        "alpha": np.tile(T("alpha"), 2).reshape(P, 1),
        "inv_index": np.tile(f(1) / np.arange(1, CH + 1, dtype=f), 2).reshape(P, 1),
        "theta_bias": np.broadcast_to(T("theta_bias").reshape(NQ, 2).T.reshape(1, NH), (P, NH)),
        "gate_b": np.broadcast_to(E("gate_b").reshape(1, EXP), (P, EXP)),
        "expert_no": np.broadcast_to(np.arange(EXP, dtype=f).reshape(1, EXP), (P, EXP)),
    }
    cols = np.zeros((P, NCOLS), f)
    for name, x in packed.items():
        at, n = COLS[name]
        cols[:, at:at + n] = x
    th = T("theta").reshape(NQ, 2, HD)
    for q in range(NQ):
        for p in range(2):
            cols[64 * p:64 * p + 64, COLS["theta"][0] + 2 * q + p] = th[q, p]
    xp_w = np.zeros((P, DC, 96), f)
    xw = A("xp_w").T.reshape(DC, P, 2 * NST).transpose(1, 0, 2)
    xp_w[:, :, 0:16], xp_w[:, :, 32:48], xp_w[:, :, 64:80] = xw[:, :, 0:16], xw[:, :, 16:32], 1
    xp_row = np.zeros((1, 96 + NB), f)
    xp_row[0, 0:16], xp_row[0, 32:48], xp_row[0, 96:] = A("xp_b")[0:16], A("xp_b")[16:32], 1
    e_init = np.zeros((P, NH * HD), f)
    e_init[0] = e_init[64] = T("b1").reshape(NH * HD)
    arrays = {
        "xT": A("x").reshape(TOK, D).T, "mats": mats, "cols": cols,
        "in_w": A("in_w").T, "w1": M("w1_w").T, "w2": M("w2_w").T,
        "h1": chunks(M("h1_w").T, KC), "h2": chunks(M("h2_w").T, KC), "w3": chunks(M("w3_w").T, KC),
        "xp_w": xp_w, "xp_row": xp_row, "out_w": A("out_w").T,
        "wq": T("wq"), "wk": T("wk"), "wv": T("wv"), "wo": chunks(T("wo"), NQ),
        "wqT": chunks(T("wq").T, NQ).reshape(P, 2, NB), "wkT": chunks(T("wk").T, NQ).reshape(P, 2, NB),
        "gamma_row": T("gamma").reshape(NH * HD), "beta_row": T("beta").reshape(NH * HD),
        "w_init": T("W1").reshape(NQ, P, HD).transpose(1, 0, 2).reshape(P, QD),
        "e_init": e_init,
        "mw1": np.concatenate([E("w1"), E("sw1")[None]]).transpose(1, 0, 2),
        "mw2": np.concatenate([E("w2").reshape(EXP * KC, P, D), E("sw2").reshape(KC, P, D)]).transpose(1, 0, 2),
        "mb2": E("b2"), "gate_w": E("gate_w").T,
    }
    nc = bacc.Bacc("TRN2", target_bir_lowering=False, num_devices=1)
    fed, aps = {}, {}
    for name, x in arrays.items():
        x = np.ascontiguousarray(x)
        fed["in_" + name] = x
        aps[name] = nc.dram_tensor("in_" + name, x.shape, mybir.dt.from_np(x.dtype), kind="ExternalInput").ap()
    out = nc.dram_tensor("out", (D, TOK), F32, kind="ExternalOutput").ap()
    build(nc, aps, out)
    r = run(nc, [fed], core_ids=[0])
    return np.ascontiguousarray(np.asarray(r.results[0]["out"]).T).reshape(BATCH, SEQ, D)
```

```python
from contextlib import ExitStack

import concourse.bass as bass
from concourse import mybir

F32 = mybir.dt.float32
F32R = mybir.dt.float32r
U32 = mybir.dt.uint32
ALU = mybir.AluOpType
ACT = mybir.ActivationFunctionType
AX_X = mybir.AxisListType.X

P = 128
BATCH, SEQ, D = 8, 256, 128
TOK = BATCH * SEQ
NB = 512
NBLK = TOK // NB
BPB = NB // SEQ
HID = 512
KC = HID // P
DI, NST, TAPS = 256, 16, 4
DC = DI // P
PAD = TAPS - 1
NH, HD, CH = 16, 64, 64
NCH = SEQ // CH
NQ = NH // 2
QD = NQ * HD
EXP = 8
NE = EXP + 1
NSPLIT = 1
MIXES = 2
LN_EPS, TTT_EPS, TOPK_EPS = 1e-5, 1e-6, 1e-6

COLS = {}
_at = 0
for _name, _n in (("in_b", DC), ("conv_w", DC * TAPS), ("conv_b", DC), ("w1_s", KC), ("w2_s", KC),
                  ("h1_s", KC), ("h2_s", KC), ("w3_s", 1), ("out_b", 1), ("gamma", NQ), ("beta", NQ),
                  ("b1", NE * KC), ("sb2", 1), ("theta", 2 * NQ), ("alpha", 1), ("inv_index", 1),
                  ("theta_bias", NH), ("gate_b", EXP), ("expert_no", EXP)):
    COLS[_name] = (_at, _n)
    _at += _n
NCOLS = _at
M_CENTER, M_MEAN, M_NEG, M_IDENT = range(4)


class Signal:

    def __init__(self, sem, per):
        self.sem, self.per = sem, per

    def at(self, i, k):
        return i * self.per + (k + self.per)

    def before(self, i, k):
        return i * self.per + k


def build(nc, a, out):
    with ExitStack() as ctx:
        def sb(name, shape, dt=F32):
            return ctx.enter_context(nc.sbuf_tensor(name, shape, dt))

        def sem(name):
            return ctx.enter_context(nc.semaphore(name))

        credited = []

        def signal(name, per):
            s = Signal(sem(name), per)
            credited.append(s)
            return s

        x_sb = sb("x_sb", [P, TOK])
        xn = sb("xn", [P, TOK])
        mats = sb("mats", [P, 4 * P])
        cols = sb("cols", [P, NCOLS])

        def mat(n):
            return mats[:, n * P:(n + 1) * P]

        def col(name, k=0, n=1, rows=P):
            return cols[0:rows, COLS[name][0] + k:COLS[name][0] + k + n]

        l0 = sb("l0", [P, 2 * KC * HID + 2 * HID + KC * D])
        h1 = l0[:, 0:KC * HID].rearrange("p (k n) -> p k n", k=KC)
        h2 = l0[:, KC * HID:2 * KC * HID].rearrange("p (k n) -> p k n", k=KC)
        w1, w2 = (l0[:, 2 * KC * HID + n * HID:2 * KC * HID + (n + 1) * HID] for n in range(2))
        w3 = l0[:, 2 * KC * HID + 2 * HID:].rearrange("p (k n) -> p k n", k=KC)

        wq = sb("wq", [P, 2, NH * HD], F32R)
        wk = sb("wk", [P, 2, NH * HD], F32R)
        wt = sb("wt", [P, 2, NH * HD], F32R)
        mw1_s = sb("mw1_s", [P, 2, NSPLIT, HID], F32R)
        xb_s = sb("xb_s", [P, 2, NB], F32R)
        esum_s = sb("esum_s", [P, 2, NH * HD], F32R)
        neg = sb("neg", [P, P], F32R)
        wo = sb("wo", [P, NQ, D])
        mw1 = sb("mw1", [P, NE - NSPLIT, HID])
        mw2 = sb("mw2", [P, NE * KC, D])
        mb2 = sb("mb2", [EXP, D])
        gate_w = sb("gate_w", [P, EXP])
        wqo = sb("wqo", [P, D])
        w_th = sb("w_th", [P, NH])
        w_init = sb("w_init", [P, QD])
        e_init = sb("e_init", [P, NH * HD])
        gg = sb("gg", [P, NH * HD])
        gb = sb("gb", [P, NH * HD])

        work = sb("work", [P, 12288])
        used = [0]

        def cut(n):
            used[0] += n
            assert used[0] <= 12288
            return work[:, used[0] - n:used[0]]

        hpad = cut(DC * BPB * (PAD + SEQ)).rearrange("p (c b s) -> p c b s", c=DC, b=BPB)
        conv = cut(DC * NB).rearrange("p (c n) -> p c n", c=DC)
        hs = cut(DC * NB).rearrange("p (c n) -> p c n", c=DC)
        u0 = cut(KC * NB).rearrange("p (c n) -> p c n", c=KC)
        g1 = cut(KC * NB).rearrange("p (c n) -> p c n", c=KC)
        g2 = u0
        ssm = cut(5 * NB).rearrange("p (c n) -> p c n", c=5)
        res = cut(NB)
        used[0] = DC * BPB * (PAD + SEQ)
        lsq = cut(TOK)
        used[0] = 0
        xkT = cut(NQ * NB).rearrange("p (q n) -> p q n", q=NQ)
        xqT = cut(NQ * NB).rearrange("p (q n) -> p q n", q=NQ)
        hid = cut(2 * KC * NB).rearrange("p (e f n) -> p e f n", e=2, f=KC)
        xb = sb("xb", [P, NB])
        combT = sb("combT", [EXP, NB])
        comb_bc = sb("comb_bc", [P, MIXES, NB])
        xh, gx, eg, esum, ktok = (l0[:, n * NH * HD:(n + 1) * NH * HD] for n in range(5))
        sq2 = sb("sq2", [P, NH * HD])
        ttok = x_sb[:, :].rearrange("p (t n) -> p t n", t=2)
        sq = sb("sq", [P, NH * HD])
        wst = sb("wst", [P, BPB, QD])
        macc = sb("macc", [P, NB])
        mtmp = sb("mtmp", [P, NB])
        osb = l0[:, 5 * NH * HD:5 * NH * HD + NB]
        small = sb("small", [P, 400])
        in_w = xb[:, 0:DI]
        xp_w = xb[:, DI:DI + DC * 96].rearrange("p (k n) -> p k n", k=DC)
        xp_b = mtmp[0:1, 0:96]
        ones = macc[0:1, :]
        out_w = mtmp[0:NST, P:P + D]
        pstat = small[:, 0:16]
        dev = small[:, 64:80]
        be_wo = small[:, 381:382]
        eps_ln = small[:, 379:381]
        wqT, wkT = mw2[:, 0:NQ], mw2[:, NQ:2 * NQ]
        wk_f, wq_f, wv_f = sq2[:, :], sq[:, :], wst[:, :, :].rearrange("p b n -> p (b n)")
        mw1_f = [comb_bc[:, n] for n in range(MIXES)]
        mw1_f += [t[:, n * HID:(n + 1) * HID] for t in (wk_f, wq_f, wv_f) for n in range(2)]
        idx = sb("idx", [P, 4, 8], U32)

        ps = ctx.enter_context(nc.psum_tensor("ps", [P, 8 * NB], F32))

        def bank(n, rows=P, a0=0):
            return ps[a0:a0 + rows, n * NB:(n + 1) * NB]

        x_dram = nc.dram_tensor("x_dram", (P, TOK), F32, kind="Internal").ap()
        comb_dram = nc.dram_tensor("comb_dram", (EXP, NB), F32, kind="Internal").ap()

        ld_x, ld_small, ld_a, ld_b, ld_c = (sem(n) for n in ("ld_x", "ld_small", "ld_a", "ld_b", "ld_c"))
        ld_m, ld_s = sem("ld_m"), sem("ld_s")
        P_FREE, P_POOL = 9, 10 + 2 * NSPLIT
        PREP = 12
        CLOADS = 12 * 16
        eps_set, pads_set = sem("eps_set"), sem("pads_set")
        stand, stand_dve, stand_sp = sem("stand"), sem("stand_dve"), sem("stand_sp")
        ln_centred, ln_sq, ln_var, ln_sd, ln_rs, ln_dg, ln_bc, ln_rb = (
            sem(n) for n in ("ln_centred", "ln_sq", "ln_var", "ln_sd", "ln_rs", "ln_dg", "ln_bc", "ln_rb"))
        ln_out = signal("ln_out", 1)
        a_in = signal("a_in", DC)
        a_pad = signal("a_pad", DC)
        a_conv = signal("a_conv", DC)
        a_hs = signal("a_hs", DC)
        a_w12 = signal("a_w12", KC)
        a_silu = signal("a_silu", KC)
        a_u = signal("a_u", KC)
        a_h1 = signal("a_h1", KC)
        a_g1 = signal("a_g1", KC)
        a_h2 = signal("a_h2", KC)
        a_g2 = signal("a_g2", KC)
        a_xp = signal("a_xp", 1)
        a_ex = signal("a_ex", 5)
        a_b = signal("a_b", 2)
        a_y = signal("a_y", BPB)
        a_o = signal("a_o", 1)
        a_w3 = signal("a_w3", 1)
        a_res = signal("a_res", 2)
        a_step = sem("a_step")
        p_dve, p_pe, p_pool = sem("p_dve"), sem("p_pe"), sem("p_pool")
        b_xb = signal("b_xb", 3)
        x_st = sem("x_st")
        x_ld = signal("x_ld", 16)
        b_gate = signal("b_gate", 1)
        b_gz = signal("b_gz", 2)
        b_th = signal("b_th", 2)
        b_comb = signal("b_comb", 1)
        b_ct = signal("b_ct", 1)
        b_ctc = signal("b_ctc", 1)
        b_cst = signal("b_cst", 16)
        b_cbc = signal("b_cbc", 16 * EXP)
        NRING = 2 * NQ + 6 * NCH + NE * KC
        r_pe = signal("r_pe", NRING)
        RA = 2 * NQ + 4 * NCH + NE * KC
        r_act = signal("r_act", RA)
        r_dve = signal("r_dve", 2 * NCH)
        b_eta = signal("b_eta", 1)
        z_pe = signal("z_pe", 2 * NCH)
        z_sq = signal("z_sq", 2 * NCH)
        z_ve = signal("z_ve", NCH)
        z_r = signal("z_r", NCH)
        z_xh = signal("z_xh", 2 * NCH)
        z_gm = signal("z_gm", NCH)
        z_gx = signal("z_gx", NCH)
        z_s2 = signal("z_s2", NCH)
        z_u = signal("z_u", NCH)
        z_eg = signal("z_eg", 2 * NCH)
        z_es = signal("z_es", 2 * NCH)
        e_hi = signal("e_hi", 2 * NCH)
        e_lo = signal("e_lo", 2 * NCH)
        w_pe = signal("w_pe", 2 * NCH)
        w_dve = signal("w_dve", 2 * NCH)
        q_pe = signal("q_pe", 2 * NCH)
        q_sq = signal("q_sq", 2 * NCH)
        q_ve = signal("q_ve", NCH)
        q_r = signal("q_r", NCH)
        q_n = signal("q_n", 2 * NCH)
        m_pe = signal("m_pe", NE)
        m_mul = signal("m_mul", NE)
        m_add = signal("m_add", NE - 1)
        t_out = signal("t_out", 1)
        t_res = signal("t_res", 2)
        t_dma = signal("t_dma", 16)
        b_step = sem("b_step")
        BSTEPS = 12 + 17 * NCH

        RING0 = 4
        ring = [("k", q, r_act) for q in range(NQ)]

        def ring_pair(kind, c, who):
            return [(kind, (c, p), who) for p in range(2)]

        def ring_up(e):
            return [("up", (e, f), r_act) for f in range(KC)]

        ring += ring_pair("t", 0, r_dve)
        ring += [("q", q, r_act) for q in range(NQ)]
        for c in range(NCH):
            ring += ring_pair("kt", c, r_act)
            if c + 1 < NCH:
                ring += ring_pair("t", c + 1, r_dve)
            ring += ring_up(2 * c) + ring_up(2 * c + 1)
            if c:
                ring += ring_pair("v", c - 1, r_act)
        ring += ring_up(EXP)
        ring += ring_pair("v", NCH - 1, r_act)
        assert len(ring) == NRING
        ring_no = {(k, w): n for n, (k, w, _) in enumerate(ring)}
        taken_no = {}
        for s in (r_act, r_dve):
            for n, (k, w, _) in enumerate([r for r in ring if r[2] is s]):
                taken_no[(k, w)] = n + 1
        assert sum(r[2] is r_act for r in ring) == RA

        def ring_bank(kind, which):
            return RING0 + ring_no[(kind, which)] % 3

        def by_parity(t, p):
            return t[:, :].rearrange("p (q h d) -> p h q d", h=2, d=HD)[:, p]

        def by_batch(t):
            return t.rearrange("p (b c k) -> p b c k", b=BPB, c=NCH)

        def by_chunk(t):
            return t.rearrange("p (c b k) -> p b c k", b=BPB, c=NCH)

        def over_d(t):
            return t.unsqueeze(2).to_broadcast([P, NQ, HD])

        def qd(t):
            return t.rearrange("p (q d) -> p q d", q=NQ)

        def blk(i):
            return bass.ds(i * NB, NB)

        block = ctx.enter_context(nc.Block())

        @block.sync
        def _(sp):
            for s in credited:
                sp.sem_inc(s.sem, s.per)
            sp.dma_start(mats[:, :], a["mats"]).then_inc(ld_x, 16)
            sp.dma_start(x_sb[:, :], a["xT"]).then_inc(ld_x, 16)
            sp.dma_start(cols[:, :], a["cols"]).then_inc(ld_small, 16)
            sp.dma_start(in_w, a["in_w"]).then_inc(ld_a, 16)
            sp.dma_start(w1[:, :], a["w1"]).then_inc(ld_a, 16)
            sp.dma_start(w2[:, :], a["w2"]).then_inc(ld_a, 16)
            sp.dma_start(xp_w[:, :, :], a["xp_w"]).then_inc(ld_a, 16)
            sp.dma_start(xp_b, a["xp_b"]).then_inc(ld_a, 16)
            sp.dma_start(ones, a["ones"]).then_inc(ld_a, 16)
            sp.dma_start(out_w, a["out_w"]).then_inc(ld_a, 16)
            sp.dma_start(h1[:, :, :], a["h1"]).then_inc(ld_b, 16)
            sp.dma_start(h2[:, :, :], a["h2"]).then_inc(ld_b, 16)
            sp.dma_start(w3[:, :, :], a["w3"]).then_inc(ld_b, 16)
            for dst, name in ((wq_f, "wq"), (wk_f, "wk"), (wv_f, "wv"), (mb2[:, :], "mb2"),
                              (gate_w[:, :], "gate_w"), (w_init[:, :], "w_init")):
                sp.dma_start(dst, a[name]).then_inc(ld_c, 16)
            sp.dma_start(e_init[:, :], a["e_init"]).then_inc(ld_c, 16)
            sp.dma_start(wo[:, :, :], a["wo"]).then_inc(ld_c, 16)
            sp.dma_start(gg[:, :], a["gamma_row"].partition_broadcast(P)).then_inc(ld_c, 16)
            sp.dma_start(gb[:, :], a["beta_row"].partition_broadcast(P)).then_inc(ld_c, 16)
            sp.dma_start(wqT, a["wqT"]).then_inc(ld_c, 16)
            sp.dma_start(wkT, a["wkT"]).then_inc(ld_c, 16)
            if NSPLIT < NE:
                sp.dma_start(mw1[:, :, :], a["mw1"][:, NSPLIT:, :]).then_inc(ld_m, 16)
            sp.wait_ge(p_pool, P_FREE)
            for e in range(NSPLIT):
                sp.dma_start(mw1_f[e], a["mw1"][:, e, :]).then_inc(ld_s, 16)
            with sp.Fori(0, NBLK) as i:
                sp.wait_ge(a_res.sem, a_res.at(i, 2))
                sp.dma_start(x_dram[:, blk(i)], x_sb[:, blk(i)]).then_inc(x_st, 16)
            sp.wait_ge(p_pe, 1)
            sp.dma_start(mw2[:, :, :], a["mw2"]).then_inc(ld_m, 16)
            sp.wait_ge(x_st, NBLK * 16)
            with sp.Fori(0, NBLK) as i:
                def wait(signal, value):
                    sp.wait_ge(signal.sem, value)
                    sp.sem_inc(stand_sp, 1)

                wait(b_gate, b_gate.at(i, 1))
                wait(b_xb, b_xb.at(i, 3))
                sp.dma_start(xb[:, :], x_dram[:, blk(i)]).then_inc(x_ld.sem, 16)
                wait(b_ctc, b_ctc.at(i, 1))
                wait(b_cbc, b_cbc.before(i, 16 * EXP))
                sp.dma_start(comb_dram, combT[:, :]).then_inc(b_cst.sem, 16)
                wait(b_cst, b_cst.at(i, 16))
                for e in range(EXP):
                    wait(m_mul, m_mul.before(i, NE) if e < MIXES else m_mul.at(i, e - MIXES + 1))
                    if e:
                        wait(b_cbc, b_cbc.at(i, 16 * e))
                    sp.dma_start(comb_bc[:, e % MIXES, :],
                                 comb_dram[e].partition_broadcast(P)).then_inc(b_cbc.sem, 16)
                wait(t_res, t_res.at(i, 2))
                sp.dma_start(out[:, bass.ds(i * NB, NB)], osb[:, :]).then_inc(t_dma.sem, 16)
            sp.wait_ge(t_dma.sem, t_dma.at(NBLK - 1, 16))

        @block.gpsimd
        def _(pool):
            pool.memset(eps_ln[:, 0:1], LN_EPS).then_inc(eps_set, 1)
            pool.memset(eps_ln[:, 1:2], TTT_EPS).then_inc(eps_set, 1)
            pool.memset(hpad[:, :, :, 0:PAD], 0.0).then_inc(pads_set, 1)
            pool.memset(small[:, 384:400], -0.5).then_inc(eps_set, 1)
            pool.wait_ge(eps_set, 3)
            pool.wait_ge(ld_x, 32)
            pool.wait_ge(ld_c, CLOADS)
            done = [0]

            def step(ins):
                done[0] += 1
                ins.then_inc(p_pool, 1)
                pool.wait_ge(p_pool, done[0])

            def split(to, src):
                step(pool.tensor_copy(to[:, 0], src))
                step(pool.tensor_tensor(to[:, 1], src, to[:, 0], ALU.subtract))

            pool.tensor_copy(neg[:, :], mat(M_NEG))
            split(wq, wq_f)
            split(wk, wk_f)
            step(pool.tensor_tensor(wv_f, wk_f, wv_f, ALU.subtract))
            step(pool.tensor_tensor(gb[:, :], gg[:, :], gb[:, :], ALU.mult))
            step(pool.tensor_tensor(wk_f, wv_f, gg[:, :], ALU.mult))
            split(wt, wk_f)
            step(pool.tensor_tensor(gg[:, :], gg[:, :], gg[:, :], ALU.mult))
            for e in range(NSPLIT):
                if e == 0:
                    pool.wait_ge(ld_s, 16 * NSPLIT)
                split(mw1_s[:, :, e], mw1_f[e])
            assert done[0] == P_POOL
            with pool.Fori(0, NBLK) as i:
                def query_deviations(c):
                    pool.wait_ge(q_ve.sem, q_ve.at(i, c + 1))
                    pool.tensor_tensor(small[:, 240:256], small[:, 224:240], small[:, 384:400],
                                       ALU.pow).then_inc(q_r.sem, 1)

                for c in range(NCH):
                    pool.wait_ge(z_ve.sem, z_ve.at(i, c + 1))
                    pool.wait_ge(w_dve.sem, w_dve.before(i, 2 * c + 2) if c == 0 else w_dve.at(i, 2 * c))
                    pool.tensor_tensor(small[:, 16:32], small[:, 0:16], small[:, 384:400],
                                       ALU.pow).then_inc(z_r.sem, 1)
                    h = slice(0, QD)
                    pool.wait_ge(z_xh.sem, z_xh.at(i, 2 * c + 1))
                    pool.tensor_tensor(qd(gx[:, h]), qd(xh[:, h]), by_parity(gg, 0),
                                       ALU.mult).then_inc(z_gm.sem, 1)
                    pool.wait_ge(z_gm.sem, z_gm.at(i, c + 1))
                    pool.wait_ge(r_dve.sem, r_dve.at(i, taken_no[("t", (c, 0))]))
                    pool.tensor_tensor(gx[:, h], gx[:, h], ttok[:, c % 2, h], ALU.add).then_inc(z_gx.sem, 1)
                    if c:
                        query_deviations(c - 1)
                    pool.wait_ge(z_s2.sem, z_s2.at(i, c + 1))
                    pool.tensor_tensor(qd(sq[:, h]), qd(xh[:, h]), over_d(small[:, 48:56]),
                                       ALU.mult).then_inc(z_u.sem, 1)
                    if c:
                        pool.wait_ge(q_pe.sem, q_pe.at(i, 2 * c))
                    for p in range(2):
                        pool.wait_ge(z_eg.sem, z_eg.at(i, 2 * c + 1 + p))
                        pool.tensor_tensor(by_parity(esum, 1 - p), by_parity(e_init if c == 0 else esum, 1 - p),
                                           by_parity(eg, 1 - p), ALU.add).then_inc(z_es.sem, 1)
                    for p in range(2):
                        pool.wait_ge(e_hi.sem, e_hi.at(i, 2 * c + 1 + p))
                        pool.tensor_tensor(by_parity(esum_s[:, 1], 1 - p), by_parity(esum, 1 - p),
                                           by_parity(esum_s[:, 0], 1 - p), ALU.subtract).then_inc(e_lo.sem, 1)
                query_deviations(NCH - 1)

        @block.tensor
        def _(pe):
            def layernorm(turn):
                base = turn * NBLK
                with pe.Fori(0, NBLK) as i:
                    pe.matmul(ps[:, bass.ds(i * 2 * NB, NB)], mat(M_CENTER), x_sb[:, blk(i)],
                              start=True, stop=True).then_inc(ln_centred, 1)
                for i in range(NBLK):
                    pe.wait_ge(ln_sq, i + base + 1)
                    for j in range(NB // P):
                        mm = pe.matmul(ps[:, bass.ds(i * 2 * NB + (NB + j), 1)],
                                       lsq[:, bass.ds(i * NB + j * P, P)], mats[:, M_MEAN * P:M_MEAN * P + 1],
                                       start=True, stop=True)
                    mm.then_inc(ln_var, 1)
                with pe.Fori(0, NBLK) as i:
                    pe.wait_ge(ln_dg, i + base + 1)
                    pe.matmul(ps[:, bass.ds(i * 2 * NB + NB, NB)], mat(M_MEAN), lsq[:, blk(i)],
                              start=True, stop=True).then_inc(ln_bc, 1)

            pe.wait_ge(ld_x, 32)
            layernorm(0)
            pe.wait_ge(ln_out.sem, ln_out.at(NBLK - 1, 1))
            pe.wait_ge(ld_a, 7 * 16)
            with pe.Fori(0, NBLK) as i:
                for m in range(DC):
                    pe.wait_ge(a_g2.sem, a_g2.before(i, 2 + m + 1))
                    pe.matmul(bank(m), in_w[:, m * P:(m + 1) * P], xn[:, blk(i)],
                              start=True, stop=True).then_inc(a_in.sem, 1)
                for m in range(KC):
                    b = (2 + 2 * m) % 8
                    if m == 0:
                        pe.wait_ge(a_res.sem, a_res.before(i, 2))
                    if m == 1:
                        pe.wait_ge(a_g2.sem, a_g2.before(i, 2))
                    if m == 3:
                        pe.wait_ge(a_pad.sem, a_pad.at(i, DC))
                    pe.matmul(bank(b), w1[:, m * P:(m + 1) * P], xn[:, blk(i)], start=True, stop=True)
                    pe.matmul(bank(b + 1), w2[:, m * P:(m + 1) * P], xn[:, blk(i)],
                              start=True, stop=True).then_inc(a_w12.sem, 1)
                pe.wait_ge(ld_b, 3 * 16)
                pe.wait_ge(a_u.sem, a_u.at(i, 2))
                for k in range(KC):
                    pe.wait_ge(a_u.sem, a_u.at(i, k + 1))
                    for m in range(KC):
                        mm = pe.matmul(bank(2 + m), h1[:, k, m * P:(m + 1) * P], u0[:, k],
                                       start=(k == 0), stop=(k == KC - 1), skip_group_check=True)
                        if k == KC - 1:
                            mm.then_inc(a_h1.sem, 1)
                for k in range(KC):
                    pe.wait_ge(a_g1.sem, a_g1.at(i, k + 1))
                    for m in range(KC):
                        mm = pe.matmul(bank((6 + m) % 8), h2[:, k, m * P:(m + 1) * P], g1[:, k],
                                       start=(k == 0), stop=(k == KC - 1), skip_group_check=True)
                        if k == KC - 1:
                            mm.then_inc(a_h2.sem, 1)
                pe.wait_ge(a_hs.sem, a_hs.at(i, DC))
                for k in range(DC):
                    pe.matmul(bank(3, 96), xp_w[:, k], hs[:, k], start=(k == 0), stop=False)
                pe.matmul(bank(3, 96), xp_b, ones, start=False,
                          stop=True).then_inc(a_xp.sem, 1)
                for k in range(KC):
                    pe.wait_ge(a_g2.sem, a_g2.at(i, k + 1))
                    mm = pe.matmul(bank(2), w3[:, k], g2[:, k], start=(k == 0), stop=(k == KC - 1))
                mm.then_inc(a_w3.sem, 1)
                pe.wait_ge(a_y.sem, a_y.at(i, BPB))
                pe.matmul(bank(4), out_w, ssm[0:NST, 4], start=True, stop=True).then_inc(a_o.sem, 1)

            pe.wait_ge(ld_c, CLOADS)
            for q in range(NQ):
                pe.matmul(bank(6)[:, 0:P], wqT[:, q], wo[:, q],
                          start=(q == 0), stop=(q == NQ - 1))
            for q in range(NQ):
                pe.matmul(bank(7)[:, 0:1], wo[:, q], col("beta", q), start=(q == 0), stop=(q == NQ - 1))
            for q in range(NQ):
                mm = pe.matmul(bank(7)[:, NH:2 * NH].rearrange("p (h q) -> p q h", h=2)[:, q],
                               wkT[:, q], col("theta", 2 * q, 2),
                               start=True, stop=True)
            mm.then_inc(p_pe, 1)
            pe.wait_ge(a_res.sem, a_res.at(NBLK - 1, 2))
            pe.wait_ge(p_dve, 3)
            layernorm(1)
            pe.wait_ge(ln_out.sem, ln_out.at(2 * NBLK - 1, 1))
            pe.wait_ge(p_dve, PREP)
            pe.wait_ge(p_pool, P_POOL)
            pe.wait_ge(ld_m, 2 * 16)

            with pe.Fori(0, NBLK) as i:
                def free(kind, which):
                    n = ring_no[(kind, which)] - 3
                    if n < 0:
                        n = max(m for m in range(-3, 0) if (m + NRING) % 3 == (n + 3) % 3)
                    k, w, s = ring[n]
                    pe.wait_ge(s.sem, (s.before if n < 0 else s.at)(i, taken_no[(k, w)]))
                    return bank(ring_bank(kind, which))

                def tokens(c):
                    return xb[:, c * P:(c + 1) * P]

                def product(to, left, right):
                    for n, (l, r) in enumerate(((0, 0), (1, 0), (0, 1))):
                        mm = pe.matmul(to, left(l), right(r), start=(n == 0), stop=(n == 2))
                    return mm

                def project_targets(c):
                    for p in range(2):
                        product(free("t", (c, p)), lambda s: xb_s[:, s, c * P:(c + 1) * P],
                                lambda s: by_parity(wt[:, s], p)).then_inc(r_pe.sem, 1)

                def turn(kind, c, pair):
                    for s in range(2):
                        to = free(kind, (c, s))
                        for n in range(4):
                            mm = pe.transpose(to[:, n * P:(n + 1) * P], pair(4 * s + n), mat(M_IDENT))
                        mm.then_inc(r_pe.sem, 1)

                def turn_queries(c):
                    pe.wait_ge(q_n.sem, q_n.at(i, 2 * c + 2))
                    turn("v", c, lambda q: sq2[:, q * P:(q + 1) * P])

                def up(e):
                    for f in range(KC):
                        to = free("up", (e, f))
                        if e < NSPLIT:
                            mm = product(to, lambda s: mw1_s[:, s, e, f * P:(f + 1) * P], lambda s: xb_s[:, s])
                        else:
                            mm = pe.matmul(to, mw1[:, e - NSPLIT, f * P:(f + 1) * P], xn[:, blk(i)],
                                           start=True, stop=True)
                        mm.then_inc(r_pe.sem, 1)

                def down(e):
                    pe.wait_ge(m_mul.sem, m_mul.at(i, e) if e else m_mul.before(i, NE))
                    for f in range(KC):
                        pe.wait_ge(r_act.sem, r_act.at(i, taken_no[("up", (e, f))]))
                        mm = pe.matmul(bank(7), mw2[:, e * KC + f], hid[:, e % 2, f], start=(f == 0),
                                       stop=(f == KC - 1))
                    mm.then_inc(m_pe.sem, 1)

                def through(to, x, w, c, done):
                    for p in range(2):
                        if c == 0 and to == 0:
                            pe.matmul(bank(to + p), mat(M_NEG), by_parity(e_init, p), start=True, stop=False,
                                      skip_group_check=True)
                        else:
                            for s in range(2):
                                pe.matmul(bank(to + p), neg[:, :], by_parity(esum_s[:, s], p), start=(s == 0),
                                          stop=False, skip_group_check=True)
                        for q in range(NQ):
                            for b in range(BPB):
                                r = slice(64 * p, 64 * p + 64)
                                at = (to + p) * NB + q * HD
                                fr = c * P + b * CH
                                mm = pe.matmul(ps[64 * b:64 * b + 64, at:at + HD], x[r, q, fr:fr + CH],
                                               w(r, b, q), start=False, stop=True, skip_group_check=True)
                        mm.then_inc(done.sem, 1)

                pe.wait_ge(b_xb.sem, b_xb.at(i, 1))
                pe.wait_ge(t_res.sem, t_res.before(i, 2))
                for j in range(NB // P):
                    pe.matmul(ps[:, j * EXP:(j + 1) * EXP], xb[:, j * P:(j + 1) * P], gate_w[:, :],
                              start=True, stop=True)
                for c in range(NCH):
                    mm = pe.matmul(ps[:, 64 + c * NH:64 + (c + 1) * NH], tokens(c), w_th[:, :],
                                   start=True, stop=True)
                mm.then_inc(b_gate.sem, 1)
                pe.wait_ge(b_xb.sem, b_xb.at(i, 3))
                for q in range(NQ):
                    product(free("k", q), lambda s: wk[:, s, q * P:(q + 1) * P],
                            lambda s: xb_s[:, s]).then_inc(r_pe.sem, 1)
                pe.wait_ge(b_comb.sem, b_comb.at(i, 1))
                for j in range(NB // P):
                    mm = pe.transpose(ps[0:EXP, NB + j * P:NB + (j + 1) * P],
                                      small[:, 96 + 8 * j:104 + 8 * j], mat(M_IDENT))
                mm.then_inc(b_ct.sem, 1)
                project_targets(0)
                pe.wait_ge(b_gz.sem, b_gz.at(i, 2))
                pe.wait_ge(b_ctc.sem, b_ctc.at(i, 1))

                def keys_through(c):
                    if c:
                        pe.wait_ge(e_lo.sem, e_lo.at(i, 2 * c))
                        pe.wait_ge(w_dve.sem, w_dve.at(i, 2 * c))
                        through(0, xkT, lambda r, b, q: wst[r, b, q * HD:(q + 1) * HD], c, z_pe)
                    else:
                        pe.wait_ge(r_act.sem, r_act.at(i, taken_no[("k", NQ - 1)]))
                        through(0, xkT, lambda r, b, q: w_init[r, q * HD:(q + 1) * HD], c, z_pe)

                def queries_through(c):
                    pe.wait_ge(w_dve.sem, w_dve.at(i, 2 * c + 2))
                    pe.wait_ge(e_lo.sem, e_lo.at(i, 2 * c + 2))
                    if c == 0:
                        pe.wait_ge(r_act.sem, r_act.at(i, taken_no[("q", NQ - 1)]))
                    through(2, xqT, lambda r, b, q: wst[r, b, q * HD:(q + 1) * HD], c, q_pe)

                keys_through(0)
                for q in range(NQ):
                    product(free("q", q), lambda s: wq[:, s, q * P:(q + 1) * P],
                            lambda s: xb_s[:, s]).then_inc(r_pe.sem, 1)
                for c in range(NCH):
                    turn("kt", c, lambda q: xkT[:, q, c * P:(c + 1) * P])
                    if c + 1 < NCH:
                        project_targets(c + 1)
                    up(2 * c)
                    down(2 * c)
                    up(2 * c + 1)
                    if c:
                        turn_queries(c - 1)
                    pe.wait_ge(z_eg.sem, z_eg.at(i, 2 * c + 2))
                    pe.wait_ge(r_act.sem, r_act.at(i, taken_no[("kt", (c, 1))]))
                    pe.sem_inc(stand, 1)
                    for b in range(BPB):
                        for q in range(NQ):
                            for p in range(2):
                                r = slice(64 * b, 64 * b + 64)
                                nat = slice((2 * q + p) * HD, (2 * q + p + 1) * HD)
                                mm = pe.matmul(ps[64 * p:64 * p + 64, (2 + b) * NB + q * HD:(2 + b) * NB + (q + 1) * HD],
                                               ktok[r, nat], eg[r, nat], start=True, stop=True,
                                               skip_group_check=True)
                        mm.then_inc(w_pe.sem, 1)
                    down(2 * c + 1)
                    if c + 1 < NCH:
                        keys_through(c + 1)
                    queries_through(c)
                up(EXP)
                down(EXP)
                turn_queries(NCH - 1)
                pe.wait_ge(r_act.sem, r_act.at(i, RA))
                pe.matmul(bank(2), wqo[:, :], xn[:, blk(i)], start=True, stop=False)
                pe.matmul(bank(2), mb2[:, :], combT[:, :], start=False, stop=False)
                for q in range(NQ):
                    mm = pe.matmul(bank(2), wo[:, q], xqT[:, q], start=False, stop=(q == NQ - 1))
                mm.then_inc(t_out.sem, 1)

        @block.scalar
        def _(act):
            def layernorm(turn):
                base = turn * NBLK
                with act.Fori(0, NBLK) as i:
                    act.wait_ge(ln_centred, i + base + 1)
                    act.activation(lsq[:, blk(i)], ps[:, bass.ds(i * 2 * NB, NB)],
                                   ACT.Square).then_inc(ln_sq, 1)
                with act.Fori(0, NBLK) as i:
                    act.wait_ge(ln_var, i + base + 1)
                    act.activation(dev[:, bass.ds(i * 4, 4)], ps[:, bass.ds(i * 2 * NB + NB, 4)],
                                   ACT.Sqrt, bias=eps_ln[:, 0:1]).then_inc(ln_sd, 1)
                with act.Fori(0, NBLK) as i:
                    act.wait_ge(ln_bc, i + base + 1)
                    act.activation(lsq[:, blk(i)], ps[:, bass.ds(i * 2 * NB + NB, NB)],
                                   ACT.Copy).then_inc(ln_rb, 1)

            act.wait_ge(eps_set, 3)
            layernorm(0)
            act.wait_ge(ld_small, 16)
            act.wait_ge(pads_set, 1)
            with act.Fori(0, NBLK) as i:
                for m in range(DC):
                    act.wait_ge(a_in.sem, a_in.at(i, m + 1))
                    act.wait_ge(a_conv.sem, a_conv.before(i, m + 1))
                    act.activation(hpad[:, m, :, PAD:PAD + SEQ], bank(m).rearrange("p (b s) -> p b s", b=BPB),
                                   ACT.Identity, bias=col("in_b", m)).then_inc(a_pad.sem, 1)
                for m in range(KC):
                    act.wait_ge(a_w12.sem, a_w12.at(i, m + 1))
                    if m == 0:
                        act.wait_ge(a_w3.sem, a_w3.before(i, 1))
                    act.activation(u0[:, m], bank((2 + 2 * m) % 8), ACT.Silu,
                                   scale=col("w1_s", m)).then_inc(a_silu.sem, 1)
                for m in range(DC):
                    act.wait_ge(a_conv.sem, a_conv.at(i, m + 1))
                    act.activation(hs[:, m], conv[:, m], ACT.Silu, bias=col("conv_b", m)).then_inc(a_hs.sem, 1)
                for m in range(KC):
                    act.wait_ge(a_h1.sem, a_h1.at(i, m + 1))
                    act.activation(g1[:, m], bank(2 + m), ACT.Gelu, scale=col("h1_s", m)).then_inc(a_g1.sem, 1)
                for m in range(KC):
                    act.wait_ge(a_h2.sem, a_h2.at(i, m + 1))
                    act.activation(g2[:, m], bank((6 + m) % 8), ACT.Gelu, scale=col("h2_s", m)).then_inc(a_g2.sem, 1)
                act.wait_ge(a_xp.sem, a_xp.at(i, 1))
                act.wait_ge(a_y.sem, a_y.before(i, BPB))
                act.activation(ssm[0:NST, 0], bank(3, NST), ACT.Exp).then_inc(a_ex.sem, 1)
                act.activation(ssm[0:NST, 1], bank(3, NST, 32), ACT.Copy).then_inc(a_ex.sem, 1)
                act.activation(ssm[0:NST, 2], bank(3, NST, 64), ACT.Copy).then_inc(a_ex.sem, 1)
                act.activation(ssm[0:NST, 3], bank(3, NST, 32), ACT.Tanh, scale=0.5).then_inc(a_ex.sem, 1)
                act.wait_ge(a_ex.sem, a_ex.at(i, 1))
                act.activation(ssm[0:NST, 0], ssm[0:NST, 0], ACT.Exp, scale=-1.0).then_inc(a_ex.sem, 1)
            layernorm(1)

            act.wait_ge(p_dve, PREP)
            with act.Fori(0, NBLK) as i:
                def take(kind, which):
                    act.wait_ge(r_pe.sem, r_pe.at(i, ring_no[(kind, which)] + 1))
                    return bank(ring_bank(kind, which))

                def keys_by_token(c):
                    for p in range(2):
                        src = take("kt", (c, p))
                        act.wait_ge(w_pe.sem, w_pe.at(i, 2 * c) if c else w_pe.before(i, 2 * NCH))
                        act.activation(ktok[:, p * QD:(p + 1) * QD], src, ACT.Copy).then_inc(r_act.sem, 1)

                def queries_turned(c):
                    for s in range(2):
                        act.activation(xqT[:, 4 * s:4 * s + 4, c * P:(c + 1) * P],
                                       take("v", (c, s)).rearrange("p (q t) -> p q t", q=4),
                                       ACT.Copy).then_inc(r_act.sem, 1)

                def query_squares(c):
                    for p in range(2):
                        act.wait_ge(q_pe.sem, q_pe.at(i, 2 * c + p + 1))
                        act.activation(sq2[:, p * QD:(p + 1) * QD], bank(2 + p), ACT.Square)\
                            .then_inc(q_sq.sem, 1)

                def gelus(e):
                    act.wait_ge(m_pe.sem, m_pe.at(i, e - 1) if e >= 2 else m_pe.before(i, NE))
                    for f in range(KC):
                        act.activation(hid[:, e % 2, f], take("up", (e, f)), ACT.Gelu,
                                       bias=col("b1", e * KC + f)).then_inc(r_act.sem, 1)

                act.wait_ge(b_gz.sem, b_gz.at(i, 2))
                for n, (o, w) in enumerate(((0, 32), (32, 64))):
                    act.activation(small[:, 128 + o:128 + o + w], small[:, 224 + o:224 + o + w], ACT.Tanh,
                                   scale=0.5).then_inc(b_th.sem, 1)
                for q in range(NQ):
                    src = take("k", q)
                    act.wait_ge(z_pe.sem, z_pe.before(i, 2 * NCH))
                    act.activation(xkT[:, q], src, ACT.Copy).then_inc(r_act.sem, 1)
                for c in range(NCH):
                    for p in range(2):
                        act.wait_ge(z_pe.sem, z_pe.at(i, 2 * c + p + 1))
                        act.wait_ge(z_eg.sem, z_eg.at(i, 2 * c) if c else z_eg.before(i, 2 * NCH))
                        act.activation(sq[:, p * QD:(p + 1) * QD], bank(p), ACT.Square).then_inc(z_sq.sem, 1)
                    if c:
                        query_squares(c - 1)
                    else:
                        for q in range(NQ):
                            src = take("q", q)
                            act.wait_ge(t_out.sem, t_out.before(i, 1))
                            act.activation(xqT[:, q], src, ACT.Copy).then_inc(r_act.sem, 1)
                    keys_by_token(c)
                    gelus(2 * c)
                    gelus(2 * c + 1)
                    for p in range(2):
                        act.wait_ge(z_es.sem, z_es.at(i, 2 * c + 1 + p))
                        act.activation(by_parity(esum_s[:, 0], 1 - p), by_parity(esum, 1 - p),
                                       ACT.Copy).then_inc(e_hi.sem, 1)
                    if c:
                        queries_turned(c - 1)
                query_squares(NCH - 1)
                gelus(EXP)
                queries_turned(NCH - 1)

        @block.vector
        def _(dve):
            tt, ts, stt = dve.tensor_tensor, dve.tensor_scalar, dve.scalar_tensor_tensor

            def layernorm(turn):
                base = turn * NBLK
                with dve.Fori(0, NBLK) as i:
                    dve.wait_ge(ln_sd, i + base + 1)
                    d = dev[:, bass.ds(i * 4, 4)]
                    dve.reciprocal(d, d).then_inc(ln_rs, 1)
                    dve.wait_ge(ln_rs, i + base + 1)
                    for j in range(NB // P):
                        ins = ts(lsq[:, bass.ds(i * NB + j * P, P)], mat(M_IDENT), dev[:, bass.ds(i * 4 + j, 1)],
                                 float(P), ALU.mult, ALU.mult)
                    ins.then_inc(ln_dg, 1)
                with dve.Fori(0, NBLK) as i:
                    dve.wait_ge(ln_rb, i + base + 1)
                    rs = lsq[:, blk(i)]
                    o = by_chunk(xn[:, blk(i)]) if turn else xn[:, blk(i)]
                    centred = ps[:, bass.ds(i * 2 * NB, NB)]
                    tt(o, by_batch(centred) if turn else centred, by_batch(rs) if turn else rs, ALU.mult)\
                        .then_inc(ln_out.sem, 1)

            layernorm(0)
            dve.wait_ge(ln_out.sem, ln_out.at(NBLK - 1, 1))
            dve.wait_ge(ld_small, 16)
            dve.wait_ge(ld_x, 32)
            with dve.Fori(0, NBLK) as i:
                for m in range(KC):
                    dve.wait_ge(a_silu.sem, a_silu.at(i, m + 1))
                    stt(u0[:, m], bank((3 + 2 * m) % 8), col("w2_s", m), u0[:, m], ALU.mult,
                        ALU.mult).then_inc(a_u.sem, 1)
                for m in range(DC):
                    dve.wait_ge(a_pad.sem, a_pad.at(i, m + 1))
                    dve.wait_ge(a_hs.sem, a_hs.before(i, m + 1))
                    o = conv[:, m].rearrange("p (b s) -> p b s", b=BPB)
                    ts(o, hpad[:, m, :, 0:SEQ], col("conv_w", m * TAPS), None, ALU.mult).then_inc(a_step, 1)
                    for t in range(1, TAPS):
                        dve.wait_ge(a_step, i * (DC * (TAPS - 1)) + (m * (TAPS - 1) + t))
                        ins = stt(o, hpad[:, m, :, t:t + SEQ], col("conv_w", m * TAPS + t), o, ALU.mult, ALU.add)
                        ins.then_inc(a_conv.sem if t == TAPS - 1 else a_step, 1)
                dve.wait_ge(a_ex.sem, a_ex.at(i, 4))
                stt(ssm[0:NST, 3], ssm[0:NST, 3], 1.0, ssm[0:NST, 1], ALU.add, ALU.mult).then_inc(a_b.sem, 1)
                dve.wait_ge(a_b.sem, a_b.at(i, 1))
                stt(ssm[0:NST, 3], ssm[0:NST, 3], 0.5, ssm[0:NST, 2], ALU.mult, ALU.mult).then_inc(a_b.sem, 1)
                dve.wait_ge(a_b.sem, a_b.at(i, 2))
                dve.wait_ge(a_ex.sem, a_ex.at(i, 5))
                dve.wait_ge(a_o.sem, a_o.before(i, 1))
                for b in range(BPB):
                    s = slice(b * SEQ, (b + 1) * SEQ)
                    dve.tensor_tensor_scan(ssm[0:NST, 4, s], ssm[0:NST, 0, s], ssm[0:NST, 3, s], 0.0,
                                           ALU.mult, ALU.add).then_inc(a_y.sem, 1)
                dve.wait_ge(a_w3.sem, a_w3.at(i, 1))
                stt(res[:, :], bank(2), col("w3_s"), x_sb[:, blk(i)], ALU.mult, ALU.add).then_inc(a_res.sem, 1)
                dve.wait_ge(a_res.sem, a_res.at(i, 1))
                dve.wait_ge(a_o.sem, a_o.at(i, 1))
                stt(x_sb[:, blk(i)], bank(4), col("out_b"), res[:, :], ALU.add, ALU.add).then_inc(a_res.sem, 1)

            done = [0]

            def step(ins):
                done[0] += 1
                ins.then_inc(p_dve, 1)
                dve.wait_ge(p_dve, done[0])

            dve.wait_ge(ld_c, CLOADS)
            dve.wait_ge(p_pe, 1)
            step(dve.tensor_copy(wqo[:, :], bank(6)[:, 0:P]))
            step(dve.tensor_copy(be_wo[:, :], bank(7)[:, 0:1]))
            step(dve.tensor_copy(w_th[:, :], bank(7)[:, NH:2 * NH]))
            for q in range(NQ):
                ins = ts(wo[:, q], wo[:, q], col("gamma", q), None, ALU.mult)
            step(ins)
            step(dve.tensor_reduce(pstat[:, 0:NQ], qd(w_init[:, :]), AX_X, ALU.add))
            step(ts(pstat[:, 0:NQ], pstat[:, 0:NQ], 1.0 / HD, None, ALU.mult))
            step(tt(qd(w_init[:, :]), qd(w_init[:, :]), over_d(pstat[:, 0:NQ]), ALU.subtract))
            e3 = e_init[:, :].rearrange("p (h d) -> p h d", d=HD)
            step(dve.tensor_reduce(pstat[:, 0:NH], e3, AX_X, ALU.add))
            step(ts(pstat[:, 0:NH], pstat[:, 0:NH], 1.0 / HD, None, ALU.mult))
            step(tt(e3, pstat[:, 0:NH].unsqueeze(2).to_broadcast([P, NH, HD]), e3, ALU.subtract))
            te = small[:, 383:384]
            t1 = small[:, 382:383]
            step(tt(t1, col("alpha"), col("inv_index"), ALU.add))
            step(ts(te, t1, 0.0, 0.5 / HD, ALU.max, ALU.mult))
            assert done[0] == PREP
            layernorm(1)
            dve.wait_ge(ln_out.sem, ln_out.at(2 * NBLK - 1, 1))
            dve.wait_ge(p_pool, P_POOL)
            dve.wait_ge(x_st, NBLK * 16)

            with dve.Fori(0, NBLK) as i:
                n_steps = [0]

                def link(ins):
                    n_steps[0] += 1
                    ins.then_inc(b_step, 1)
                    dve.wait_ge(b_step, i * BSTEPS + n_steps[0])

                def link_later(ins):
                    n_steps[0] += 1
                    return ins.then_inc(b_step, 1) and n_steps[0]

                def after(n):
                    dve.wait_ge(b_step, i * BSTEPS + n)

                def take(kind, which):
                    dve.wait_ge(r_pe.sem, r_pe.at(i, ring_no[(kind, which)] + 1))
                    return bank(ring_bank(kind, which))

                def targets(c):
                    for p in range(2):
                        src = take("t", (c, p))
                        tt(qd(ttok[:, c % 2, p * QD:(p + 1) * QD]), qd(src), by_parity(gb, p),
                           ALU.add).then_inc(r_dve.sem, 1)

                def query_variances(c):
                    v2 = small[:, 224:240]
                    for p in range(2):
                        dve.wait_ge(q_sq.sem, q_sq.at(i, 2 * c + p + 1))
                        ins = dve.tensor_reduce(v2[:, 8 * p:8 * p + 8], qd(sq2[:, p * QD:(p + 1) * QD]), AX_X, ALU.add)
                    link(ins)
                    ts(v2, v2, 1.0 / HD, TTT_EPS, ALU.mult, ALU.add).then_inc(q_ve.sem, 1)

                def normalise_queries(c):
                    dve.wait_ge(q_r.sem, q_r.at(i, c + 1))
                    for p in range(2):
                        tt(by_parity(sq2, p), qd(bank(2 + p)), over_d(small[:, 240 + 8 * p:248 + 8 * p]),
                           ALU.mult).then_inc(q_n.sem, 1)

                def mix(e):
                    dve.wait_ge(m_pe.sem, m_pe.at(i, e + 1))
                    if e < EXP:
                        dve.wait_ge(b_cbc.sem, b_cbc.at(i, 16 * (e + 1)))
                    if e == 0:
                        dve.wait_ge(t_res.sem, t_res.before(i, 2))
                        tt(macc[:, :], bank(7), comb_bc[:, 0], ALU.mult).then_inc(m_mul.sem, 1)
                        return
                    if e >= 2:
                        dve.wait_ge(m_add.sem, m_add.at(i, e - 1))
                    if e < EXP:
                        tt(mtmp[:, :], bank(7), comb_bc[:, e % MIXES], ALU.mult).then_inc(m_mul.sem, 1)
                    else:
                        ts(mtmp[:, :], bank(7), col("sb2"), 0.1, ALU.add, ALU.mult).then_inc(m_mul.sem, 1)
                    dve.wait_ge(m_mul.sem, m_mul.at(i, e + 1))
                    tt(macc[:, :], macc[:, :], mtmp[:, :], ALU.add).then_inc(m_add.sem, 1)

                dve.wait_ge(t_res.sem, t_res.before(i, 2))
                dve.tensor_copy(xb[:, :], xn[:, blk(i)]).then_inc(b_xb.sem, 1)
                dve.tensor_copy(xb_s[:, 0], xn[:, blk(i)]).then_inc(b_xb.sem, 1)
                dve.wait_ge(b_xb.sem, b_xb.at(i, 2))
                tt(xb_s[:, 1], xb[:, :], xb_s[:, 0], ALU.subtract).then_inc(b_xb.sem, 1)
                dve.wait_ge(b_gate.sem, b_gate.at(i, 1))
                tt(small[:, 224:256].rearrange("p (j e) -> p j e", e=EXP),
                   ps[:, 0:32].rearrange("p (j e) -> p j e", e=EXP),
                   col("gate_b", 0, EXP).unsqueeze(1).to_broadcast([P, 4, EXP]), ALU.add).then_inc(b_gz.sem, 1)
                tt(small[:, 256:320].rearrange("p (c h) -> p c h", h=NH),
                   ps[:, 64:128].rearrange("p (c h) -> p c h", h=NH),
                   col("theta_bias", 0, NH).unsqueeze(1).to_broadcast([P, NCH, NH]), ALU.add).then_inc(b_gz.sem, 1)
                dve.wait_ge(b_th.sem, b_th.at(i, 2))
                score = small[:, 320:352]
                link(ts(score, small[:, 128:160], 1.0, 0.5, ALU.add, ALU.mult))
                top = small[:, 64:96]
                dve.sem_inc(stand_dve, 1)
                for j in range(4):
                    ins = dve.max(top[:, 8 * j:8 * j + 8], score[:, 8 * j:8 * j + 8])
                link(ins)
                dve.sem_inc(stand_dve, 1)
                for j in range(4):
                    ins = dve.max_index(idx[:, j], top[:, 8 * j:8 * j + 8], score[:, 8 * j:8 * j + 8])
                link(ins)
                t3 = top.rearrange("p (j e) -> p j e", e=8)
                idf = small[:, 352:360].rearrange("p (j e) -> p j e", e=2)
                tsum = small[:, 360:364].rearrange("p (j e) -> p j e", e=1)
                link(dve.tensor_copy(idf, idx[:, :, 0:2]))
                link(tt(tsum, t3[:, :, 0:1], t3[:, :, 1:2], ALU.add))
                link(ts(tsum, tsum, TOPK_EPS, None, ALU.add))
                link(dve.reciprocal(tsum, tsum))
                link(tt(t3[:, :, 0:2], t3[:, :, 0:2], tsum.to_broadcast([P, 4, 2]), ALU.mult))
                comb = small[:, 96:128].rearrange("p (j e) -> p j e", e=EXP)
                c1 = small[:, 32:64].rearrange("p (j e) -> p j e", e=EXP)
                nos = col("expert_no", 0, EXP).unsqueeze(1).to_broadcast([P, 4, EXP])
                link(tt(comb, nos, idf[:, :, 0:1].to_broadcast([P, 4, EXP]), ALU.is_equal))
                link(tt(comb, comb, t3[:, :, 0:1].to_broadcast([P, 4, EXP]), ALU.mult))
                link(tt(c1, nos, idf[:, :, 1:2].to_broadcast([P, 4, EXP]), ALU.is_equal))
                link(tt(c1, c1, t3[:, :, 1:2].to_broadcast([P, 4, EXP]), ALU.mult))
                tt(comb, comb, c1, ALU.add).then_inc(b_comb.sem, 1)
                eta = small[:, 160:224]
                ts(eta, eta, 1.0, te, ALU.add, ALU.mult).then_inc(b_eta.sem, 1)
                dve.wait_ge(b_ct.sem, b_ct.at(i, 1))
                dve.wait_ge(b_cst.sem, b_cst.before(i, 16))
                dve.wait_ge(t_out.sem, t_out.before(i, 1))
                dve.tensor_copy(combT[:, :], bank(1, EXP)).then_inc(b_ctc.sem, 1)
                targets(0)
                for c in range(NCH):
                    ve = small[:, 0:16]
                    rr = small[:, 16:32]
                    s1, s2, ce = small[:, 32:48], small[:, 48:64], small[:, 64:80]
                    for p in range(2):
                        dve.wait_ge(z_sq.sem, z_sq.at(i, 2 * c + p + 1))
                        ins = dve.tensor_reduce(ve[:, 8 * p:8 * p + 8], qd(sq[:, p * QD:(p + 1) * QD]), AX_X, ALU.add)
                    link(ins)
                    ts(ve, ve, 1.0 / HD, TTT_EPS, ALU.mult, ALU.add).then_inc(z_ve.sem, 1)
                    if c:
                        query_variances(c - 1)
                    if c + 1 < NCH:
                        targets(c + 1)
                    dve.wait_ge(z_r.sem, z_r.at(i, c + 1))
                    for p in range(2):
                        h = slice(p * QD, (p + 1) * QD)
                        tt(qd(xh[:, h]), qd(bank(p)), over_d(rr[:, 8 * p:8 * p + 8]), ALU.mult).then_inc(z_xh.sem, 1)
                    ev, od = slice(0, QD), slice(QD, 2 * QD)
                    e8, o8 = slice(0, 8), slice(8, 16)
                    dve.wait_ge(z_xh.sem, z_xh.at(i, 2 * c + 2))
                    a1 = link_later(tt(qd(gx[:, od]), qd(xh[:, od]), by_parity(gg, 1), ALU.mult))
                    tt(ce, rr, eta[:, c * NH:(c + 1) * NH], ALU.mult)
                    after(a1)
                    a1 = link_later(tt(gx[:, od], gx[:, od], ttok[:, c % 2, od], ALU.add))
                    after(a1)
                    a1 = link_later(tt(sq[:, od], gx[:, od], xh[:, od], ALU.mult))
                    a2 = link_later(dve.tensor_reduce(s1[:, o8], qd(gx[:, od]), AX_X, ALU.add))
                    after(a1)
                    a1 = link_later(dve.tensor_reduce(s2[:, o8], qd(sq[:, od]), AX_X, ALU.add))
                    dve.wait_ge(z_gx.sem, z_gx.at(i, c + 1))
                    b1 = link_later(tt(sq[:, ev], gx[:, ev], xh[:, ev], ALU.mult))
                    after(b1)
                    b1 = link_later(dve.tensor_reduce(s2[:, e8], qd(sq[:, ev]), AX_X, ALU.add))
                    a1 = link_later(ts(s2[:, o8], s2[:, o8], 1.0 / HD, None, ALU.mult))
                    after(b1)
                    ts(s2[:, e8], s2[:, e8], 1.0 / HD, None, ALU.mult).then_inc(z_s2.sem, 1)
                    b2 = link_later(dve.tensor_reduce(s1[:, e8], qd(gx[:, ev]), AX_X, ALU.add))
                    after(a1)
                    a1 = link_later(tt(qd(sq[:, od]), qd(xh[:, od]), over_d(s2[:, o8]), ALU.mult))
                    after(b2)
                    b2 = link_later(ts(s1, s1, 1.0 / HD, None, ALU.mult))
                    after(a1)
                    a1 = link_later(tt(gx[:, od], gx[:, od], sq[:, od], ALU.subtract))
                    after(b2)
                    b2 = link_later(tt(qd(gx[:, ev]), qd(gx[:, ev]), over_d(s1[:, e8]), ALU.subtract))
                    after(a1)
                    a1 = link_later(tt(qd(gx[:, od]), qd(gx[:, od]), over_d(s1[:, o8]), ALU.subtract))
                    dve.wait_ge(z_u.sem, z_u.at(i, c + 1))
                    after(b2)
                    b2 = link_later(tt(gx[:, ev], gx[:, ev], sq[:, ev], ALU.subtract))
                    after(a1)
                    tt(by_parity(eg, 1), qd(gx[:, od]), over_d(ce[:, o8]), ALU.mult).then_inc(z_eg.sem, 1)
                    after(b2)
                    tt(by_parity(eg, 0), qd(gx[:, ev]), over_d(ce[:, e8]), ALU.mult).then_inc(z_eg.sem, 1)
                    if c:
                        normalise_queries(c - 1)
                    mix(2 * c)
                    for b in range(BPB):
                        dve.wait_ge(w_pe.sem, w_pe.at(i, 2 * c + b + 1))
                        tt(wst[:, b], (w_init[:, :] if c == 0 else wst[:, b]), bank(2 + b),
                           ALU.subtract).then_inc(w_dve.sem, 1)
                    mix(2 * c + 1)
                query_variances(NCH - 1)
                mix(EXP)
                normalise_queries(NCH - 1)
                dve.wait_ge(t_out.sem, t_out.at(i, 1))
                dve.wait_ge(t_dma.sem, t_dma.before(i, 16))
                dve.wait_ge(m_add.sem, m_add.at(i, NE - 1))
                stt(mtmp[:, :], bank(2), be_wo[:, 0:1], macc[:, :], ALU.add, ALU.add).then_inc(t_res.sem, 1)
                dve.wait_ge(t_res.sem, t_res.at(i, 1))
                dve.wait_ge(x_ld.sem, x_ld.at(i, 16))
                tt(by_batch(osb), by_chunk(mtmp[:, :]), by_batch(xb[:, :]), ALU.add).then_inc(t_res.sem, 1)
                assert n_steps[0] == BSTEPS, n_steps[0]


def kernel(**v):
    import numpy as np
    import concourse.bacc as bacc
    from concourse.bass_utils import run_bass_kernel_spmd as run

    v = {k: np.ascontiguousarray(x) for k, x in v.items()}

    def A(n):
        return v["L0_attn_" + n]

    def M(n):
        return v["L0_ffn_" + n]

    def T(n):
        return v["L1_attn_" + n]

    def E(n):
        return v["L1_ffn_" + n]

    f = np.float32

    def chunks(w, n):
        return w.reshape(n, P, -1).transpose(1, 0, 2)

    half = np.arange(P) // 64
    same = half[:, None] == half[None, :]
    eye = np.eye(P, dtype=f)
    mats = np.concatenate([eye - f(1 / P), np.full((P, P), 1 / P, f), -same.astype(f),
                           eye], axis=1)
    packed = {
        "in_b": A("in_b").reshape(DC, P).T, "conv_w": A("conv_w").reshape(DC, P, TAPS).transpose(1, 0, 2).reshape(P, -1),
        "conv_b": A("conv_b").reshape(DC, P).T,
        "w1_s": M("w1_s").reshape(KC, P).T, "w2_s": M("w2_s").reshape(KC, P).T,
        "h1_s": M("h1_s").reshape(KC, P).T, "h2_s": M("h2_s").reshape(KC, P).T,
        "w3_s": M("w3_s").reshape(1, P).T, "out_b": A("out_b").reshape(1, P).T,
        "gamma": T("gamma").reshape(NQ, P).T, "beta": T("beta").reshape(NQ, P).T,
        "b1": np.concatenate([E("b1").reshape(EXP * KC, P), E("sb1").reshape(KC, P)]).T,
        "sb2": E("sb2").reshape(1, P).T,
        "alpha": np.tile(T("alpha"), 2).reshape(P, 1),
        "inv_index": np.tile(f(1) / np.arange(1, CH + 1, dtype=f), 2).reshape(P, 1),
        "theta_bias": np.broadcast_to(T("theta_bias").reshape(NQ, 2).T.reshape(1, NH), (P, NH)),
        "gate_b": np.broadcast_to(E("gate_b").reshape(1, EXP), (P, EXP)),
        "expert_no": np.broadcast_to(np.arange(EXP, dtype=f).reshape(1, EXP), (P, EXP)),
    }
    cols = np.zeros((P, NCOLS), f)
    for name, x in packed.items():
        at, n = COLS[name]
        cols[:, at:at + n] = x
    th = T("theta").reshape(NQ, 2, HD)
    for q in range(NQ):
        for p in range(2):
            cols[64 * p:64 * p + 64, COLS["theta"][0] + 2 * q + p] = th[q, p]
    xp_w = np.zeros((P, DC, 96), f)
    xw = A("xp_w").T.reshape(DC, P, 2 * NST).transpose(1, 0, 2)
    xp_w[:, :, 0:16], xp_w[:, :, 32:48], xp_w[:, :, 64:80] = xw[:, :, 0:16], xw[:, :, 16:32], 1
    xp_b = np.zeros((1, 96), f)
    xp_b[0, 0:16], xp_b[0, 32:48] = A("xp_b")[0:16], A("xp_b")[16:32]
    e_init = np.zeros((P, NH * HD), f)
    e_init[0] = e_init[64] = T("b1").reshape(NH * HD)
    arrays = {
        "xT": A("x").reshape(TOK, D).T, "mats": mats, "cols": cols,
        "in_w": A("in_w").T, "w1": M("w1_w").T, "w2": M("w2_w").T,
        "h1": chunks(M("h1_w").T, KC), "h2": chunks(M("h2_w").T, KC), "w3": chunks(M("w3_w").T, KC),
        "xp_w": xp_w, "xp_b": xp_b, "ones": np.ones((1, NB), f), "out_w": A("out_w").T,
        "wq": T("wq"), "wk": T("wk"), "wv": T("wv"), "wo": chunks(T("wo"), NQ),
        "wqT": chunks(T("wq").T, NQ) , "wkT": chunks(T("wk").T, NQ) ,
        "gamma_row": T("gamma").reshape(NH * HD), "beta_row": T("beta").reshape(NH * HD),
        "w_init": T("W1").reshape(NQ, P, HD).transpose(1, 0, 2).reshape(P, QD),
        "e_init": e_init,
        "mw1": np.concatenate([E("w1"), E("sw1")[None]]).transpose(1, 0, 2),
        "mw2": np.concatenate([E("w2").reshape(EXP * KC, P, D), E("sw2").reshape(KC, P, D)]).transpose(1, 0, 2),
        "mb2": E("b2"), "gate_w": E("gate_w").T,
    }
    nc = bacc.Bacc("TRN2", target_bir_lowering=False, num_devices=1)
    fed, aps = {}, {}
    for name, x in arrays.items():
        x = np.ascontiguousarray(x)
        fed["in_" + name] = x
        aps[name] = nc.dram_tensor("in_" + name, x.shape, mybir.dt.from_np(x.dtype), kind="ExternalInput").ap()
    out = nc.dram_tensor("out", (D, TOK), F32, kind="ExternalOutput").ap()
    build(nc, aps, out)
    r = run(nc, [fed], core_ids=[0])
    return np.ascontiguousarray(np.asarray(r.results[0]["out"]).T).reshape(BATCH, SEQ, D)
```
